# Optimizing a Trainium2 kernel written in Bass

```python
import numpy as np
import jax
import jax.numpy as jnp

def _softmax(x, axis=-1):
    return jax.nn.softmax(x, axis=axis)

def _gelu(x):
    return jax.nn.gelu(x, approximate=True)

def _silu(x):
    return jax.nn.silu(x)

def _sigmoid(x):
    return jax.nn.sigmoid(x)

def _layernorm(x, axis=-1, eps=1e-05):
    m = jnp.mean(x, axis=axis, keepdims=True)
    v = jnp.var(x, axis=axis, keepdims=True)
    return (x - m) / jnp.sqrt(v + eps)

def _scatter_add(tgt, idx, src, axis=0):
    return tgt.at[idx].add(src)

def _segment_sum(src, seg, n):
    return jax.ops.segment_sum(src, seg, n)
kernel_name = 'mk_adj_ffn_d2_adj_r2_e361f4'

def setup_inputs(seed: int=0):
    np.random.seed(seed)
    _w = jnp.asarray

    def _rec_inputs():
        import jax
        import jax.numpy as jnp
        _gk = jax.random.key(seed)
        x = -0.0005207 + 1.001 * jax.random.normal(jax.random.fold_in(_gk, 1), (4096, 128), jnp.float32)
        _w = (1.0 + jnp.arange(4096, dtype=jnp.float32)) ** (-0.5)
        _w = _w / _w.mean()
        _pij = jnp.clip(0.00195312 * _w[:, None] * _w[None, :], 0.0, 1.0)
        _a = jax.random.uniform(jax.random.fold_in(_gk, 2), (4096, 4096)) < _pij
        adj = _a.astype(jnp.int32)
        return (x, adj)
    x, adj = _rec_inputs()

    def _L0_gnn_setup():
        import jax, jax.numpy as jnp
        import numpy as np
        N, D, H = (4096, 128, 128)
        KEEP_RATIO = 0.5
        TEMP = 1.0
        COS_EPS = 0.0001
        NEG = -9000000000000000.0

        def _cos_normalize(x):
            n = jnp.linalg.norm(x, axis=-1, keepdims=True)
            return x / jnp.maximum(n, COS_EPS)
        key = jax.random.key(seed)
        k1, k2, k3, k4 = jax.random.split(key, 4)
        features = jax.random.normal(k1, (N, D), dtype=jnp.float32)
        adj = jax.random.randint(k2, (N, N), 0, 2, dtype=jnp.int32)
        Wq = jax.random.normal(k3, (H, D), dtype=jnp.float32) * 0.001
        Wk = jax.random.normal(k4, (H, D), dtype=jnp.float32) * 0.001
        return {'features': features, 'adj': adj, 'Wq': Wq, 'Wk': Wk}
    _L0_gnn_all = _L0_gnn_setup()
    _L0_gnn_in = {k: v for k, v in _L0_gnn_all.items() if k in ('Wq', 'Wk')}
    del _L0_gnn_all

    def _L0_ffn_setup():
        import jax, jax.numpy as jnp
        import numpy as np
        C = 128
        EPS = 1e-05
        N_ITERS = 30

        def _layernorm(x, w, bias):
            mu = jnp.mean(x, axis=-1, keepdims=True)
            var = jnp.mean(jnp.square(x - mu), axis=-1, keepdims=True)
            return (x - mu) * jax.lax.rsqrt(var + EPS) * w + bias
        key = jax.random.key(seed)
        kx, kw, kb, klw, klb = jax.random.split(key, 5)
        x = jax.random.normal(kx, (8, 1024, C), dtype=jnp.float32)
        bound = 1.0 / np.sqrt(C)
        W = jax.random.uniform(kw, (C, C), minval=-bound, maxval=bound, dtype=jnp.float32)
        b = jax.random.uniform(kb, (C,), minval=-bound, maxval=bound, dtype=jnp.float32)
        ln_w = jnp.ones((C,), dtype=jnp.float32)
        ln_b = jnp.zeros((C,), dtype=jnp.float32)
        return {'x': x, 'ln_w': ln_w, 'ln_b': ln_b, 'W': W, 'b': b}
    _L0_ffn_all = _L0_ffn_setup()
    _L0_ffn_in = {k: v for k, v in _L0_ffn_all.items() if k in ('ln_w', 'ln_b', 'W', 'b')}
    del _L0_ffn_all

    def _L1_gnn_setup():
        import math
        import jax, jax.numpy as jnp
        import numpy as np
        N = 4096
        F_IN = 128
        F_OUT = 128
        key = jax.random.key(seed)
        ks = jax.random.split(key, 9)
        s = 1.0 / math.sqrt(F_IN)
        return {'x': jax.random.normal(ks[0], (N, F_IN), dtype=jnp.float32), 'adj': jax.random.randint(ks[1], (N, N), 0, 2, dtype=jnp.int32), 'Wq': jax.random.uniform(ks[2], (F_OUT, F_IN), jnp.float32, -s, s), 'bq': jax.random.uniform(ks[3], (F_OUT,), jnp.float32, -s, s), 'Wk': jax.random.uniform(ks[4], (F_OUT, F_IN), jnp.float32, -s, s), 'bk': jax.random.uniform(ks[5], (F_OUT,), jnp.float32, -s, s), 'Wv': jax.random.uniform(ks[6], (F_OUT, F_IN), jnp.float32, -s, s), 'bv': jax.random.uniform(ks[7], (F_OUT,), jnp.float32, -s, s)}
    _L1_gnn_all = _L1_gnn_setup()
    _L1_gnn_in = {k: v for k, v in _L1_gnn_all.items() if k in ('Wq', 'bq', 'Wk', 'bk', 'Wv', 'bv')}
    del _L1_gnn_all

    def _L1_ffn_setup():
        import jax, jax.numpy as jnp
        import numpy as np
        C = 128
        HID = 512
        E = 8
        TEMP = 1.0
        key = jax.random.key(seed)
        ks = jax.random.split(key, 7)
        x = jax.random.normal(ks[0], (8, 8192, C), dtype=jnp.float32)
        W1 = jax.random.normal(ks[1], (C, HID), dtype=jnp.float32) * 0.02
        b1 = jnp.zeros((HID,), dtype=jnp.float32)
        Wg = jax.random.normal(ks[2], (HID, E), dtype=jnp.float32) * 0.02
        bg = jnp.zeros((E,), dtype=jnp.float32)
        Wd = jax.random.normal(ks[3], (E, HID, C), dtype=jnp.float32) * 0.02
        bd = jnp.zeros((E, C), dtype=jnp.float32)
        return {'x': x, 'W1': W1, 'b1': b1, 'Wg': Wg, 'bg': bg, 'Wd': Wd, 'bd': bd}
    _L1_ffn_all = _L1_ffn_setup()
    _L1_ffn_in = {k: v for k, v in _L1_ffn_all.items() if k in ('W1', 'b1', 'Wg', 'bg', 'Wd', 'bd')}
    del _L1_ffn_all
    return {'x': x, 'adj': adj, 'L0_gnn_Wq': _L0_gnn_in['Wq'], 'L0_gnn_Wk': _L0_gnn_in['Wk'], 'L0_ffn_ln_w': _L0_ffn_in['ln_w'], 'L0_ffn_ln_b': _L0_ffn_in['ln_b'], 'L0_ffn_W': _L0_ffn_in['W'], 'L0_ffn_b': _L0_ffn_in['b'], 'L1_gnn_Wq': _L1_gnn_in['Wq'], 'L1_gnn_bq': _L1_gnn_in['bq'], 'L1_gnn_Wk': _L1_gnn_in['Wk'], 'L1_gnn_bk': _L1_gnn_in['bk'], 'L1_gnn_Wv': _L1_gnn_in['Wv'], 'L1_gnn_bv': _L1_gnn_in['bv'], 'L1_ffn_W1': _L1_ffn_in['W1'], 'L1_ffn_b1': _L1_ffn_in['b1'], 'L1_ffn_Wg': _L1_ffn_in['Wg'], 'L1_ffn_bg': _L1_ffn_in['bg'], 'L1_ffn_Wd': _L1_ffn_in['Wd'], 'L1_ffn_bd': _L1_ffn_in['bd']}

def reference(x, adj, L0_gnn_Wq, L0_gnn_Wk, L0_ffn_ln_w, L0_ffn_ln_b, L0_ffn_W, L0_ffn_b, L1_gnn_Wq, L1_gnn_bq, L1_gnn_Wk, L1_gnn_bk, L1_gnn_Wv, L1_gnn_bv, L1_ffn_W1, L1_ffn_b1, L1_ffn_Wg, L1_ffn_bg, L1_ffn_Wd, L1_ffn_bd):
    import jax
    import jax.numpy as jnp

    def _L0_gnn_ref(features, adj, Wq, Wk):
        import jax, jax.numpy as jnp
        import numpy as np
        N, D, H = (4096, 128, 128)
        KEEP_RATIO = 0.5
        TEMP = 1.0
        COS_EPS = 0.0001
        NEG = -9000000000000000.0

        def _cos_normalize(x):
            n = jnp.linalg.norm(x, axis=-1, keepdims=True)
            return x / jnp.maximum(n, COS_EPS)
        Qn = _cos_normalize(features @ Wq.T)
        Kn = _cos_normalize(features @ Wk.T)
        raw_att = Kn @ Qn.T
        att = jnp.where(adj > 0, raw_att, NEG) * TEMP
        att = jax.nn.softmax(att, axis=1)
        prop_fea = att @ features
        adj_mask = (jnp.sum(adj, axis=1) > 0).astype(features.dtype)[:, None]
        prop_fea = adj_mask * prop_fea + (1.0 - adj_mask) * features
        return (1.0 - KEEP_RATIO) * prop_fea + KEEP_RATIO * features

    def _L0_ffn_ref(x, ln_w, ln_b, W, b):
        import jax, jax.numpy as jnp
        import numpy as np
        C = 128
        EPS = 1e-05
        N_ITERS = 30

        def _layernorm(x, w, bias):
            mu = jnp.mean(x, axis=-1, keepdims=True)
            var = jnp.mean(jnp.square(x - mu), axis=-1, keepdims=True)
            return (x - mu) * jax.lax.rsqrt(var + EPS) * w + bias

        def step(h, _):
            h = h + 0.01 * jnp.tanh(h)
            h = h * jax.nn.sigmoid(h)
            h = _layernorm(h, ln_w, ln_b)
            h = jnp.einsum('bsc,dc->bsd', h, W) + b
            return (h, None)
        x, _ = jax.lax.scan(step, x, None, length=N_ITERS)
        return x

    def _L1_gnn_ref(x, adj, Wq, bq, Wk, bk, Wv, bv):
        import math
        import jax, jax.numpy as jnp
        import numpy as np
        N = 4096
        F_IN = 128
        F_OUT = 128
        q = x @ Wq.T + bq
        k = x @ Wk.T + bk
        v = x @ Wv.T + bv
        d = q.shape[-1]
        scores = q @ k.T / jnp.sqrt(jnp.asarray(d, q.dtype))
        neg = jnp.asarray(-9000000000000000.0, scores.dtype)
        scores = jnp.where(adj > 0, scores, neg)
        attention = jax.nn.softmax(scores, axis=-1)
        att = attention @ v
        return jax.nn.elu(att)

    def _L1_ffn_ref(x, W1, b1, Wg, bg, Wd, bd):
        import jax, jax.numpy as jnp
        import numpy as np
        C = 128
        HID = 512
        E = 8
        TEMP = 1.0
        orig_shape = x.shape
        xf = x.reshape(-1, orig_shape[-1])
        H = jax.nn.gelu(xf @ W1 + b1, approximate=False)
        probs = jax.nn.softmax((H @ Wg + bg) / TEMP, axis=-1)
        assign = jnp.argmax(probs, axis=-1)
        out = jnp.zeros_like(xf)
        for e in range(Wd.shape[0]):
            y = H @ Wd[e] + bd[e]
            sel = (assign == e)[:, None]
            out = out + jnp.where(sel, probs[:, e:e + 1] * y, 0.0)
        return out.reshape(orig_shape)
    x = x + _L0_gnn_ref(_layernorm(x, axis=-1), adj, L0_gnn_Wq, L0_gnn_Wk)
    x = x + _L0_ffn_ref(_layernorm(x, axis=-1)[None], L0_ffn_ln_w, L0_ffn_ln_b, L0_ffn_W, L0_ffn_b)[0]
    x = x + _L1_gnn_ref(_layernorm(x, axis=-1), adj, L1_gnn_Wq, L1_gnn_bq, L1_gnn_Wk, L1_gnn_bk, L1_gnn_Wv, L1_gnn_bv)
    x = x + _L1_ffn_ref(_layernorm(x, axis=-1)[None], L1_ffn_W1, L1_ffn_b1, L1_ffn_Wg, L1_ffn_bg, L1_ffn_Wd, L1_ffn_bd)[0]
    return x

_drawn_inputs = setup_inputs


def setup_inputs(seed=0):
    import zlib

    import numpy as np

    out = dict(_drawn_inputs(seed))
    spreads = {'L0_ffn_ln_w': (1.0, 0.2),
     'L0_ffn_ln_b': (0.0, 0.1),
     'L1_ffn_b1': (0.0, 0.8),
     'L1_ffn_bg': (0.0, 0.742),
     'L1_ffn_bd': (0.0, 0.8)}
    factors = {'L0_gnn_Wq': 2.755,
     'L0_gnn_Wk': 2.797,
     'L1_gnn_bq': 8.0,
     'L1_gnn_bk': 8.0,
     'L1_ffn_W1': 6.753,
     'L1_ffn_Wg': 6.715,
     'L1_ffn_Wd': 8.0}
    for name, (base, spread) in spreads.items():
        noise = np.random.default_rng([zlib.crc32(name.encode()), seed]).standard_normal(out[name].shape)
        drawn = base * np.exp(spread * noise) if base else spread * noise
        out[name] = jnp.asarray(drawn.astype(out[name].dtype))
    for name, factor in factors.items():
        out[name] = (out[name] * factor).astype(out[name].dtype)
    return out
```

```python
from contextlib import ExitStack

import concourse.bass as bass
from concourse import mybir

F32 = mybir.dt.float32
F16 = mybir.dt.float16
BF16 = mybir.dt.bfloat16
I32 = mybir.dt.int32
ALU = mybir.AluOpType
ACT = mybir.ActivationFunctionType
AX = mybir.AxisListType
ds = bass.ds

P = 128
N = 4096
D = 128
T = N // P
CHUNK = 512
CHUNKS = N // CHUNK
TPC = CHUNK // P
STEPS = T // 2
STEPS_KERNEL = 30
HID = 512
HC = HID // P
E = 8
LN_EPS = 1e-5
COS_EPS = 1e-4
UNIT = 64.0
SHIFT = 3.5
S_MAX = 7.25


class Core:

    def __init__(self, nc, ctx, io):
        self.nc, self.ctx, self.io = nc, ctx, io

    def sb(self, name, shape, dt=F32, ctx=None):
        return (ctx or self.ctx).enter_context(self.nc.sbuf_tensor(name, shape, dt))

    def ps(self, name, shape, ctx):
        return ctx.enter_context(self.nc.psum_tensor(name, shape, F32))

    def sem(self, name, ctx):
        return ctx.enter_context(self.nc.semaphore(name))


def peeled(eng, n, body):
    body(0, True)
    with eng.Fori(1, n) as i:
        body(i, False)


def load(k):
    nc, io = k.nc, k.io
    with ExitStack() as ctx:
        loaded = k.sem("loaded", ctx)
        block = ctx.enter_context(nc.Block())

        @block.sync
        def _(sp):
            pairs = [(k.x[:, 8 * i:8 * i + 8, :], io["x"].rearrange("(t p) d -> p t d", p=P)[:, 8 * i:8 * i + 8, :])
                     for i in range(4)]
            pairs += [(k.ident[:], io["eye"]), (k.center[:], io["centering"]), (k.unaug[:], io["unaugment"]),
                      (k.unaug_t[:], io["unaugment_t"]), (k.last_row[:], io["last_row"]), (k.ranks[:], io["ranks"]),
                      (k.wkq_t[:, 0:D], io["wk0_t"]), (k.wkq_t[:, D:2 * D], io["wq0_t"]),
                      (k.lnw[:], io["lnw"]), (k.lnb[:], io["lnb"]), (k.w_ffn_t[:], io["w_ffn_t"]),
                      (k.b_ffn[0:1, :], io["b_ffn"]), (k.wq1[:], io["wq1"]), (k.wk1[:], io["wk1"]),
                      (k.wv1_t[:], io["wv1_t"]), (k.bq1[:], io["bq1"]), (k.bv1[0:1, :], io["bv1"]),
                      (k.w1[:], io["w1"]), (k.b1[:], io["b1"]), (k.wg[:], io["wg"]), (k.bg[:], io["bg"]),
                      (k.wd[:], io["wd"]), (k.bd[0:E, :], io["bd"])]
            for to, of in pairs:
                sp.dma_start(to, of).then_inc(loaded, 16)
            sp.wait_ge(loaded, 16 * len(pairs))

        @block.vector
        def _(dve):
            nc.vector.memset(k.row_hi[:, :, D - 1:D], 1.0)
            nc.vector.memset(k.row_lo[:, :, D - 1:D], 0.0)
            nc.vector.memset(k.ones_bf[:], 1.0)
            nc.vector.memset(k.ones[:], 1.0)
            nc.vector.memset(k.ones_half[:], 1.0)
            nc.vector.memset(k.zero_half[:], 0.0)
            nc.vector.memset(k.minus_half[:], -0.5)
            nc.vector.memset(k.eps[:], LN_EPS)
            nc.vector.memset(k.shift[:], SHIFT)


def row_stats(k, tag):
    nc = k.nc
    with ExitStack() as ctx:
        parts = k.sb(tag + "parts", [P, T, 6], F32, ctx)
        tmp = k.sb(tag + "tmp", [P, 5, T], F32, ctx)
        sums, diff, m2, var4, std = (tmp[:, i, :] for i in range(5))
        halves_done = k.sem(tag + "halves_done", ctx)
        combined = k.sem(tag + "combined", ctx)
        std_done = k.sem(tag + "std_done", ctx)
        block = ctx.enter_context(nc.Block())

        @block.vector
        def _(dve):
            with dve.Fori(0, T // 4) as g:
                for t in range(4):
                    nc.vector.bn_stats(parts[:, ds(4 * g + t, 1), :], k.x[:, ds(4 * g + t, 1), :]).then_inc(halves_done, 1)
            dve.wait_ge(halves_done, T)
            nc.vector.tensor_tensor(sums, parts[:, :, 1], parts[:, :, 4], ALU.add).then_inc(combined, 1)
            nc.vector.tensor_tensor(diff, parts[:, :, 1], parts[:, :, 4], ALU.subtract).then_inc(combined, 1)
            nc.vector.tensor_tensor(m2, parts[:, :, 2], parts[:, :, 5], ALU.add).then_inc(combined, 1)
            dve.wait_ge(combined, 2)
            nc.vector.tensor_scalar(k.mean[:], sums, 0.5, None, ALU.mult)
            nc.vector.tensor_tensor(std, diff, diff, ALU.mult).then_inc(combined, 1)
            dve.wait_ge(combined, 4)
            nc.vector.scalar_tensor_tensor(var4, m2, 4.0 / D, std, ALU.mult, ALU.add).then_inc(combined, 1)
            dve.wait_ge(std_done, 1)
            nc.vector.reciprocal(k.rstd[:], std)

        @block.scalar
        def _(act):
            act.wait_ge(combined, 5)
            nc.scalar.activation(std, var4, ACT.Sqrt, bias=k.eps[:, 0:1], scale=0.25).then_inc(std_done, 1)


def normalise_a(k):
    nc = k.nc
    with ExitStack() as ctx:
        f = [k.sb(f"a_f{i}", [P, TPC, D], F32, ctx) for i in range(2)]
        f_t = [k.sb(f"a_f_t{i}", [P, TPC * P], F32, ctx) for i in range(2)]
        square = k.sb("a_square", [P, 2 * TPC, D], F32, ctx)
        unit = k.sb("a_unit", [P, 2 * TPC, D], F32, ctx)
        norm = k.sb("a_norm", [P, 3, 2 * TPC], F32, ctx)
        p_ft = k.ps("a_p_ft", [P, TPC * P], ctx)
        p_kq = k.ps("a_p_kq", [P, TPC, 2 * D], ctx)
        p_t = k.ps("a_p_t", [P, 2, TPC * P], ctx)
        names = ("f_ready", "f_kept", "rows_hi", "rows_lo", "ft_ready", "ft_copied", "kq_ready", "squared", "summed",
                 "rooted", "clamped", "inverted", "unit_ready", "t_ready", "hi_ready", "lo_ready")
        s = {n: k.sem("a_" + n, ctx) for n in names}
        block = ctx.enter_context(nc.Block())

        @block.vector
        def _(dve):
            def group(gg, first):
                for par in range(2):
                    g = 2 * gg + par
                    if not first:
                        dve.wait_ge(s["ft_ready"], g - 1)
                        dve.wait_ge(s["f_kept"], g - 1)
                    for t in range(TPC):
                        nc.vector.tensor_scalar(f[par][:, t, :], k.x[:, ds(TPC * g + t, 1), :],
                                                k.mean[:, ds(TPC * g + t, 1)], k.rstd[:, ds(TPC * g + t, 1)],
                                                ALU.subtract, ALU.mult).then_inc(s["f_ready"], 1)
                    dve.wait_ge(s["f_ready"], TPC * (g + 1))
                    nc.vector.tensor_copy(k.row_hi[:, ds(TPC * g, TPC), 0:D - 1], f[par][:, :, 0:D - 1]).then_inc(s["rows_hi"], 1)
                    dve.wait_ge(s["rows_hi"], g + 1)
                    nc.vector.tensor_tensor(k.row_lo[:, ds(TPC * g, TPC), 0:D - 1], f[par][:, :, 0:D - 1],
                                            k.row_hi[:, ds(TPC * g, TPC), 0:D - 1], ALU.subtract).then_inc(s["rows_lo"], 1)
                    dve.wait_ge(s["squared"], g + 1)
                    nc.vector.tensor_reduce(norm[:, 0, :], square[:], AX.X, ALU.add).then_inc(s["summed"], 1)
                    dve.wait_ge(s["rooted"], g + 1)
                    nc.vector.tensor_scalar(norm[:, 2, :], norm[:, 1, :], COS_EPS, 1.0 / UNIT, ALU.max,
                                            ALU.mult).then_inc(s["clamped"], 1)
                    dve.wait_ge(s["clamped"], g + 1)
                    nc.vector.reciprocal(norm[:, 0, :], norm[:, 2, :]).then_inc(s["inverted"], 1)
                    dve.wait_ge(s["inverted"], g + 1)
                    if not (first and par == 0):
                        dve.wait_ge(s["t_ready"], g)
                    for h in range(2):
                        last = nc.vector.tensor_tensor(
                            unit[:, TPC * h:TPC * h + TPC, :],
                            p_kq[:, 2 * h:2 * h + 2, :].rearrange("p t (w d) -> p (t w) d", w=2),
                            norm[:, 0, TPC * h:TPC * h + TPC].unsqueeze(2).broadcast_to([P, TPC, D]), ALU.mult)
                    last.then_inc(s["unit_ready"], 1)
                    dve.wait_ge(s["hi_ready"], 2 * (g + 1))
                    for w, lo, hi in ((0, k.mov_lo, k.mov_hi), (1, k.sta_lo, k.sta_hi)):
                        last = nc.vector.tensor_tensor(lo[:, ds(CHUNK * g, CHUNK)], p_t[:, w, :],
                                                       hi[:, ds(CHUNK * g, CHUNK)], ALU.subtract)
                    last.then_inc(s["lo_ready"], 1)

            peeled(dve, CHUNKS // 2, group)

        @block.scalar
        def _(act):
            def group(gg, first):
                for par in range(2):
                    g = 2 * gg + par
                    act.wait_ge(s["f_ready"], TPC * (g + 1))
                    nc.scalar.copy(k.f_rows[:, ds(TPC * g, TPC), :], f[par][:]).then_inc(s["f_kept"], 1)
                    act.wait_ge(s["ft_ready"], g + 1)
                    if not first:
                        act.wait_ge(s["kq_ready"], g - 1)
                    nc.scalar.copy(f_t[par][:], p_ft[:]).then_inc(s["ft_copied"], 1)
                    act.wait_ge(s["kq_ready"], g + 1)
                    if not (first and par == 0):
                        act.wait_ge(s["summed"], g)
                    for h in range(2):
                        last = nc.scalar.activation(square[:, TPC * h:TPC * h + TPC, :],
                                                    p_kq[:, 2 * h:2 * h + 2, :].rearrange("p t (w d) -> p (t w) d", w=2),
                                                    ACT.Square)
                    last.then_inc(s["squared"], 1)
                    act.wait_ge(s["summed"], g + 1)
                    if not (first and par == 0):
                        act.wait_ge(s["clamped"], g)
                    nc.scalar.activation(norm[:, 1, :], norm[:, 0, :], ACT.Sqrt).then_inc(s["rooted"], 1)
                    act.wait_ge(s["t_ready"], g + 1)
                    nc.scalar.copy(k.mov_hi[:, ds(CHUNK * g, CHUNK)], p_t[:, 0, :]).then_inc(s["hi_ready"], 1)
                    nc.scalar.copy(k.sta_hi[:, ds(CHUNK * g, CHUNK)], p_t[:, 1, :]).then_inc(s["hi_ready"], 1)

            peeled(act, CHUNKS // 2, group)

        @block.tensor
        def _(pe):
            def group(gg, first):
                for par in range(2):
                    g = 2 * gg + par
                    pe.wait_ge(s["f_ready"], TPC * (g + 1))
                    if not (first and par == 0):
                        pe.wait_ge(s["ft_copied"], g)
                    for t in range(TPC):
                        last = nc.tensor.transpose(p_ft[:, P * t:P * t + P], f[par][:, t, :], k.ident[:])
                    last.then_inc(s["ft_ready"], 1)
                    pe.wait_ge(s["ft_copied"], g + 1)
                    if not (first and par == 0):
                        pe.wait_ge(s["unit_ready"], g)
                    for t in range(TPC):
                        last = nc.tensor.matmul(p_kq[:, t, :], f_t[par][:, P * t:P * t + P], k.wkq_t[:], start=True, stop=True)
                    last.then_inc(s["kq_ready"], 1)
                    pe.wait_ge(s["unit_ready"], g + 1)
                    if not (first and par == 0):
                        pe.wait_ge(s["lo_ready"], g)
                    for t in range(TPC):
                        for w in range(2):
                            last = nc.tensor.transpose(p_t[:, w, P * t:P * t + P], unit[:, 2 * t + w, :], k.ident[:])
                    last.then_inc(s["t_ready"], 1)

            peeled(pe, CHUNKS // 2, group)


def attention(k, tag):
    nc = k.nc
    is_a = tag == "a_"
    RING = 4
    ADJ = 4
    LAG = 3
    adj_dram = k.io["adj_t"]
    with ExitStack() as ctx:
        adj = [k.sb(f"{tag}adj{i}", [P, 2, 2 * CHUNK], I32, ctx) for i in range(ADJ)]
        prob = [k.sb(f"{tag}prob{i}", [P, 2 * CHUNK], F32, ctx) for i in range(RING)]
        hi = [k.sb(f"{tag}hi{i}", [P, 2 * CHUNK], F16, ctx) for i in range(RING)]
        lo = [k.sb(f"{tag}lo{i}", [P, 2 * CHUNK], F16, ctx) for i in range(RING)]
        gathered = k.sb(tag + "gathered", [P, CHUNK], F32, ctx)
        small = k.sb(tag + "small", [P, 4, TPC], F32, ctx)
        rows = k.sb(tag + "rows", [P, 4, TPC, D], F32, ctx)
        p_s = [k.ps(f"{tag}p_s{i}", [P, 2 * CHUNK], ctx) for i in range(2)]
        p_o = k.ps(tag + "p_o", [P, CHUNK], ctx)
        p_r = k.ps(tag + "p_r", [P, 2, 512], ctx)
        names = ("s_ready", "exp_ready", "masked", "hi_ready", "lo_ready", "o_ready", "gathered_ready", "r_ready",
                 "post", "row_part", "elu_exp", "x_done")
        s = {n: k.sem(tag + n, ctx) for n in names}
        adj_in = [k.sem(f"{tag}adj_in{i}", ctx) for i in range(ADJ)]
        block = ctx.enter_context(nc.Block())

        r_row = [p_r[:, t // 2, 129 * (t % 2):129 * (t % 2) + D] for t in range(TPC)]
        den = p_r[:, :, 0:258].rearrange("p b (t e) -> p b t e", e=129)[:, :, :, D]

        @block.sync
        def _(sp):
            def chunk(c, first):
                for q in range(CHUNKS):
                    m = CHUNKS * c + q
                    if not (first and q < ADJ):
                        sp.wait_ge(s["masked"], 2 * (m - ADJ) + 2)
                    sp.dma_start(adj[q % ADJ][:], adj_dram[ds(m, 1)]).then_inc(adj_in[q % ADJ], 16)

            peeled(sp, CHUNKS, chunk)

        @block.tensor
        def _(pe):
            def scores(n, st, first):
                if not (first and st < 2):
                    pe.wait_ge(s["exp_ready"], n - 1)
                c = n_chunk[0]
                for j in range(2):
                    key = ds(P * (2 * n_step[0] + j), P)
                    out = p_s[st % 2][:, CHUNK * j:CHUNK * j + CHUNK]
                    q_hi, q_lo = (m[:, ds(CHUNK * c, CHUNK)] for m in (k.mov_hi, k.mov_lo))
                    nc.tensor.matmul(out, k.sta_hi[:, key], q_hi, start=True, stop=False)
                    nc.tensor.matmul(out, k.sta_hi[:, key], q_lo, start=False, stop=False)
                    last = nc.tensor.matmul(out, k.sta_lo[:, key], q_hi, start=False, stop=True)
                last.then_inc(s["s_ready"], 1)

            def values(n, at, st):
                pe.wait_ge(s["lo_ready"], n + 1)
                b = st % RING
                for j in range(2):
                    t = 2 * at + j
                    part = slice(CHUNK * j, CHUNK * j + CHUNK)
                    begin = isinstance(at, int) and at == 0 and j == 0
                    end = isinstance(at, int) and at == STEPS - 1 and j == 1
                    v_hi, v_lo = (m[:, ds(t, 1), :] for m in (k.row_hi, k.row_lo))
                    nc.tensor.matmul(p_o[:], v_hi, hi[b][:, part], start=begin, stop=False, skip_group_check=True)
                    nc.tensor.matmul(p_o[:], v_hi, lo[b][:, part], start=False, stop=False, skip_group_check=True)
                    last = nc.tensor.matmul(p_o[:], v_lo, hi[b][:, part], start=False, stop=end, skip_group_check=True)
                last.then_inc(s["o_ready"], 1)

            def to_rows(c, first):
                pe.wait_ge(s["gathered_ready"], c + 1)
                if not first:
                    pe.wait_ge(s["post"], c)
                for t in range(TPC):
                    last = nc.tensor.matmul(p_r[:, t // 2, 129 * (t % 2):129 * (t % 2) + 129],
                                            gathered[:, P * t:P * t + P], (k.unaug if is_a else k.wv_aug)[:],
                                            start=True, stop=True)
                last.then_inc(s["r_ready"], 1)

            n_chunk, n_step = [0], [0]

            def chunk(c, first):
                n_chunk[0] = c
                for st in range(4):
                    n_step[0] = st
                    scores(STEPS * c + st, st, first)
                    if st < LAG:
                        if not first:
                            values(STEPS * c + st - LAG, STEPS + st - LAG, st - LAG)
                    else:
                        if not first:
                            pe.wait_ge(s["gathered_ready"], c)
                        values(STEPS * c, 0, 0)
                if not first:
                    to_rows(c - 1, False) if not isinstance(c, int) else to_rows(c - 1, c == 1)
                with pe.Fori(1, STEPS // 4) as q:
                    for st in range(4):
                        n_step[0] = 4 * q + st
                        scores(STEPS * c + 4 * q + st, st, False)
                        values(STEPS * c + 4 * q + st - LAG, 4 * q + st - LAG, (st - LAG) % 4)

            chunk(0, True)
            chunk(1, False)
            with pe.Fori(2, CHUNKS) as c:
                chunk(c, False)
            for st in range(LAG):
                values(STEPS * CHUNKS - LAG + st, STEPS - LAG + st, (STEPS - LAG + st) % RING)
            to_rows(CHUNKS - 1, False)

        @block.scalar
        def _(act):
            def exps(n, st, first):
                act.wait_ge(s["s_ready"], n + 1)
                if not (first and st < RING):
                    act.wait_ge(s["lo_ready"], n - RING + 1)
                nc.scalar.activation(prob[st][:], p_s[st % 2][:], ACT.Exp,
                                     bias=0.0 if is_a else k.shift[:, 0:1],
                                     scale=1.0 / UNIT ** 2 if is_a else k.g_unit[:, 0:1]).then_inc(s["exp_ready"], 1)

            def highs(n, st):
                act.wait_ge(s["masked"], n + 1)
                if not (isinstance(n, int) and n < RING):
                    act.wait_ge(s["o_ready"], n - RING + 1)
                nc.scalar.copy(hi[st][:], prob[st][:]).then_inc(s["hi_ready"], 1)

            def four(c, q, first):
                for st in range(4):
                    exps(STEPS * c + 4 * q + st, st, first)
                    if not (first and st == 0):
                        highs(STEPS * c + 4 * q + st - 1, (st - 1) % 4)

            def chunk(c, first):
                four(c, 0, first)
                four(c, 1, False)
                with act.Fori(2, STEPS // 4) as q:
                    four(c, q, False)
                if not first and not is_a:
                    elu(c - 1)

            def elu(c):
                act.wait_ge(s["row_part"], c + 1)
                nc.scalar.activation(rows[:, 2], rows[:, 1], ACT.Exp).then_inc(s["elu_exp"], 1)

            peeled(act, CHUNKS, chunk)
            highs(STEPS * CHUNKS - 1, 3)
            if not is_a:
                elu(CHUNKS - 1)

        @block.vector
        def _(dve):
            def mask(n, st, first, fill):
                dve.wait_ge(s["exp_ready"], n + 1)
                dve.wait_ge(adj_in[(st // 2) % ADJ], 16 * fill)
                nc.vector.scalar_tensor_tensor(prob[st % RING][:], adj[(st // 2) % ADJ][:, st % 2, :], 0.0,
                                               prob[st % RING][:], ALU.is_gt, ALU.mult).then_inc(s["masked"], 1)

            def lows(n, st):
                dve.wait_ge(s["hi_ready"], n + 1)
                if not (isinstance(n, int) and n < RING):
                    dve.wait_ge(s["o_ready"], n - RING + 1)
                nc.vector.tensor_tensor(lo[st % RING][:], prob[st % RING][:], hi[st % RING][:],
                                        ALU.subtract).then_inc(s["lo_ready"], 1)

            def leave(c, first):
                dve.wait_ge(s["o_ready"], STEPS * (c + 1))
                if not first:
                    dve.wait_ge(s["r_ready"], c)
                nc.vector.tensor_copy(gathered[:], p_o[:]).then_inc(s["gathered_ready"], 1)

            def finish_a(c):
                per = 5 * c
                dve.wait_ge(s["r_ready"], c + 1)
                empty = k.empty[:, ds(TPC * c, TPC)]
                nc.vector.tensor_scalar(empty, den, 0.0, None, ALU.is_equal).then_inc(s["row_part"], 1)
                nc.vector.tensor_scalar(small[:, 0, :], den, 1e-30, 2.0, ALU.max, ALU.mult).then_inc(s["row_part"], 1)
                dve.wait_ge(s["row_part"], per + 2)
                nc.vector.reciprocal(small[:, 1, :], small[:, 0, :]).then_inc(s["row_part"], 1)
                nc.vector.tensor_scalar(small[:, 2, :], empty, 0.5, 0.5, ALU.mult, ALU.add).then_inc(s["row_part"], 1)
                dve.wait_ge(s["row_part"], per + 4)
                for t in range(TPC):
                    xr = k.x[:, ds(TPC * c + t, 1), :]
                    last = nc.vector.scalar_tensor_tensor(rows[:, 0, t, :], r_row[t], small[:, 1, t:t + 1], xr,
                                                          ALU.mult, ALU.add)
                last.then_inc(s["post"], 1)
                dve.wait_ge(s["post"], c + 1)
                for t in range(TPC):
                    last = nc.vector.scalar_tensor_tensor(k.x[:, ds(TPC * c + t, 1), :], k.f_rows[:, ds(TPC * c + t, 1), :],
                                                          small[:, 2, t:t + 1], rows[:, 0, t, :], ALU.mult, ALU.add)
                last.then_inc(s["row_part"], 1)

            def start_b(c):
                dve.wait_ge(s["r_ready"], c + 1)
                nc.vector.tensor_scalar(small[:, 0, :], den, 1e-30, None, ALU.max).then_inc(s["x_done"], 1)
                dve.wait_ge(s["x_done"], 5 * c + 1)
                nc.vector.reciprocal(small[:, 1, :], small[:, 0, :]).then_inc(s["x_done"], 1)
                dve.wait_ge(s["x_done"], 5 * c + 2)
                for t in range(TPC):
                    last = nc.vector.tensor_scalar(rows[:, 3, t, :], r_row[t], small[:, 1, t:t + 1], None, ALU.mult)
                last.then_inc(s["post"], 1)
                dve.wait_ge(s["post"], c + 1)
                for t in range(TPC):
                    last = nc.vector.scalar_tensor_tensor(rows[:, 0, t, :], k.v_mean[:], k.empty[:, ds(TPC * c + t, 1)],
                                                          rows[:, 3, t, :], ALU.mult, ALU.add)
                last.then_inc(s["x_done"], 1)
                dve.wait_ge(s["x_done"], 5 * c + 3)
                nc.vector.tensor_scalar(rows[:, 1], rows[:, 0], 0.0, None, ALU.min).then_inc(s["row_part"], 1)

            def finish_b(c):
                dve.wait_ge(s["elu_exp"], c + 1)
                nc.vector.scalar_tensor_tensor(rows[:, 3], rows[:, 0], 0.0, rows[:, 2], ALU.max, ALU.add).then_inc(s["x_done"], 1)
                dve.wait_ge(s["x_done"], 5 * c + 4)
                xr = k.x[:, ds(TPC * c, TPC), :]
                nc.vector.scalar_tensor_tensor(xr, rows[:, 3], -1.0, xr, ALU.add, ALU.add).then_inc(s["x_done"], 1)

            def chunk(c, first):
                for st in range(4):
                    mask(STEPS * c + st, st, first, 2 * c + 1)
                    if not (first and st == 0):
                        lows(STEPS * c + st - 1, (st - 1) % 4)
                    if st == 2 and not first:
                        leave(c - 1, isinstance(c, int) and c == 1)
                for q in range(1, STEPS // 4):
                    for st in range(4 * q, 4 * q + 4):
                        mask(STEPS * c + st, st, False, 2 * c + 1 + (st // 2) // ADJ)
                        lows(STEPS * c + st - 1, (st - 1) % 4)
                        if st == 5 and not first:
                            finish_a(c - 1) if is_a else start_b(c - 1)
                if not first and not is_a:
                    finish_b(c - 1)

            chunk(0, True)
            chunk(1, False)
            with dve.Fori(2, CHUNKS) as c:
                chunk(c, False)
            lows(STEPS * CHUNKS - 1, 3)
            leave(CHUNKS - 1, False)
            if is_a:
                finish_a(CHUNKS - 1)
            else:
                start_b(CHUNKS - 1)
                finish_b(CHUNKS - 1)


def prepare_weights(k):
    nc = k.nc
    with ExitStack() as ctx:
        scaled = k.sb("w_scaled", [P, D], F32, ctx)
        row = k.sb("w_row", [1, 4, D], F32, ctx)
        m_qk = k.sb("w_m_qk", [P, D], F32, ctx)
        p_a = k.ps("w_p_a", [P, D], ctx)
        p_b = k.ps("w_p_b", [P, D], ctx)
        p_c = k.ps("w_p_c", [P, D], ctx)
        p_d = k.ps("w_p_d", [P, D], ctx)
        p_e = k.ps("w_p_e", [P, D], ctx)
        p_f = k.ps("w_p_f", [P, D], ctx)
        vec = k.sem("w_vec", ctx)
        first_products = k.sem("w_first", ctx)
        second_products = k.sem("w_second", ctx)
        block = ctx.enter_context(nc.Block())

        @block.vector
        def _(dve):
            nc.vector.tensor_scalar(scaled[:], k.w_ffn_t[:], k.lnw[:, 0:1], None, ALU.mult).then_inc(vec, 1)
            nc.vector.memset(k.bias_ffn[:], 0.0).then_inc(vec, 1)
            dve.wait_ge(first_products, 4)
            nc.vector.tensor_scalar(k.w_ffn[:], p_a[:], 2.0, None, ALU.mult)
            nc.vector.tensor_tensor(row[:, 0, :], p_b[0:1, :], k.b_ffn[0:1, :], ALU.add).then_inc(vec, 1)
            nc.vector.tensor_scalar(m_qk[:], p_c[:], D ** -0.5, None, ALU.mult).then_inc(vec, 1)
            nc.vector.tensor_scalar(row[:, 3, :], p_d[0:1, :], D ** -0.5, None, ALU.mult).then_inc(vec, 1)
            dve.wait_ge(vec, 3)
            for t in range(TPC):
                last = nc.vector.tensor_copy(k.bias_ffn[0:1, t, :], row[:, 0, :])
            last.then_inc(vec, 1)
            dve.wait_ge(vec, 6)
            nc.vector.tensor_tensor(row[:, 1, :], row[:, 0, :], k.bias_ffn[0:1, 0, :], ALU.subtract).then_inc(vec, 1)
            dve.wait_ge(vec, 7)
            for t in range(TPC):
                last = nc.vector.tensor_copy(k.bias_ffn[32:33, t, :], row[:, 1, :])
            last.then_inc(vec, 1)
            nc.vector.tensor_copy(k.bias_mid[:], row[:, 1, :]).then_inc(vec, 1)
            dve.wait_ge(vec, 9)
            nc.vector.tensor_tensor(row[:, 2, :], row[:, 1, :], k.bias_mid[:], ALU.subtract).then_inc(vec, 1)
            dve.wait_ge(vec, 10)
            for t in range(TPC):
                nc.vector.tensor_copy(k.bias_ffn[64:65, t, :], row[:, 2, :])
            dve.wait_ge(second_products, 2)
            nc.vector.tensor_copy(k.m_aug[:, 0:D], p_e[:]).then_inc(vec, 1)
            nc.vector.tensor_copy(k.wv_aug[:, 0:D], p_f[:])
            nc.vector.tensor_copy(k.wv_aug[:, D:D + 1], k.unaug[:, D:D + 1])
            dve.wait_ge(vec, 11)
            nc.vector.tensor_scalar(k.m_aug[:, D:2 * D], k.m_aug[:, 0:D], k.m_aug[:, D - 1:D], None, ALU.subtract)

        @block.tensor
        def _(pe):
            pe.wait_ge(vec, 1)
            nc.tensor.matmul(p_a[:], k.center[:], scaled[:], start=True, stop=True).then_inc(first_products, 1)
            nc.tensor.matmul(p_b[0:1, :], k.lnb[:], k.w_ffn_t[:], start=True, stop=True).then_inc(first_products, 1)
            nc.tensor.matmul(p_c[:], k.wq1[:], k.wk1[:], start=True, stop=True).then_inc(first_products, 1)
            nc.tensor.matmul(p_d[0:1, :], k.bq1[:], k.wk1[:], start=True, stop=True).then_inc(first_products, 1)
            pe.wait_ge(vec, 5)
            nc.tensor.matmul(p_e[:], k.unaug_t[:], m_qk[:], start=True, stop=False)
            nc.tensor.matmul(p_e[:], k.last_row[0:1, :], row[:, 3, :], start=False, stop=True).then_inc(second_products, 1)
            nc.tensor.matmul(p_f[:], k.unaug_t[:], k.wv1_t[:], start=True, stop=False)
            nc.tensor.matmul(p_f[:], k.last_row[0:1, :], k.bv1[0:1, :], start=False, stop=True).then_inc(second_products, 1)


def recurrence(k):
    nc = k.nc
    G = T // TPC
    ITEMS = G * STEPS_KERNEL
    YB, TB = 4, 2
    with ExitStack() as ctx:
        def ring(name, n):
            return [k.sb(f"r_{name}{g}", [P, TPC * D], F32, ctx) for g in range(n)]

        R = 4
        tanh, h, z_t, z, z_unit = ring("tanh", R), ring("h", R), ring("z_t", R), ring("z", G), ring("z_unit", G)
        parts = [k.sb(f"r_parts{g}", [P, TPC, 6], F32, ctx) for g in range(G)]
        stat = [k.sb(f"r_stat{g}", [P, 5, TPC], F32, ctx) for g in range(G)]
        p_y = [k.ps(f"r_p_y{i}", [P, TPC * D], ctx) for i in range(YB)]
        p_t = [k.ps(f"r_p_t{i}", [P, TPC * P], ctx) for i in range(TB)]
        names = ("start_ready", "y_ready", "tanh_ready", "h_ready", "z_ready", "halves", "stat1", "stat2", "var_ready",
                 "rstd_ready", "unit_ready", "t_ready", "zt_ready")
        s = {n: k.sem("r_" + n, ctx) for n in names}
        block = ctx.enter_context(nc.Block())

        def tiles(a):
            return a[:].rearrange("p (t d) -> p t d", t=TPC)

        @block.tensor
        def _(pe):
            def start(m):
                pe.wait_ge(s["start_ready"], m + 1)
                if m >= YB:
                    pe.wait_ge(s["h_ready"], m - YB + 1)
                nc.tensor.matmul(p_y[m % YB][:], k.ident[:], z_unit[m][:], start=True, stop=True).then_inc(s["y_ready"], 1)

            def turn(n, g, first):
                pe.wait_ge(s["unit_ready"], n + 1)
                if not (first and g < TB):
                    pe.wait_ge(s["zt_ready"], n - TB + 1)
                for t in range(TPC):
                    last = nc.tensor.transpose(p_t[g % TB][:, P * t:P * t + P], z_unit[g][:, D * t:D * t + D], k.ident[:])
                last.then_inc(s["t_ready"], 1)

            def linear(n, g):
                pe.wait_ge(s["zt_ready"], n + 1)
                pe.wait_ge(s["h_ready"], n + G - YB + 1)
                out = p_y[g % YB]
                nc.tensor.matmul(out[:], k.ones_bf[:], k.bias_ffn[:].rearrange("p t d -> p (t d)"), start=True,
                                 stop=False, skip_group_check=True)
                for t in range(TPC):
                    last = nc.tensor.matmul(out[:, D * t:D * t + D], z_t[g % R][:, P * t:P * t + P], k.w_ffn[:], start=False,
                                            stop=(t == TPC - 1), skip_group_check=True)
                last.then_inc(s["y_ready"], 1)

            for m in range(G):
                start(m)

            def step(i, first):
                for g in range(G):
                    turn(G * i + g, g, first)
                    if not (first and g == 0):
                        linear(G * i + g - 1, (g - 1) % G)

            peeled(pe, STEPS_KERNEL, step)
            linear(ITEMS - 1, G - 1)

        @block.scalar
        def _(act):
            def tanhs(n, g):
                act.wait_ge(s["y_ready"], n + 1)
                nc.scalar.activation(tanh[g % R][:], p_y[g % YB][:], ACT.Tanh).then_inc(s["tanh_ready"], 1)

            def silus(n, g):
                act.wait_ge(s["h_ready"], n + 1)
                nc.scalar.activation(z[g][:], h[g % R][:], ACT.Silu).then_inc(s["z_ready"], 1)

            def leave(n, g):
                act.wait_ge(s["t_ready"], n + 1)
                nc.scalar.copy(z_t[g % R][:], p_t[g % TB][:]).then_inc(s["zt_ready"], 1)

            def step(i, first):
                for g in range(G):
                    tanhs(G * i + g, g)
                    if not (first and g < 1):
                        silus(G * i + g - 1, (g - 1) % G)
                    if not (first and g < 4):
                        leave(G * i + g - 4, (g - 4) % G)

            peeled(act, STEPS_KERNEL, step)
            silus(ITEMS - 1, G - 1)
            for g in range(4, G):
                leave(ITEMS - G + g, g)

        @block.vector
        def _(dve):
            for g in range(G):
                for t in range(TPC):
                    i = TPC * g + t
                    last = nc.vector.tensor_scalar(z_unit[g][:, D * t:D * t + D], k.x[:, i, :], k.mean[:, i:i + 1],
                                                   k.rstd[:, i:i + 1], ALU.subtract, ALU.mult)
                last.then_inc(s["start_ready"], 1)

            def add_tanh(n, g):
                dve.wait_ge(s["tanh_ready"], n + 1)
                nc.vector.scalar_tensor_tensor(h[g % R][:], tanh[g % R][:], 0.01, p_y[g % YB][:], ALU.mult, ALU.add)\
                    .then_inc(s["h_ready"], 1)

            def variance(n, g):
                dve.wait_ge(s["z_ready"], n + 1)
                for t in range(TPC):
                    last = nc.vector.bn_stats(parts[g][:, t, :], z[g][:, D * t:D * t + D])
                last.then_inc(s["halves"], 1)
                dve.wait_ge(s["halves"], n + 1)
                nc.vector.tensor_tensor(stat[g][:, 0, :], parts[g][:, :, 1], parts[g][:, :, 4], ALU.subtract).then_inc(s["stat1"], 1)
                nc.vector.scalar_tensor_tensor(stat[g][:, 1, :], parts[g][:, :, 2], LN_EPS * D, parts[g][:, :, 5], ALU.add,
                                               ALU.add).then_inc(s["stat1"], 1)
                dve.wait_ge(s["stat1"], 2 * n + 1)
                nc.vector.tensor_tensor(stat[g][:, 2, :], stat[g][:, 0, :], stat[g][:, 0, :], ALU.mult).then_inc(s["stat2"], 1)
                dve.wait_ge(s["stat1"], 2 * n + 2)
                dve.wait_ge(s["stat2"], n + 1)
                nc.vector.scalar_tensor_tensor(stat[g][:, 3, :], stat[g][:, 1, :], 4.0 / D, stat[g][:, 2, :], ALU.mult,
                                               ALU.add).then_inc(s["var_ready"], 1)

            def unit(n, g):
                dve.wait_ge(s["rstd_ready"], n + 1)
                nc.vector.tensor_tensor(tiles(z_unit[g]), tiles(z[g]), stat[g][:, 4, :].unsqueeze(2).broadcast_to([P, TPC, D]),
                                        ALU.mult).then_inc(s["unit_ready"], 1)

            def step(i, first):
                for g in range(G):
                    add_tanh(G * i + g, g)
                    if not (first and g < 1):
                        variance(G * i + g - 1, (g - 1) % G)
                    if not (first and g < 3):
                        unit(G * i + g - 3, (g - 3) % G)

            peeled(dve, STEPS_KERNEL, step)
            variance(ITEMS - 1, G - 1)
            for g in range(5, G):
                unit(ITEMS - G + g, g)
            for g in range(G):
                dve.wait_ge(s["y_ready"], ITEMS + g + 1)
                xr = k.x[:, TPC * g:TPC * g + TPC, :]
                nc.vector.tensor_tensor(xr, xr, tiles(p_y[g % YB]), ALU.add).then_inc(s["h_ready"], 1)

        @block.gpsimd
        def _(pool):
            def rstds(n, g):
                pool.wait_ge(s["var_ready"], n + 1)
                nc.gpsimd.tensor_tensor(stat[g][:, 4, :], stat[g][:, 3, :], k.minus_half[:], ALU.pow).then_inc(s["rstd_ready"], 1)

            def step(i, first):
                for g in range(G):
                    rstds(G * i + g, g)

            peeled(pool, STEPS_KERNEL, step)


def normalise_b(k):
    nc = k.nc
    with ExitStack() as ctx:
        f = [k.sb(f"n_f{i}", [P, TPC, D], F32, ctx) for i in range(2)]
        f_t = [k.sb(f"n_f_t{i}", [P, TPC * P], F32, ctx) for i in range(2)]
        square = k.sb("n_square", [P, TPC, D], F32, ctx)
        length = k.sb("n_length", [P, T], F32, ctx)
        f_sum = k.sb("n_f_sum", [P, 1], F32, ctx)
        f_sums = k.sb("n_f_sums", [P, P], F32, ctx)
        p_ft = k.ps("n_p_ft", [P, TPC * P], ctx)
        p_g = k.ps("n_p_g", [P, TPC, 2 * D], ctx)
        p_sum = k.ps("n_p_sum", [P, 1], ctx)
        p_mean = k.ps("n_p_mean", [P, D + 1], ctx)
        names = ("preset", "f_ready", "rows_hi", "rows_lo", "ft_ready", "ft_copied", "hi_ready", "lo_ready", "g_ready",
                 "squared", "summed", "g_kept", "sum_ready", "sum_copied", "sums_ready", "mean_ready")
        s = {n: k.sem("n_" + n, ctx) for n in names}
        block = ctx.enter_context(nc.Block())

        @block.vector
        def _(dve):
            for i in range(2):
                nc.vector.memset(f[i][:, :, D - 1:D], 1.0).then_inc(s["preset"], 1)

            def group(gg, first):
                for par in range(2):
                    g = 2 * gg + par
                    if not first:
                        dve.wait_ge(s["ft_ready"], g - 1)
                    for t in range(TPC):
                        last = nc.vector.tensor_scalar(f[par][:, t, 0:D - 1], k.x[:, ds(TPC * g + t, 1), 0:D - 1],
                                                       k.mean[:, ds(TPC * g + t, 1)], k.rstd[:, ds(TPC * g + t, 1)],
                                                       ALU.subtract, ALU.mult)
                    last.then_inc(s["f_ready"], 1)
                    dve.wait_ge(s["f_ready"], g + 1)
                    nc.vector.tensor_copy(k.row_hi[:, ds(TPC * g, TPC), 0:D - 1], f[par][:, :, 0:D - 1]).then_inc(s["rows_hi"], 1)
                    dve.wait_ge(s["rows_hi"], g + 1)
                    nc.vector.tensor_tensor(k.row_lo[:, ds(TPC * g, TPC), 0:D - 1], f[par][:, :, 0:D - 1],
                                            k.row_hi[:, ds(TPC * g, TPC), 0:D - 1], ALU.subtract).then_inc(s["rows_lo"], 1)
                    dve.wait_ge(s["hi_ready"], g + 1)
                    nc.vector.tensor_tensor(k.sta_lo[:, ds(CHUNK * g, CHUNK)], f_t[par][:], k.sta_hi[:, ds(CHUNK * g, CHUNK)],
                                            ALU.subtract).then_inc(s["lo_ready"], 1)
                    dve.wait_ge(s["squared"], g + 1)
                    nc.vector.tensor_reduce(length[:, ds(TPC * g, TPC)], square[:], AX.X, ALU.add).then_inc(s["summed"], 1)

            peeled(dve, CHUNKS // 2, group)
            dve.wait_ge(s["summed"], CHUNKS)
            nc.vector.tensor_reduce(k.g_length[:, 0:1], length[:], AX.X, ALU.max)
            dve.wait_ge(s["sum_ready"], 1)
            nc.vector.tensor_copy(f_sum[:], p_sum[:]).then_inc(s["sum_copied"], 1)
            dve.wait_ge(s["sum_copied"], 1)
            nc.vector.tensor_scalar(f_sums[:], k.ones[:], f_sum[:, 0:1], None, ALU.mult).then_inc(s["sums_ready"], 1)
            dve.wait_ge(s["mean_ready"], 1)
            nc.vector.tensor_scalar(k.v_mean[:], p_mean[:, 0:D], 1.0 / N, None, ALU.mult)

        @block.scalar
        def _(act):
            def group(gg, first):
                for par in range(2):
                    g = 2 * gg + par
                    act.wait_ge(s["ft_ready"], g + 1)
                    if not first:
                        act.wait_ge(s["g_ready"], g - 1)
                        act.wait_ge(s["lo_ready"], g - 1)
                    nc.scalar.copy(f_t[par][:], p_ft[:]).then_inc(s["ft_copied"], 1)
                    nc.scalar.copy(k.sta_hi[:, ds(CHUNK * g, CHUNK)], p_ft[:]).then_inc(s["hi_ready"], 1)
                    act.wait_ge(s["g_ready"], g + 1)
                    if not (first and par == 0):
                        act.wait_ge(s["summed"], g)
                    for h in range(2):
                        last = nc.scalar.activation(square[:, 2 * h:2 * h + 2, :], p_g[:, 2 * h:2 * h + 2, 0:D], ACT.Square)
                    last.then_inc(s["squared"], 1)
                    for h in range(2):
                        last = nc.scalar.copy(k.f_rows[:, ds(TPC * g + 2 * h, 2), :], p_g[:, 2 * h:2 * h + 2, D:2 * D])
                    last.then_inc(s["g_kept"], 1)

            peeled(act, CHUNKS // 2, group)

        @block.tensor
        def _(pe):
            pe.wait_ge(s["preset"], 2)

            def group(gg, first):
                for par in range(2):
                    g = 2 * gg + par
                    pe.wait_ge(s["f_ready"], g + 1)
                    if not (first and par == 0):
                        pe.wait_ge(s["hi_ready"], g)
                    for t in range(TPC):
                        last = nc.tensor.transpose(p_ft[:, P * t:P * t + P], f[par][:, t, :], k.ident[:])
                    last.then_inc(s["ft_ready"], 1)
                    pe.wait_ge(s["ft_copied"], g + 1)
                    if not (first and par == 0):
                        pe.wait_ge(s["g_kept"], g)
                    for t in range(TPC):
                        last = nc.tensor.matmul(p_g[:, t, :], f_t[par][:, P * t:P * t + P], k.m_aug[:], start=True, stop=True)
                    last.then_inc(s["g_ready"], 1)
                    pe.wait_ge(s["rows_lo"], g + 1)
                    for t in range(TPC):
                        for part in (k.row_hi, k.row_lo):
                            last = nc.tensor.matmul(p_sum[:], part[:, ds(TPC * g + t, 1), :], k.ones_half[:, 0:1],
                                                    start=(first and par == 0 and t == 0 and part is k.row_hi), stop=False,
                                                    skip_group_check=True)

            peeled(pe, CHUNKS // 2, group)
            nc.tensor.matmul(p_sum[:], k.zero_half[:], k.ones_half[:, 0:1], start=False, stop=True,
                             skip_group_check=True).then_inc(s["sum_ready"], 1)
            pe.wait_ge(s["sums_ready"], 1)
            nc.tensor.matmul(p_mean[:], f_sums[:], k.wv_aug[:], start=True, stop=True).then_inc(s["mean_ready"], 1)


def scale_queries(k):
    nc = k.nc
    with ExitStack() as ctx:
        top = k.sb("q_top", [P, 2], F32, ctx)
        unit = [k.sb(f"q_unit{i}", [P, TPC, D], F32, ctx) for i in range(2)]
        p_t = [k.ps(f"q_p_t{i}", [P, TPC * P], ctx) for i in range(2)]
        names = ("top_ready", "rooted", "clamped", "scale_ready", "unit_ready", "t_ready", "hi_ready", "lo_ready")
        s = {n: k.sem("q_" + n, ctx) for n in names}
        block = ctx.enter_context(nc.Block())

        @block.gpsimd
        def _(pool):
            nc.gpsimd.partition_all_reduce(top[:, 0:1], k.g_length[:, 0:1], P, bass.bass_isa.ReduceOp.max).then_inc(s["top_ready"], 1)

        @block.scalar
        def _(act):
            act.wait_ge(s["top_ready"], 1)
            nc.scalar.activation(top[:, 1:2], top[:, 0:1], ACT.Sqrt).then_inc(s["rooted"], 1)

            def group(gg, first):
                for par in range(2):
                    g = 2 * gg + par
                    act.wait_ge(s["t_ready"], g + 1)
                    nc.scalar.copy(k.mov_hi[:, ds(CHUNK * g, CHUNK)], p_t[par][:]).then_inc(s["hi_ready"], 1)

            peeled(act, CHUNKS // 2, group)

        @block.vector
        def _(dve):
            dve.wait_ge(s["rooted"], 1)
            nc.vector.tensor_scalar(k.g_unit[:], top[:, 1:2], 1e-15, 1.0 / 32, ALU.max, ALU.mult).then_inc(s["clamped"], 1)
            dve.wait_ge(s["clamped"], 1)
            nc.vector.reciprocal(k.g_scale[:], k.g_unit[:]).then_inc(s["scale_ready"], 1)
            nc.vector.tensor_scalar(k.wide_scores[:], top[:, 0:1], S_MAX ** 2 / D, None, ALU.is_gt)
            dve.wait_ge(s["scale_ready"], 1)

            def group(gg, first):
                for par in range(2):
                    g = 2 * gg + par
                    if not first:
                        dve.wait_ge(s["t_ready"], g - 1)
                    nc.vector.tensor_scalar(unit[par][:], k.f_rows[:, ds(TPC * g, TPC), :], k.g_scale[:, 0:1], None,
                                            ALU.mult).then_inc(s["unit_ready"], 1)
                    dve.wait_ge(s["hi_ready"], g + 1)
                    nc.vector.tensor_tensor(k.mov_lo[:, ds(CHUNK * g, CHUNK)], p_t[par][:], k.mov_hi[:, ds(CHUNK * g, CHUNK)],
                                            ALU.subtract).then_inc(s["lo_ready"], 1)

            peeled(dve, CHUNKS // 2, group)

        @block.tensor
        def _(pe):
            def group(gg, first):
                for par in range(2):
                    g = 2 * gg + par
                    pe.wait_ge(s["unit_ready"], g + 1)
                    if not first:
                        pe.wait_ge(s["lo_ready"], g - 1)
                    for t in range(TPC):
                        last = nc.tensor.transpose(p_t[par][:, P * t:P * t + P], unit[par][:, t, :], k.ident[:])
                    last.then_inc(s["t_ready"], 1)

            peeled(pe, CHUNKS // 2, group)


def row_maxima(k):
    nc = k.nc
    LIFT = 384.0
    with ExitStack() as ctx:
        adj = k.sb("m_adj", [P, 2, 2 * CHUNK], I32, ctx)
        lifted = k.sb("m_lifted", [P, 2 * CHUNK], F32, ctx)
        masked = k.sb("m_masked", [P, 2 * CHUNK], F32, ctx)
        run = k.sb("m_run", [P, CHUNK], F32, ctx)
        top = k.sb("m_top", [P, 3, TPC], F32, ctx)
        lift = k.sb("m_lift", [P, 1], F32, ctx)
        unit = k.sb("m_unit", [P, TPC, D], F32, ctx)
        p_s = k.ps("m_p_s", [P, 2 * CHUNK], ctx)
        p_t = k.ps("m_p_t", [P, TPC * P], ctx)
        p_q = k.ps("m_p_q", [P, TPC * P], ctx)
        names = ("adj_in", "adj_free", "s_free", "s_ready", "lift_set", "run_step", "turned", "top_step", "unit_ready",
                 "q_turned", "q_hi", "q_lo")
        s = {n: k.sem("m_" + n, ctx) for n in names}
        block = ctx.enter_context(nc.Block())
        TRANSFERS = CHUNKS * STEPS // 2

        def wide(eng):
            return eng.value_load(k.wide_scores[0:1, 0:1], min_val=0, max_val=1) > 0

        @block.sync
        def _(sp):
            with sp.If(wide(sp)):
                with sp.Fori(0, TRANSFERS) as m:
                    sp.wait_ge(s["adj_free"], 2 * m + 1)
                    sp.dma_start(adj[:], k.io["adj_t"][ds(m, 1)]).then_inc(s["adj_in"], 16)

        @block.tensor
        def _(pe):
            with pe.If(wide(pe)):
                with pe.Fori(0, CHUNKS) as c:
                    q_hi, q_lo = (m[:, ds(CHUNK * c, CHUNK)] for m in (k.mov_hi, k.mov_lo))
                    with pe.Fori(0, STEPS) as st:
                        pe.wait_ge(s["s_free"], STEPS * c + st + 1)
                        for j in range(2):
                            key = ds(P * (2 * st + j), P)
                            out = p_s[:, CHUNK * j:CHUNK * j + CHUNK]
                            nc.tensor.matmul(out, k.sta_hi[:, key], q_hi, start=True, stop=False)
                            nc.tensor.matmul(out, k.sta_hi[:, key], q_lo, start=False, stop=False)
                            last = nc.tensor.matmul(out, k.sta_lo[:, key], q_hi, start=False, stop=True)
                        last.then_inc(s["s_ready"], 1)
                    pe.wait_ge(s["run_step"], (2 * STEPS + 1) * (c + 1))
                    for t in range(TPC):
                        last = nc.tensor.transpose(p_t[:, P * t:P * t + P], run[:, P * t:P * t + P], k.ident[:])
                    last.then_inc(s["turned"], 1)
                    pe.wait_ge(s["unit_ready"], c + 1)
                    for t in range(TPC):
                        last = nc.tensor.transpose(p_q[:, P * t:P * t + P], unit[:, t, :], k.ident[:])
                    last.then_inc(s["q_turned"], 1)

        @block.scalar
        def _(act):
            with act.If(wide(act)):
                act.wait_ge(s["lift_set"], 1)
                nc.scalar.activation(lifted[:, 0:1], lift[:], ACT.Identity).then_inc(s["s_free"], 1)
                with act.Fori(0, CHUNKS) as c:
                    with act.Fori(0, STEPS) as st:
                        act.wait_ge(s["s_ready"], STEPS * c + st + 1)
                        act.wait_ge(s["s_free"], STEPS * c + st + 1)
                        act.wait_ge(s["adj_free"], STEPS * c + st + 1)
                        nc.scalar.activation(lifted[:], p_s[:], ACT.Identity, bias=lift[:, 0:1]).then_inc(s["s_free"], 1)
                    act.wait_ge(s["q_turned"], c + 1)
                    nc.scalar.copy(k.mov_hi[:, ds(CHUNK * c, CHUNK)], p_q[:]).then_inc(s["q_hi"], 1)

        @block.vector
        def _(dve):
            with dve.If(wide(dve)):
                nc.vector.memset(lift[:], LIFT).then_inc(s["lift_set"], 1)
                nc.vector.memset(masked[:, 0:1], 0.0).then_inc(s["adj_free"], 1)
                dve.wait_ge(s["adj_free"], 1)
                with dve.Fori(0, CHUNKS) as c:
                    nc.vector.memset(run[:], 0.0).then_inc(s["run_step"], 1)
                    with dve.Fori(0, STEPS // 2) as q:
                        for half in range(2):
                            n = STEPS * c + 2 * q + half
                            dve.wait_ge(s["s_free"], n + 2)
                            dve.wait_ge(s["adj_in"], 8 * (n + 2 - half))
                            dve.wait_ge(s["run_step"], 2 * n + c + 1)
                            nc.vector.scalar_tensor_tensor(masked[:], adj[:, half, :], 0.0, lifted[:], ALU.is_gt,
                                                           ALU.mult).then_inc(s["adj_free"], 1)
                            dve.wait_ge(s["adj_free"], n + 2)
                            for j in range(2):
                                dve.wait_ge(s["run_step"], 2 * n + c + 1 + j)
                                nc.vector.tensor_tensor(run[:], run[:], masked[:, CHUNK * j:CHUNK * j + CHUNK],
                                                        ALU.max).then_inc(s["run_step"], 1)
                    dve.wait_ge(s["turned"], c + 1)
                    nc.vector.tensor_reduce(top[:, 0, :], p_t[:].rearrange("p (t j) -> p t j", t=TPC), AX.X,
                                            ALU.max).then_inc(s["top_step"], 1)
                    dve.wait_ge(s["top_step"], 4 * c + 1)
                    nc.vector.tensor_scalar(top[:, 1, :], top[:, 0, :], -LIFT, -1.0, ALU.add, ALU.mult)\
                        .then_inc(s["top_step"], 1)
                    dve.wait_ge(s["top_step"], 4 * c + 2)
                    nc.vector.scalar_tensor_tensor(top[:, 2, :], top[:, 0, :], 0.0, top[:, 1, :], ALU.is_gt,
                                                   ALU.mult).then_inc(s["top_step"], 1)
                    nc.vector.tensor_scalar(unit[:], k.f_rows[:, ds(TPC * c, TPC), :], k.g_scale[:, 0:1], None,
                                            ALU.mult).then_inc(s["top_step"], 1)
                    dve.wait_ge(s["top_step"], 4 * c + 4)
                    nc.vector.tensor_copy(unit[:, :, D - 1], top[:, 2, :]).then_inc(s["unit_ready"], 1)
                    dve.wait_ge(s["q_hi"], c + 1)
                    nc.vector.tensor_tensor(k.mov_lo[:, ds(CHUNK * c, CHUNK)], p_q[:], k.mov_hi[:, ds(CHUNK * c, CHUNK)],
                                            ALU.subtract).then_inc(s["q_lo"], 1)
                    dve.wait_ge(s["unit_ready"], c + 1)


def scale_experts(k):
    nc = k.nc
    with ExitStack() as ctx:
        square = k.sb("s_square", [P, HID], F32, ctx)
        bound = k.sb("s_bound", [P, 2, HC], F32, ctx)
        own = k.sb("s_own", [P, 3], F32, ctx)
        every = k.sb("s_every", [P, 3], F32, ctx)
        every2 = k.sb("s_every2", [P, 3], F32, ctx)
        wd = k.wd[:].rearrange("p c e d -> p (c e d)")
        p_b = k.ps("s_p_b", [P, HC], ctx)
        names = ("squared", "columns", "rooted", "bounds", "b1", "owned", "all_ready", "scaled", "inverted", "split",
                 "products")
        s = {n: k.sem("s_" + n, ctx) for n in names}
        block = ctx.enter_context(nc.Block())

        @block.scalar
        def _(act):
            nc.scalar.activation(square[:], k.w1[:], ACT.Square).then_inc(s["squared"], 1)
            act.wait_ge(s["columns"], 1)
            nc.scalar.activation(bound[:, 0, :], p_b[:], ACT.Sqrt, scale=float(D)).then_inc(s["rooted"], 1)
            act.wait_ge(s["scaled"], 1)
            nc.scalar.activation(wd, wd, ACT.Copy, scale=k.e_scale[:, 1:2]).then_inc(s["split"], 1)
            act.wait_ge(s["split"], 1)
            nc.scalar.copy(k.wd_hi[:].rearrange("p c e d -> p (c e d)"), wd).then_inc(s["split"], 1)

        @block.tensor
        def _(pe):
            pe.wait_ge(s["squared"], 1)
            for c in range(HC):
                last = nc.tensor.matmul(p_b[:, c:c + 1], square[:, P * c:P * c + P], k.ones[:, 0:1], start=True, stop=True)
            last.then_inc(s["columns"], 1)

        @block.gpsimd
        def _(pool):
            pool.wait_ge(s["owned"], 3)
            nc.gpsimd.partition_all_reduce(every[:], own[:], P, bass.bass_isa.ReduceOp.max).then_inc(s["all_ready"], 1)

        @block.vector
        def _(dve):
            nc.vector.tensor_reduce(own[:, 1:2], wd, AX.X, ALU.max, apply_absolute_value=True).then_inc(s["owned"], 1)
            nc.vector.tensor_reduce(own[:, 2:3], k.wg[:].rearrange("p c e -> p (c e)"), AX.X, ALU.max,
                                    apply_absolute_value=True).then_inc(s["owned"], 1)
            nc.vector.tensor_scalar(bound[:, 1, :], k.b1[:], -1.0, None, ALU.mult).then_inc(s["bounds"], 1)
            dve.wait_ge(s["bounds"], 1)
            nc.vector.tensor_tensor(bound[:, 1, :], bound[:, 1, :], k.b1[:], ALU.max).then_inc(s["bounds"], 1)
            dve.wait_ge(s["bounds"], 2)
            dve.wait_ge(s["rooted"], 1)
            nc.vector.tensor_tensor(bound[:, 0, :], bound[:, 0, :], bound[:, 1, :], ALU.add).then_inc(s["bounds"], 1)
            dve.wait_ge(s["bounds"], 3)
            nc.vector.tensor_reduce(own[:, 0:1], bound[:, 0, :], AX.X, ALU.max).then_inc(s["owned"], 1)
            dve.wait_ge(s["all_ready"], 1)
            nc.vector.tensor_scalar(k.e_unit[:], every[:], 1e-15, 2.0 ** -14, ALU.max, ALU.mult).then_inc(s["inverted"], 1)
            dve.wait_ge(s["inverted"], 1)
            nc.vector.reciprocal(k.e_scale[:], k.e_unit[:]).then_inc(s["scaled"], 1)
            nc.vector.tensor_scalar(k.e_back[:], k.e_unit[:, 1:3], k.e_unit[:, 0:1], None, ALU.mult)
            dve.wait_ge(s["scaled"], 1)
            wg = k.wg[:].rearrange("p c e -> p (c e)")
            nc.vector.tensor_scalar(wg, wg, k.e_scale[:, 2:3], None, ALU.mult).then_inc(s["b1"], 1)
            dve.wait_ge(s["b1"], 1)
            nc.vector.tensor_copy(k.wg_hi[:].rearrange("p c e -> p (c e)"), wg).then_inc(s["b1"], 1)
            dve.wait_ge(s["b1"], 2)
            nc.vector.tensor_tensor(k.wg_lo[:].rearrange("p c e -> p (c e)"), wg,
                                    k.wg_hi[:].rearrange("p c e -> p (c e)"), ALU.subtract)
            dve.wait_ge(s["split"], 2)
            nc.vector.tensor_tensor(k.wd_lo[:].rearrange("p c e d -> p (c e d)"), wd,
                                    k.wd_hi[:].rearrange("p c e d -> p (c e d)"), ALU.subtract)


def experts(k):
    nc = k.nc
    with ExitStack() as ctx:
        f = k.sb("e_f", [P, TPC, D], F32, ctx)
        f_t = k.sb("e_f_t", [P, TPC * P], F32, ctx)
        hid = [k.sb(f"e_hid{i}", [P, CHUNK], F32, ctx) for i in range(2)]
        hid_hi = [k.sb(f"e_hid_hi{i}", [P, HC, CHUNK], F16, ctx) for i in range(2)]
        hid_lo = [k.sb(f"e_hid_lo{i}", [P, HC, CHUNK], F16, ctx) for i in range(2)]
        logit = k.sb("e_logit", [P, TPC, E], F32, ctx)
        shifted = k.sb("e_shifted", [P, TPC, E], F32, ctx)
        expo = k.sb("e_expo", [P, TPC, E], F32, ctx)
        chosen = k.sb("e_chosen", [P, 3, TPC, E], F32, ctx)
        red = k.sb("e_red", [P, 4, TPC], F32, ctx)
        gate = k.sb("e_gate", [P, TPC, E], F32, ctx)
        gate_y = [k.sb(f"e_gate_y{i}", [P, TPC, E], F32, ctx) for i in range(2)]
        gate_t = k.sb("e_gate_t", [E, TPC * P], F32, ctx)
        acc = [k.sb(f"e_acc{i}", [P, TPC, D], F32, ctx) for i in range(2)]
        p_ft = k.ps("e_p_ft", [P, TPC * P], ctx)
        p_h = [k.ps(f"e_p_h{i}", [P, CHUNK], ctx) for i in range(2)]
        p_l = k.ps("e_p_l", [P, TPC, E], ctx)
        p_gt = k.ps("e_p_gt", [P, TPC * P], ctx)
        p_y = [k.ps(f"e_p_y{i}", [P, E // 2, D], ctx) for i in range(2)]
        p_b = k.ps("e_p_b", [P, TPC, D], ctx)
        names = ("f_ready", "ft_ready", "ft_copied", "h_ready", "gelu_ready", "hi_ready", "lo_ready", "l_ready", "logits",
                 "tops", "shifts", "exps", "sums", "recips", "equals", "ranks", "firsts", "choices", "gates", "gates_y",
                 "gt_ready", "gt_copied", "b_ready", "acc_started", "y_ready", "sum_step")
        s = {n: k.sem("e_" + n, ctx) for n in names}
        ROUNDS = 2 * TPC
        SUMS = E // 2
        stored = [k.sem(f"e_stored{i}", ctx) for i in range(2)]
        out_dram = k.io["out"].rearrange("(t p) d -> p t d", p=P)
        block = ctx.enter_context(nc.Block())

        @block.sync
        def _(sp):
            with sp.Fori(0, CHUNKS // 2) as cc:
                for par in range(2):
                    c = 2 * cc + par
                    sp.wait_ge(s["sum_step"], SUMS * ROUNDS * (c + 1))
                    sp.dma_start(out_dram[:, ds(TPC * c, TPC), :], acc[par][:]).then_inc(stored[par], 16)
            for par in range(2):
                sp.wait_ge(stored[par], 16 * (CHUNKS // 2))

        @block.tensor
        def _(pe):
            def hidden(c, par, first):
                pe.wait_ge(s["f_ready"], c + 1)
                if not first:
                    pe.wait_ge(s["ft_copied"], c)
                for t in range(TPC):
                    last = nc.tensor.transpose(p_ft[:, P * t:P * t + P], f[:, t, :], k.ident[:])
                last.then_inc(s["ft_ready"], 1)
                pe.wait_ge(s["ft_copied"], c + 1)
                for h in range(HC):
                    if not (first and h < 2):
                        pe.wait_ge(s["gelu_ready"], HC * c + h - 1)
                    nc.tensor.matmul(p_h[h % 2][:], k.w1[:, P * h:P * h + P], f_t[:], start=True, stop=True)\
                        .then_inc(s["h_ready"], 1)

            def logits(c, par, first):
                pe.wait_ge(s["lo_ready"], HC * (c + 1))
                if not first:
                    pe.wait_ge(s["logits"], c)
                for t in range(TPC):
                    rows = slice(P * t, P * t + P)
                    for h in range(HC):
                        nc.tensor.matmul(p_l[:, t, :], hid_hi[par][:, h, rows], k.wg_hi[:, h, :], start=(h == 0), stop=False)
                        nc.tensor.matmul(p_l[:, t, :], hid_hi[par][:, h, rows], k.wg_lo[:, h, :], start=False, stop=False)
                        last = nc.tensor.matmul(p_l[:, t, :], hid_lo[par][:, h, rows], k.wg_hi[:, h, :], start=False,
                                                stop=(h == HC - 1))
                last.then_inc(s["l_ready"], 1)

            def biases(c, first):
                pe.wait_ge(s["gates"], c + 1)
                if not first:
                    pe.wait_ge(s["gt_copied"], c)
                for t in range(TPC):
                    last = nc.tensor.transpose(p_gt[0:E, P * t:P * t + P], gate[:, t, :], k.ident[:])
                last.then_inc(s["gt_ready"], 1)
                pe.wait_ge(s["gt_copied"], c + 1)
                if not first:
                    pe.wait_ge(s["acc_started"], c)
                for t in range(TPC):
                    last = nc.tensor.matmul(p_b[:, t, :], gate_t[:, P * t:P * t + P], k.bd[0:E, :], start=True, stop=True)
                last.then_inc(s["b_ready"], 1)

            def products(c, par, first, t):
                for half in range(2):
                    r = 2 * t + half
                    if not (first and r < 2):
                        pe.wait_ge(s["sum_step"], SUMS * (ROUNDS * c + r - 1))
                    rows = slice(P * t, P * t + P)
                    out = p_y[half][:].rearrange("p e d -> p (e d)")
                    for h in range(HC):
                        w_hi, w_lo = (w[:, h, 4 * half:4 * half + 4, :].rearrange("p e d -> p (e d)")
                                      for w in (k.wd_hi, k.wd_lo))
                        nc.tensor.matmul(out, hid_hi[par][:, h, rows], w_hi, start=(h == 0), stop=False)
                        nc.tensor.matmul(out, hid_hi[par][:, h, rows], w_lo, start=False, stop=False)
                        last = nc.tensor.matmul(out, hid_lo[par][:, h, rows], w_hi, start=False, stop=(h == HC - 1))
                    last.then_inc(s["y_ready"], 1)

            def chunk(c, par, first=False, last=False):
                biases(c, first)
                if not last:
                    hidden(c + 1, 1 - par, False)
                products(c, par, first, 0)
                products(c, par, first, 1)
                if not last:
                    logits(c + 1, 1 - par, False)
                products(c, par, first, 2)
                products(c, par, first, 3)

            hidden(0, 0, True)
            logits(0, 0, True)
            chunk(0, 0, first=True)
            chunk(1, 1)
            with pe.Fori(1, CHUNKS // 2 - 1) as cc:
                chunk(2 * cc, 0)
                chunk(2 * cc + 1, 1)
            chunk(CHUNKS - 2, 0)
            chunk(CHUNKS - 1, 1, last=True)

        @block.scalar
        def _(act):
            def front(c, par, first):
                act.wait_ge(s["ft_ready"], c + 1)
                if not first:
                    act.wait_ge(s["h_ready"], HC * c)
                nc.scalar.copy(f_t[:], p_ft[:]).then_inc(s["ft_copied"], 1)
                for h in range(HC):
                    act.wait_ge(s["h_ready"], HC * c + h + 1)
                    if not (first and h < 2):
                        act.wait_ge(s["lo_ready"], HC * c + h - 1)
                    nc.scalar.activation(hid[h % 2][:], p_h[h % 2][:], ACT.Gelu, bias=k.b1[:, h:h + 1])\
                        .then_inc(s["gelu_ready"], 1)
                    act.wait_ge(s["gelu_ready"], HC * c + h + 1)
                    if h == 0 and not (isinstance(c, int) and c < 2):
                        act.wait_ge(s["y_ready"], ROUNDS * (c - 1))
                    nc.scalar.activation(hid_hi[par][:, h, :], hid[h % 2][:], ACT.Copy, scale=k.e_scale[:, 0:1])\
                        .then_inc(s["hi_ready"], 1)

            front(0, 0, True)

            def step(c, par, first=False, last=False):
                act.wait_ge(s["shifts"], c + 1)
                nc.scalar.activation(expo[:], shifted[:], ACT.Exp).then_inc(s["exps"], 1)
                act.wait_ge(s["gt_ready"], c + 1)
                if not first:
                    act.wait_ge(s["b_ready"], c)
                nc.scalar.copy(gate_t[:], p_gt[0:E, :]).then_inc(s["gt_copied"], 1)
                if not last:
                    front(c + 1, 1 - par, False)

            step(0, 0, first=True)
            step(1, 1)
            with act.Fori(1, CHUNKS // 2 - 1) as cc:
                step(2 * cc, 0)
                step(2 * cc + 1, 1)
            step(CHUNKS - 2, 0)
            step(CHUNKS - 1, 1, last=True)

        @block.vector
        def _(dve):
            def rows(c, first):
                if not first:
                    dve.wait_ge(s["ft_ready"], c)
                for t in range(TPC):
                    last = nc.vector.tensor_scalar(f[:, t, :], k.x[:, ds(TPC * c + t, 1), :],
                                                   k.mean[:, ds(TPC * c + t, 1)], k.rstd[:, ds(TPC * c + t, 1)],
                                                   ALU.subtract, ALU.mult)
                last.then_inc(s["f_ready"], 1)

            def lows(c, par):
                for h in range(HC):
                    dve.wait_ge(s["hi_ready"], HC * c + h + 1)
                    nc.vector.scalar_tensor_tensor(hid_lo[par][:, h, :], hid[h % 2][:], k.e_scale[:, 0:1],
                                                   hid_hi[par][:, h, :], ALU.mult, ALU.subtract).then_inc(s["lo_ready"], 1)

            def wide(a):
                return a.unsqueeze(2).broadcast_to([P, TPC, E])

            def choose(c, par, first):
                dve.wait_ge(s["l_ready"], c + 1)
                nc.vector.scalar_tensor_tensor(logit[:].rearrange("p t e -> p (t e)"), p_l[:].rearrange("p t e -> p (t e)"),
                                               k.e_back[:, 1:2], k.bg[:], ALU.mult, ALU.add).then_inc(s["logits"], 1)
                dve.wait_ge(s["logits"], c + 1)
                nc.vector.tensor_reduce(red[:, 0, :], logit[:], AX.X, ALU.max).then_inc(s["tops"], 1)
                dve.wait_ge(s["tops"], c + 1)
                nc.vector.tensor_tensor(shifted[:], logit[:], wide(red[:, 0, :]), ALU.subtract).then_inc(s["shifts"], 1)
                nc.vector.tensor_tensor(chosen[:, 0], logit[:], wide(red[:, 0, :]), ALU.is_equal).then_inc(s["equals"], 1)
                dve.wait_ge(s["equals"], c + 1)
                nc.vector.tensor_tensor(chosen[:, 1], chosen[:, 0], k.ranks[:], ALU.mult).then_inc(s["ranks"], 1)
                dve.wait_ge(s["ranks"], c + 1)
                nc.vector.tensor_reduce(red[:, 1, :], chosen[:, 1], AX.X, ALU.max).then_inc(s["firsts"], 1)
                dve.wait_ge(s["firsts"], c + 1)
                nc.vector.tensor_tensor(chosen[:, 2], chosen[:, 1], wide(red[:, 1, :]), ALU.is_equal).then_inc(s["choices"], 1)
                dve.wait_ge(s["exps"], c + 1)
                nc.vector.tensor_reduce(red[:, 2, :], expo[:], AX.X, ALU.add).then_inc(s["sums"], 1)
                dve.wait_ge(s["sums"], c + 1)
                nc.vector.reciprocal(red[:, 3, :], red[:, 2, :]).then_inc(s["recips"], 1)
                dve.wait_ge(s["recips"], c + 1)
                dve.wait_ge(s["choices"], c + 1)
                if not first:
                    dve.wait_ge(s["gt_ready"], c)
                nc.vector.tensor_tensor(gate[:], chosen[:, 2], wide(red[:, 3, :]), ALU.mult).then_inc(s["gates"], 1)
                dve.wait_ge(s["gates"], c + 1)
                nc.vector.tensor_scalar(gate_y[par][:], gate[:], k.e_back[:, 0:1], None, ALU.mult).then_inc(s["gates_y"], 1)

            def begin(c, par):
                dve.wait_ge(s["b_ready"], c + 1)
                if not (isinstance(c, int) and c < 2):
                    dve.wait_ge(stored[par], 8 * (c - par))
                nc.vector.tensor_tensor(acc[par][:], p_b[:], k.x[:, ds(TPC * c, TPC), :], ALU.add).then_inc(s["acc_started"], 1)

            def add(c, par, t):
                dve.wait_ge(s["gates_y"], c + 1)
                for half in range(2):
                    r = 2 * t + half
                    dve.wait_ge(s["y_ready"], ROUNDS * c + r + 1)
                    for e in range(SUMS):
                        if r == 0 and e == 0:
                            dve.wait_ge(s["acc_started"], c + 1)
                        else:
                            dve.wait_ge(s["sum_step"], SUMS * (ROUNDS * c + r) + e)
                        nc.vector.scalar_tensor_tensor(acc[par][:, t, :], p_y[half][:, e, :],
                                                       gate_y[par][:, t, SUMS * half + e:SUMS * half + e + 1],
                                                       acc[par][:, t, :], ALU.mult, ALU.add).then_inc(s["sum_step"], 1)

            def step(c, par, first=False, last=False, rows_left=True):
                begin(c, par)
                add(c, par, 0)
                if rows_left:
                    rows(c + 2, False)
                if not last:
                    lows(c + 1, 1 - par)
                add(c, par, 1)
                if not last:
                    choose(c + 1, 1 - par, False)
                add(c, par, 2)
                add(c, par, 3)

            rows(0, True)
            rows(1, False)
            lows(0, 0)
            choose(0, 0, True)
            step(0, 0, first=True)
            step(1, 1)
            with dve.Fori(1, CHUNKS // 2 - 1) as cc:
                step(2 * cc, 0)
                step(2 * cc + 1, 1)
            step(CHUNKS - 2, 0, rows_left=False)
            step(CHUNKS - 1, 1, last=True, rows_left=False)


def build(nc, io):
    with ExitStack() as ctx:
        k = Core(nc, ctx, io)
        k.x = k.sb("x_rows", [P, T, D])
        k.f_rows = k.sb("f_rows", [P, T, D])
        k.row_hi, k.row_lo = (k.sb(n, [P, T, D], F16) for n in ("row_hi", "row_lo"))
        k.mov_hi, k.mov_lo = (k.sb(n, [P, N], F16) for n in ("mov_hi", "mov_lo"))
        k.sta_hi, k.sta_lo = (k.sb(n, [P, N], F16) for n in ("sta_hi", "sta_lo"))
        k.mean, k.rstd, k.empty = (k.sb(n, [P, T]) for n in ("mean", "rstd", "empty"))
        k.ident, k.center, k.unaug_t = (k.sb(n, [P, D]) for n in ("ident", "center", "unaug_t"))
        k.unaug, k.wv_aug = (k.sb(n, [P, D + 1]) for n in ("unaug", "wv_aug"))
        k.ones = k.sb("ones", [P, P])
        k.ones_bf = k.sb("ones_bf", [P, P], BF16)
        k.ones_half = k.sb("ones_half", [P, 1], F16)
        k.zero_half = k.sb("zero_half", [P, P], F16)
        k.last_row = k.sb("last_row", [1, P])
        k.minus_half = k.sb("minus_half", [P, TPC])
        k.eps, k.shift = (k.sb(n, [P, 1]) for n in ("eps", "shift"))
        k.wkq_t = k.sb("wkq_t", [P, 2 * D])
        k.lnw, k.lnb, k.bq1 = (k.sb(n, [P, 1]) for n in ("lnw_col", "lnb_col", "bq1_col"))
        k.b_ffn, k.bv1 = (k.sb(n, [1, D]) for n in ("b_ffn_row", "bv1_row"))
        k.w_ffn_t, k.w_ffn, k.wq1, k.wk1 = (k.sb(n, [P, D]) for n in ("w_ffn_raw", "w_ffn", "wq1_raw", "wk1_raw"))
        k.wv1_t = k.sb("wv1_raw", [P, D])
        k.bias_ffn = k.sb("bias_ffn", [P, TPC, D], BF16)
        k.bias_mid = k.sb("bias_mid", [1, D], BF16)
        k.m_aug = k.sb("m_aug", [P, 2 * D])
        k.v_mean = k.sb("v_mean", [P, D])
        k.g_length, k.g_unit, k.g_scale = (k.sb(n, [P, 1]) for n in ("g_length", "g_unit", "g_scale"))
        k.wide_scores = k.sb("wide_scores", [P, 1], I32)
        k.w1 = k.sb("w1_raw", [P, HID])
        k.b1 = k.sb("b1_cols", [P, HC])
        k.wg = k.sb("wg_raw", [P, HC, E])
        k.wg_hi, k.wg_lo = (k.sb(n, [P, HC, E], F16) for n in ("wg_hi", "wg_lo"))
        k.bg, k.ranks = k.sb("bg_rows", [P, TPC * E]), k.sb("ranks", [P, TPC, E])
        k.wd = k.sb("wd_raw", [P, HC, E, D])
        k.wd_hi, k.wd_lo = (k.sb(n, [P, HC, E, D], F16) for n in ("wd_hi", "wd_lo"))
        k.bd = k.sb("bd_rows", [E, D])
        k.e_unit, k.e_scale, k.e_back = (k.sb(n, [P, w]) for n, w in (("e_unit", 3), ("e_scale", 3), ("e_back", 2)))

        load(k)
        prepare_weights(k)
        scale_experts(k)
        row_stats(k, "sa_")
        normalise_a(k)
        attention(k, "a_")
        row_stats(k, "sr_")
        recurrence(k)
        row_stats(k, "sb_")
        normalise_b(k)
        scale_queries(k)
        row_maxima(k)
        attention(k, "b_")
        row_stats(k, "se_")
        experts(k)


def kernel(**inputs):
    import numpy as np
    import concourse.bacc as bacc
    from concourse.bass_utils import run_bass_kernel_spmd

    a = {n: np.ascontiguousarray(v) for n, v in inputs.items()}
    eye = np.eye(D, dtype=np.float32)
    unaug = np.concatenate([eye, eye[:, D - 1:]], axis=1)
    unaug[:D - 1, D - 1] = -1.0
    unaug[D - 1, D - 1] = 0.0
    arrays = {
        "x": a["x"],
        "adj_t": a["adj"].reshape(CHUNKS, CHUNK, STEPS // 2, 2, 2, P).transpose(0, 2, 5, 3, 4, 1)
                         .reshape(CHUNKS * STEPS // 2, P, 2, 2 * CHUNK),
        "wk0_t": a["L0_gnn_Wk"].T, "wq0_t": a["L0_gnn_Wq"].T,
        "lnw": a["L0_ffn_ln_w"].reshape(D, 1), "lnb": a["L0_ffn_ln_b"].reshape(D, 1),
        "w_ffn_t": a["L0_ffn_W"].T, "b_ffn": a["L0_ffn_b"].reshape(1, D),
        "wq1": a["L1_gnn_Wq"], "wk1": a["L1_gnn_Wk"], "wv1_t": a["L1_gnn_Wv"].T,
        "bq1": a["L1_gnn_bq"].reshape(D, 1), "bv1": a["L1_gnn_bv"].reshape(1, D),
        "w1": a["L1_ffn_W1"], "b1": a["L1_ffn_b1"].reshape(HC, P).T,
        "wg": a["L1_ffn_Wg"].reshape(HC, P, E).transpose(1, 0, 2),
        "bg": np.broadcast_to(a["L1_ffn_bg"], (P, TPC, E)).reshape(P, TPC * E),
        "wd": a["L1_ffn_Wd"].reshape(E, HC, P, D).transpose(2, 1, 0, 3),
        "bd": a["L1_ffn_bd"],
        "eye": eye, "centering": eye - np.float32(1.0 / D), "unaugment": unaug,
        "unaugment_t": unaug[:, :D].T, "last_row": eye[D - 1:],
        "ranks": np.broadcast_to(np.arange(E, 0, -1, dtype=np.float32), (P, TPC, E)),
    }
    arrays = {n: np.ascontiguousarray(v) for n, v in arrays.items()}
    nc = bacc.Bacc("TRN2", target_bir_lowering=False, num_devices=1)
    io = {n: nc.dram_tensor("in_" + n, v.shape, mybir.dt.from_np(v.dtype), kind="ExternalInput").ap()
          for n, v in arrays.items()}
    io["out"] = nc.dram_tensor("out_x", (N, D), F32, kind="ExternalOutput").ap()
    build(nc, io)
    result = run_bass_kernel_spmd(nc, [{"in_" + n: v for n, v in arrays.items()}], core_ids=[0])
    return result.results[0]["out_x"]
```

```python
from contextlib import ExitStack

import concourse.bass as bass
from concourse import mybir

F32 = mybir.dt.float32
F16 = mybir.dt.float16
BF16 = mybir.dt.bfloat16
I32 = mybir.dt.int32
ALU = mybir.AluOpType
ACT = mybir.ActivationFunctionType
AX = mybir.AxisListType
ds = bass.ds

P = 128
N = 4096
D = 128
T = N // P
CHUNK = 512
CHUNKS = N // CHUNK
TPC = CHUNK // P
STEPS = T // 2
STEPS_KERNEL = 30
HID = 512
HC = HID // P
E = 8
LN_EPS = 1e-5
COS_EPS = 1e-4
UNIT = 64.0
SHIFT = 3.5
S_MAX = 7.25


class Core:

    def __init__(self, nc, ctx, io):
        self.nc, self.ctx, self.io = nc, ctx, io

    def sb(self, name, shape, dt=F32, ctx=None):
        return (ctx or self.ctx).enter_context(self.nc.sbuf_tensor(name, shape, dt))

    def ps(self, name, shape, ctx):
        return ctx.enter_context(self.nc.psum_tensor(name, shape, F32))

    def sem(self, name, ctx):
        return ctx.enter_context(self.nc.semaphore(name))


def peeled(eng, n, body):
    body(0, True)
    with eng.Fori(1, n) as i:
        body(i, False)


def slots(eng, tail, slot):
    slot(0, 0)
    slot(1, 1)
    with eng.Fori(1, CHUNKS // 2) as i:
        slot(2 * i, 0)
        slot(2 * i + 1, 1)
    for i in range(CHUNKS, CHUNKS + tail):
        slot(i, i % 2)


def has(i, lag):
    return not isinstance(i, int) or 0 <= i - lag < CHUNKS


def past(g, before):
    return not isinstance(g, int) or g >= before


def load(k):
    nc, io = k.nc, k.io
    with ExitStack() as ctx:
        loaded = k.sem("loaded", ctx)
        x_in = [k.sem(f"x_in{i}", ctx) for i in range(4)]
        preset = k.sem("preset", ctx)
        x_stats = row_stats(k, "l_", ctx)
        block = ctx.enter_context(nc.Block())

        @block.sync
        def _(sp):
            for i in range(4):
                sp.dma_start(k.x[:, 8 * i:8 * i + 8, :],
                             io["x"].rearrange("(t p) d -> p t d", p=P)[:, 8 * i:8 * i + 8, :]).then_inc(x_in[i], 16)
            pairs = [(k.ident[:], io["eye"]), (k.center[:], io["centering"]), (k.unaug[:], io["unaugment"]),
                      (k.unaug_t[:], io["unaugment_t"]), (k.last_row[:], io["last_row"]), (k.ranks[:], io["ranks"]),
                      (k.wkq_t[:, 0:D], io["wk0_t"]), (k.wkq_t[:, D:2 * D], io["wq0_t"]),
                      (k.lnw[:], io["lnw"]), (k.lnb[:], io["lnb"]), (k.w_ffn_t[:], io["w_ffn_t"]),
                      (k.b_ffn[0:1, :], io["b_ffn"]), (k.wq1[:], io["wq1"]), (k.wk1[:], io["wk1"]),
                      (k.wv1_t[:], io["wv1_t"]), (k.bq1[:], io["bq1"]), (k.bv1[0:1, :], io["bv1"]),
                      (k.w1[:], io["w1"]), (k.b1[:], io["b1"]), (k.wg[:], io["wg"]), (k.bg[:], io["bg"]),
                      (k.wd[:], io["wd"]), (k.bd[0:E, :], io["bd"])]
            for to, of in pairs:
                sp.dma_start(to, of).then_inc(loaded, 16)
            sp.wait_ge(loaded, 16 * len(pairs))

        @block.vector
        def _(dve):
            nc.vector.memset(k.row_hi[:, :, D - 1:D], 1.0)
            nc.vector.memset(k.row_lo[:, :, D - 1:D], 0.0)
            nc.vector.memset(k.ones_bf[:], 1.0)
            nc.vector.memset(k.ones[:], 1.0)
            nc.vector.memset(k.ones_half[:], 1.0)
            nc.vector.memset(k.zero_half[:], 0.0)
            nc.vector.memset(k.shift[:], SHIFT)
            nc.vector.memset(k.minus_half[:], -0.5)
            nc.vector.memset(k.inv_d[:], 1.0 / D)
            nc.vector.memset(k.eps[:], LN_EPS)
            nc.vector.memset(k.eps_sum[:], LN_EPS * D).then_inc(preset, 1)
            for g in range(CHUNKS):
                dve.wait_ge(x_in[g // 2], 16)
                measure_rows(k, x_stats, g)

        @block.gpsimd
        def _(pool):
            pool.wait_ge(preset, 1)
            peeled(pool, T // TPC, lambda g, first: invert_rows(k, x_stats, pool, g))


def row_stats(k, tag, ctx):
    names = ("measured", "inverting")
    s = {n: k.sem(tag + n, ctx) for n in names}
    s["variance"] = k.sb(tag + "variance", [P, 2, TPC], F32, ctx)
    return s


def measure_rows(k, s, g):
    for i in range(TPC // 2):
        k.nc.vector.bn_stats(k.x_stats[:, ds(TPC // 2 * g + i, 1), :],
                             k.x[:, ds(TPC * g + 2 * i, 2), :].rearrange("p t d -> p d t")).then_inc(s["measured"], 1)


def invert_rows(k, s, pool, g):
    nc = k.nc
    var, padded = s["variance"][:, 0], s["variance"][:, 1]
    pool.wait_ge(s["measured"], TPC // 2 * (g + 1))
    nc.gpsimd.tensor_tensor(var.rearrange("p (a b) -> p a b", b=2), k.x_stats[:, ds(TPC // 2 * g, TPC // 2), 2:6:3],
                            k.inv_d[:].rearrange("p (a b) -> p a b", b=2), ALU.mult).then_inc(s["inverting"], 1)
    pool.wait_ge(s["inverting"], 3 * g + 1)
    nc.gpsimd.tensor_tensor(padded, var, k.eps[:], ALU.add).then_inc(s["inverting"], 1)
    pool.wait_ge(s["inverting"], 3 * g + 2)
    nc.gpsimd.tensor_tensor(k.rstd[:, ds(TPC * g, TPC)], padded, k.minus_half[:], ALU.pow).then_inc(s["inverting"], 1)
    pool.wait_ge(s["inverting"], 3 * g + 3)


def normalised(k, out, g, t, features=D):
    tile = ds(TPC * g + t, 1)
    mean = k.x_stats[:, ds(TPC // 2 * g + t // 2, 1), 1 + 3 * (t % 2)]
    return k.nc.vector.tensor_scalar(out, k.x[:, tile, 0:features], mean, k.rstd[:, tile], ALU.subtract, ALU.mult)


def normalise_a(k):
    nc = k.nc
    with ExitStack() as ctx:
        f = [k.sb(f"a_f{i}", [P, TPC, D], F32, ctx) for i in range(2)]
        f_t = [k.sb(f"a_f_t{i}", [P, TPC * P], F32, ctx) for i in range(2)]
        square = k.sb("a_square", [P, 2 * TPC, D], F32, ctx)
        unit = k.sb("a_unit", [P, 2 * TPC, D], F32, ctx)
        norm = k.sb("a_norm", [P, 4, 2 * TPC], F32, ctx)
        p_ft = k.ps("a_p_ft", [P, TPC * P], ctx)
        p_kq = [k.ps(f"a_p_kq{i}", [P, TPC, 2 * D], ctx) for i in range(2)]
        p_t = k.ps("a_p_t", [P, 2, TPC * P], ctx)
        names = ("f_ready", "rows_hi", "rows_lo", "ft_ready", "ft_copied", "kq_ready", "squared", "rooted", "clamped",
                 "inverted", "unit_ready", "t_ready", "hi_ready", "lo_ready")
        s = {n: k.sem("a_" + n, ctx) for n in names}
        block = ctx.enter_context(nc.Block())

        @block.vector
        def _(dve):
            def normalise(g, b):
                if past(g, 2):
                    dve.wait_ge(s["ft_ready"], g - 1)
                    dve.wait_ge(s["rows_hi"], g - 1)
                    dve.wait_ge(s["rows_lo"], g - 1)
                for t in range(TPC):
                    last = normalised(k, f[b][:, t, :], g, t)
                last.then_inc(s["f_ready"], 1)

            def scale(g, b):
                dve.wait_ge(s["rooted"], g + 1)
                nc.vector.tensor_scalar(norm[:, 2, :], norm[:, 1, :], COS_EPS, 1.0 / UNIT, ALU.max,
                                        ALU.mult).then_inc(s["clamped"], 1)
                dve.wait_ge(s["clamped"], g + 1)
                nc.vector.reciprocal(norm[:, 3, :], norm[:, 2, :]).then_inc(s["inverted"], 1)
                dve.wait_ge(s["inverted"], g + 1)
                if past(g, 1):
                    dve.wait_ge(s["t_ready"], g)
                for h in range(2):
                    last = nc.vector.tensor_tensor(
                        unit[:, TPC * h:TPC * h + TPC, :],
                        p_kq[b][:, 2 * h:2 * h + 2, :].rearrange("p t (w d) -> p (t w) d", w=2),
                        norm[:, 3, TPC * h:TPC * h + TPC].unsqueeze(2).broadcast_to([P, TPC, D]), ALU.mult)
                last.then_inc(s["unit_ready"], 1)

            def lows(g):
                dve.wait_ge(s["hi_ready"], g + 1)
                for w, lo, hi in ((0, k.mov_lo, k.mov_hi), (1, k.sta_lo, k.sta_hi)):
                    last = nc.vector.tensor_tensor(lo[:, ds(CHUNK * g, CHUNK)], p_t[:, w, :],
                                                   hi[:, ds(CHUNK * g, CHUNK)], ALU.subtract)
                last.then_inc(s["lo_ready"], 1)

            def slot(i, b):
                if has(i, 0):
                    normalise(i, b)
                if has(i, 2):
                    lows(i - 2)
                if has(i, 1):
                    scale(i - 1, 1 - b)

            slots(dve, 2, slot)

        @block.gpsimd
        def _(pool):
            def slot(i, b):
                pool.wait_ge(s["rows_hi"], i + 1)
                nc.gpsimd.tensor_tensor(k.row_lo[:, ds(TPC * i, TPC), 0:D - 1], f[b][:, :, 0:D - 1],
                                        k.row_hi[:, ds(TPC * i, TPC), 0:D - 1], ALU.subtract).then_inc(s["rows_lo"], 1)

            slots(pool, 0, slot)

        @block.scalar
        def _(act):
            def lengths(g, b):
                act.wait_ge(s["kq_ready"], g + 1)
                if past(g, 1):
                    act.wait_ge(s["rooted"], g)
                for t in range(TPC):
                    for w in range(2):
                        j = 2 * t + w
                        last = nc.scalar.activation(square[:, j, :], p_kq[b][:, t, D * w:D * w + D], ACT.Square,
                                                    accum_out=norm[:, 0, j:j + 1])
                last.then_inc(s["squared"], 1)
                act.wait_ge(s["squared"], g + 1)
                if past(g, 1):
                    act.wait_ge(s["clamped"], g)
                nc.scalar.activation(norm[:, 1, :], norm[:, 0, :], ACT.Sqrt).then_inc(s["rooted"], 1)

            def slot(i, b):
                if has(i, 1):
                    lengths(i - 1, 1 - b)
                if has(i, 0):
                    act.wait_ge(s["ft_ready"], i + 1)
                    if past(i, 2):
                        act.wait_ge(s["kq_ready"], i - 1)
                    nc.scalar.copy(f_t[b][:], p_ft[:]).then_inc(s["ft_copied"], 1)
                    nc.scalar.copy(k.row_hi[:, ds(TPC * i, TPC), 0:D - 1], f[b][:, :, 0:D - 1]).then_inc(s["rows_hi"], 1)
                if has(i, 2):
                    act.wait_ge(s["t_ready"], i - 1)
                    nc.scalar.copy(k.mov_hi[:, ds(CHUNK * (i - 2), CHUNK)], p_t[:, 0, :])
                    nc.scalar.copy(k.sta_hi[:, ds(CHUNK * (i - 2), CHUNK)], p_t[:, 1, :]).then_inc(s["hi_ready"], 1)

            slots(act, 2, slot)

        @block.tensor
        def _(pe):
            def keys_queries(g, b):
                pe.wait_ge(s["f_ready"], g + 1)
                if past(g, 1):
                    pe.wait_ge(s["ft_copied"], g)
                for t in range(TPC):
                    last = nc.tensor.transpose(p_ft[:, P * t:P * t + P], f[b][:, t, :], k.ident[:])
                last.then_inc(s["ft_ready"], 1)
                pe.wait_ge(s["ft_copied"], g + 1)
                if past(g, 2):
                    pe.wait_ge(s["unit_ready"], g - 1)
                for t in range(TPC):
                    last = nc.tensor.matmul(p_kq[b][:, t, :], f_t[b][:, P * t:P * t + P], k.wkq_t[:], start=True, stop=True)
                last.then_inc(s["kq_ready"], 1)

            def turn(g):
                pe.wait_ge(s["unit_ready"], g + 1)
                if past(g, 1):
                    pe.wait_ge(s["lo_ready"], g)
                for t in range(TPC):
                    for w in range(2):
                        last = nc.tensor.transpose(p_t[:, w, P * t:P * t + P], unit[:, 2 * t + w, :], k.ident[:])
                last.then_inc(s["t_ready"], 1)

            def slot(i, b):
                if has(i, 0):
                    keys_queries(i, b)
                if has(i, 1):
                    turn(i - 1)

            slots(pe, 1, slot)


def attention(k, tag):
    nc = k.nc
    is_a = tag == "a_"
    RING = 4
    ADJ = 4
    LAG = 3
    POOL_STEP = 3
    QUADS = STEPS // 4
    LEAVE, TO_ROWS, FINISH = 3, 5, 6
    adj_dram = k.io["adj_t"]
    with ExitStack() as ctx:
        adj = [k.sb(f"{tag}adj{i}", [P, 2, 2 * CHUNK], I32, ctx) for i in range(ADJ)]
        prob = [k.sb(f"{tag}prob{i}", [P, 2 * CHUNK], F32, ctx) for i in range(RING)]
        hi = [k.sb(f"{tag}hi{i}", [P, 2 * CHUNK], F16, ctx) for i in range(RING)]
        lo = [k.sb(f"{tag}lo{i}", [P, 2 * CHUNK], F16, ctx) for i in range(RING)]
        gathered = k.sb(tag + "gathered", [P, CHUNK], F32, ctx)
        small = k.sb(tag + "small", [P, 6, TPC], F32, ctx)
        rows = k.sb(tag + "rows", [P, 4, TPC, D], F32, ctx)
        p_s = [k.ps(f"{tag}p_s{i}", [P, 2 * CHUNK], ctx) for i in range(2)]
        p_o = [k.ps(f"{tag}p_o{i}", [P, CHUNK], ctx) for i in range(2)]
        p_r = k.ps(tag + "p_r", [P, 2, 512], ctx)
        names = ("s_ready", "exp_ready", "masked", "hi_ready", "lo_ready", "lo_pool_ready", "o_ready", "gathered_ready",
                 "r_ready", "post", "row_part", "elu_exp", "x_done")
        s = {n: k.sem(tag + n, ctx) for n in names}
        adj_in = [k.sem(f"{tag}adj_in{i}", ctx) for i in range(ADJ)]
        x_stats = row_stats(k, tag, ctx)
        block = ctx.enter_context(nc.Block())

        def exists(f):
            return not isinstance(f, int) or f >= 0

        def wait_split(eng, f, st):
            if st == POOL_STEP:
                eng.wait_ge(s["lo_pool_ready"], f + 1)
            else:
                eng.wait_ge(s["lo_ready"], 3 * f + st + 1)

        def wait_used(eng, f, st):
            if exists(f - 1):
                eng.wait_ge(s["o_ready"], 4 * f + st - RING + 1)

        r_row = [p_r[:, t // 2, 129 * (t % 2):129 * (t % 2) + D] for t in range(TPC)]
        den = p_r[:, :, 0:258].rearrange("p b (t e) -> p b t e", e=129)[:, :, :, D]

        @block.sync
        def _(sp):
            def chunk(c, first):
                for q in range(CHUNKS):
                    m = CHUNKS * c + q
                    if not (first and q < ADJ):
                        sp.wait_ge(s["masked"], 2 * (m - ADJ) + 2)
                    sp.dma_start(adj[q % ADJ][:], adj_dram[ds(m, 1)]).then_inc(adj_in[q % ADJ], 16)

            peeled(sp, CHUNKS, chunk)

        @block.tensor
        def _(pe):
            def scores(c, q, st):
                f = QUADS * c + q
                if exists(4 * f + st - 2):
                    pe.wait_ge(s["exp_ready"], 4 * f + st - 1)
                for j in range(2):
                    key = ds(P * (2 * (4 * q + st) + j), P)
                    out = p_s[st % 2][:, CHUNK * j:CHUNK * j + CHUNK]
                    q_hi, q_lo = (m[:, ds(CHUNK * c, CHUNK)] for m in (k.mov_hi, k.mov_lo))
                    nc.tensor.matmul(out, k.sta_hi[:, key], q_hi, start=True, stop=False)
                    nc.tensor.matmul(out, k.sta_hi[:, key], q_lo, start=False, stop=False)
                    last = nc.tensor.matmul(out, k.sta_lo[:, key], q_hi, start=False, stop=True)
                last.then_inc(s["s_ready"], 1)

            def values(c, par, q, st):
                wait_split(pe, QUADS * c + q, st)
                for j in range(2):
                    begin = isinstance(q, int) and q == 0 and st == 0 and j == 0
                    end = isinstance(q, int) and q == QUADS - 1 and st == 3 and j == 1
                    part = slice(CHUNK * j, CHUNK * j + CHUNK)
                    v_hi, v_lo = (m[:, ds(2 * (4 * q + st) + j, 1), :] for m in (k.row_hi, k.row_lo))
                    nc.tensor.matmul(p_o[par][:], v_hi, hi[st][:, part], start=begin, stop=False, skip_group_check=True)
                    nc.tensor.matmul(p_o[par][:], v_hi, lo[st][:, part], start=False, stop=False, skip_group_check=True)
                    last = nc.tensor.matmul(p_o[par][:], v_lo, hi[st][:, part], start=False, stop=end,
                                            skip_group_check=True)
                last.then_inc(s["o_ready"], 1)

            def to_rows(c):
                pe.wait_ge(s["gathered_ready"], c + 1)
                if exists(c - 1):
                    pe.wait_ge(s["post"], c)
                for t in range(TPC):
                    last = nc.tensor.matmul(p_r[:, t // 2, 129 * (t % 2):129 * (t % 2) + 129],
                                            gathered[:, P * t:P * t + P], (k.unaug if is_a else k.wv_aug)[:],
                                            start=True, stop=True)
                last.then_inc(s["r_ready"], 1)

            def steps(c, par, q):
                for st in range(4):
                    scores(c, q, st)
                    if st >= LAG:
                        if isinstance(q, int) and q == 0 and exists(c - 2):
                            pe.wait_ge(s["gathered_ready"], c - 1)
                        values(c, par, q, st - LAG)
                    elif not (isinstance(q, int) and q == 0):
                        values(c, par, q - 1, st - LAG + 4)
                    elif exists(c - 1):
                        values(c - 1, 1 - par, QUADS - 1, st - LAG + 4)
                    if isinstance(q, int) and 4 * q + st == TO_ROWS and exists(c - 1):
                        to_rows(c - 1)

            def chunk(c, par):
                steps(c, par, 0)
                steps(c, par, 1)
                with pe.Fori(2, QUADS) as q:
                    steps(c, par, q)

            chunk(0, 0)
            chunk(1, 1)
            with pe.Fori(1, CHUNKS // 2) as cc:
                chunk(2 * cc, 0)
                chunk(2 * cc + 1, 1)
            for st in range(4 - LAG, 4):
                values(CHUNKS - 1, 1, QUADS - 1, st)
            to_rows(CHUNKS - 1)

        @block.scalar
        def _(act):
            def exps(f, st):
                act.wait_ge(s["s_ready"], 4 * f + st + 1)
                if exists(f - 1):
                    wait_split(act, f - 1, st)
                nc.scalar.activation(prob[st][:], p_s[st % 2][:], ACT.Exp,
                                     bias=0.0 if is_a else k.shift[:, 0:1],
                                     scale=1.0 / UNIT ** 2 if is_a else k.g_unit[:, 0:1]).then_inc(s["exp_ready"], 1)

            def highs(f, st):
                act.wait_ge(s["masked"], 4 * f + st + 1)
                wait_used(act, f, st)
                nc.scalar.copy(hi[st][:], prob[st][:]).then_inc(s["hi_ready"], 1)

            def elu(c):
                act.wait_ge(s["row_part"], c + 1)
                nc.scalar.activation(rows[:, 2], rows[:, 1], ACT.Exp).then_inc(s["elu_exp"], 1)

            def chunk(c, first):
                for q in range(QUADS):
                    f = QUADS * c + q
                    for st in range(4):
                        exps(f, st)
                        if st > 0:
                            highs(f, st - 1)
                        elif exists(f - 1):
                            highs(f - 1, 3)
                        if not is_a and not first and 4 * q + st == FINISH + 5:
                            elu(c - 1)

            peeled(act, CHUNKS, chunk)
            highs(QUADS * CHUNKS - 1, 3)
            if not is_a:
                elu(CHUNKS - 1)

        @block.gpsimd
        def _(pool):
            def lows(f, first):
                pool.wait_ge(s["hi_ready"], 4 * f + POOL_STEP + 1)
                wait_used(pool, f, POOL_STEP)
                nc.gpsimd.tensor_tensor(lo[POOL_STEP][:], prob[POOL_STEP][:], hi[POOL_STEP][:],
                                        ALU.subtract).then_inc(s["lo_pool_ready"], 1)

            def chunk(c, first):
                for q in range(QUADS):
                    lows(QUADS * c + q, first)
                if not first:
                    invert_rows(k, x_stats, pool, c - 1)

            peeled(pool, CHUNKS, chunk)
            invert_rows(k, x_stats, pool, CHUNKS - 1)

        @block.vector
        def _(dve):
            def mask(c, q, st):
                f = QUADS * c + q
                dve.wait_ge(s["exp_ready"], 4 * f + st + 1)
                transfer = 2 * q + st // 2
                dve.wait_ge(adj_in[transfer % ADJ], 16 * (2 * c + transfer // ADJ + 1))
                nc.vector.scalar_tensor_tensor(prob[st][:], adj[transfer % ADJ][:, st % 2, :], 0.0, prob[st][:],
                                               ALU.is_gt, ALU.mult).then_inc(s["masked"], 1)

            def lows(f, st):
                if st == POOL_STEP:
                    return
                dve.wait_ge(s["hi_ready"], 4 * f + st + 1)
                wait_used(dve, f, st)
                nc.vector.tensor_tensor(lo[st][:], prob[st][:], hi[st][:], ALU.subtract).then_inc(s["lo_ready"], 1)

            def leave(c, par):
                dve.wait_ge(s["o_ready"], STEPS * (c + 1))
                if exists(c - 1):
                    dve.wait_ge(s["r_ready"], c)
                nc.vector.tensor_copy(gathered[:], p_o[par][:]).then_inc(s["gathered_ready"], 1)

            def tile(c, t):
                return k.x[:, ds(TPC * c + t, 1), :]

            def finish_a(c, part):
                empty = k.empty[:, ds(TPC * c, TPC)]
                half_den, inv_den, w, w_rstd, x_factor, offset = (small[:, i, :] for i in range(6))
                if part == 0:
                    dve.wait_ge(s["r_ready"], c + 1)
                    nc.vector.tensor_scalar(empty, den, 0.0, None, ALU.is_equal).then_inc(s["row_part"], 1)
                    nc.vector.tensor_scalar(half_den, den, 1e-30, 2.0, ALU.max, ALU.mult).then_inc(s["row_part"], 1)
                elif part == 1:
                    dve.wait_ge(s["row_part"], 7 * c + 2)
                    nc.vector.tensor_scalar(w, empty, 0.5, 0.5, ALU.mult, ALU.add).then_inc(s["row_part"], 1)
                    nc.vector.reciprocal(inv_den, half_den).then_inc(s["row_part"], 1)
                elif part == 2:
                    dve.wait_ge(s["row_part"], 7 * c + 4)
                    nc.vector.tensor_tensor(w_rstd, w, k.rstd[:, ds(TPC * c, TPC)], ALU.mult).then_inc(s["row_part"], 1)
                elif part == 3:
                    dve.wait_ge(s["row_part"], 7 * c + 5)
                    nc.vector.tensor_scalar(x_factor, w_rstd, 1.0, None, ALU.add).then_inc(s["row_part"], 1)
                    nc.vector.scalar_tensor_tensor(offset.rearrange("p (a b) -> p a b", b=2),
                                                   k.x_stats[:, ds(TPC // 2 * c, TPC // 2), 1:5:3], -1.0,
                                                   w_rstd.rearrange("p (a b) -> p a b", b=2),
                                                   ALU.mult, ALU.mult).then_inc(s["row_part"], 1)
                elif part == 4:
                    dve.wait_ge(s["row_part"], 7 * c + 7)
                    for t in range(TPC):
                        last = nc.vector.tensor_scalar(rows[:, 0, t, :], tile(c, t), x_factor[:, t:t + 1],
                                                       offset[:, t:t + 1], ALU.mult, ALU.add)
                    last.then_inc(s["x_done"], 1)
                elif part == 5:
                    dve.wait_ge(s["x_done"], c + 1)
                    for t in range(TPC):
                        last = nc.vector.scalar_tensor_tensor(tile(c, t), r_row[t], inv_den[:, t:t + 1],
                                                              rows[:, 0, t, :], ALU.mult, ALU.add)
                    last.then_inc(s["post"], 1)
                elif part == 6:
                    dve.wait_ge(s["post"], c + 1)
                    measure_rows(k, x_stats, c)

            def finish_b(c, part):
                some_den, inv_den = small[:, 0, :], small[:, 1, :]
                att, negative, expo, total = (rows[:, i] for i in range(4))
                x = k.x[:, ds(TPC * c, TPC), :]
                if part == 0:
                    dve.wait_ge(s["r_ready"], c + 1)
                    nc.vector.tensor_scalar(some_den, den, 1e-30, None, ALU.max).then_inc(s["x_done"], 1)
                elif part == 1:
                    dve.wait_ge(s["x_done"], 5 * c + 1)
                    nc.vector.reciprocal(inv_den, some_den).then_inc(s["x_done"], 1)
                elif part == 2:
                    dve.wait_ge(s["x_done"], 5 * c + 2)
                    for t in range(TPC):
                        last = nc.vector.tensor_scalar(total[:, t, :], r_row[t], inv_den[:, t:t + 1], None, ALU.mult)
                    last.then_inc(s["post"], 1)
                elif part == 3:
                    dve.wait_ge(s["post"], c + 1)
                    for t in range(TPC):
                        last = nc.vector.scalar_tensor_tensor(att[:, t, :], k.v_mean[:], k.empty[:, ds(TPC * c + t, 1)],
                                                              total[:, t, :], ALU.mult, ALU.add)
                    last.then_inc(s["x_done"], 1)
                elif part == 4:
                    dve.wait_ge(s["x_done"], 5 * c + 3)
                    nc.vector.tensor_scalar(negative, att, 0.0, None, ALU.min).then_inc(s["row_part"], 1)
                elif part == 7:
                    dve.wait_ge(s["elu_exp"], c + 1)
                    nc.vector.scalar_tensor_tensor(total, att, 0.0, expo, ALU.max, ALU.add).then_inc(s["x_done"], 1)
                elif part == 8:
                    dve.wait_ge(s["x_done"], 5 * c + 4)
                    nc.vector.scalar_tensor_tensor(x, total, -1.0, x, ALU.add, ALU.add).then_inc(s["x_done"], 1)
                elif part == 9:
                    dve.wait_ge(s["x_done"], 5 * c + 5)
                    measure_rows(k, x_stats, c)

            finish = finish_a if is_a else finish_b

            def chunk(c, par):
                for q in range(QUADS):
                    for st in range(4):
                        mask(c, q, st)
                        if st > 0:
                            lows(QUADS * c + q, st - 1)
                        elif exists(QUADS * c + q - 1):
                            lows(QUADS * c + q - 1, 3)
                        if exists(c - 1):
                            if 4 * q + st == LEAVE:
                                leave(c - 1, 1 - par)
                            if 4 * q + st >= FINISH:
                                finish(c - 1, 4 * q + st - FINISH)

            chunk(0, 0)
            chunk(1, 1)
            with dve.Fori(1, CHUNKS // 2) as cc:
                chunk(2 * cc, 0)
                chunk(2 * cc + 1, 1)
            lows(QUADS * CHUNKS - 1, 3)
            leave(CHUNKS - 1, 1)
            for part in range(STEPS - FINISH):
                finish(CHUNKS - 1, part)


def prepare_weights(k):
    nc = k.nc
    with ExitStack() as ctx:
        scaled = k.sb("w_scaled", [P, D], F32, ctx)
        row = k.sb("w_row", [1, 4, D], F32, ctx)
        m_qk = k.sb("w_m_qk", [P, D], F32, ctx)
        p_a = k.ps("w_p_a", [P, D], ctx)
        p_b = k.ps("w_p_b", [P, D], ctx)
        p_c = k.ps("w_p_c", [P, D], ctx)
        p_d = k.ps("w_p_d", [P, D], ctx)
        p_e = k.ps("w_p_e", [P, D], ctx)
        p_f = k.ps("w_p_f", [P, D], ctx)
        vec = k.sem("w_vec", ctx)
        first_products = k.sem("w_first", ctx)
        second_products = k.sem("w_second", ctx)
        block = ctx.enter_context(nc.Block())

        @block.vector
        def _(dve):
            nc.vector.tensor_scalar(scaled[:], k.w_ffn_t[:], k.lnw[:, 0:1], None, ALU.mult).then_inc(vec, 1)
            nc.vector.memset(k.bias_ffn[:], 0.0).then_inc(vec, 1)
            dve.wait_ge(first_products, 4)
            nc.vector.tensor_scalar(k.w_ffn[:], p_a[:], D ** 0.5, None, ALU.mult)
            nc.vector.tensor_tensor(row[:, 0, :], p_b[0:1, :], k.b_ffn[0:1, :], ALU.add).then_inc(vec, 1)
            nc.vector.tensor_scalar(m_qk[:], p_c[:], D ** -0.5, None, ALU.mult).then_inc(vec, 1)
            nc.vector.tensor_scalar(row[:, 3, :], p_d[0:1, :], D ** -0.5, None, ALU.mult).then_inc(vec, 1)
            dve.wait_ge(vec, 3)
            for t in range(TPC):
                last = nc.vector.tensor_copy(k.bias_ffn[0:1, t, :], row[:, 0, :])
            last.then_inc(vec, 1)
            dve.wait_ge(vec, 6)
            nc.vector.tensor_tensor(row[:, 1, :], row[:, 0, :], k.bias_ffn[0:1, 0, :], ALU.subtract).then_inc(vec, 1)
            dve.wait_ge(vec, 7)
            for t in range(TPC):
                last = nc.vector.tensor_copy(k.bias_ffn[32:33, t, :], row[:, 1, :])
            last.then_inc(vec, 1)
            nc.vector.tensor_copy(k.bias_mid[:], row[:, 1, :]).then_inc(vec, 1)
            dve.wait_ge(vec, 9)
            nc.vector.tensor_tensor(row[:, 2, :], row[:, 1, :], k.bias_mid[:], ALU.subtract).then_inc(vec, 1)
            dve.wait_ge(vec, 10)
            for t in range(TPC):
                nc.vector.tensor_copy(k.bias_ffn[64:65, t, :], row[:, 2, :])
            dve.wait_ge(second_products, 2)
            nc.vector.tensor_copy(k.m_aug[:, 0:D], p_e[:]).then_inc(vec, 1)
            nc.vector.tensor_copy(k.wv_aug[:, 0:D], p_f[:])
            nc.vector.tensor_copy(k.wv_aug[:, D:D + 1], k.unaug[:, D:D + 1])
            dve.wait_ge(vec, 11)
            nc.vector.tensor_scalar(k.m_aug[:, D:2 * D], k.m_aug[:, 0:D], k.m_aug[:, D - 1:D], None, ALU.subtract)

        @block.tensor
        def _(pe):
            pe.wait_ge(vec, 1)
            nc.tensor.matmul(p_a[:], k.center[:], scaled[:], start=True, stop=True).then_inc(first_products, 1)
            nc.tensor.matmul(p_b[0:1, :], k.lnb[:], k.w_ffn_t[:], start=True, stop=True).then_inc(first_products, 1)
            nc.tensor.matmul(p_c[:], k.wq1[:], k.wk1[:], start=True, stop=True).then_inc(first_products, 1)
            nc.tensor.matmul(p_d[0:1, :], k.bq1[:], k.wk1[:], start=True, stop=True).then_inc(first_products, 1)
            pe.wait_ge(vec, 5)
            nc.tensor.matmul(p_e[:], k.unaug_t[:], m_qk[:], start=True, stop=False)
            nc.tensor.matmul(p_e[:], k.last_row[0:1, :], row[:, 3, :], start=False, stop=True).then_inc(second_products, 1)
            nc.tensor.matmul(p_f[:], k.unaug_t[:], k.wv1_t[:], start=True, stop=False)
            nc.tensor.matmul(p_f[:], k.last_row[0:1, :], k.bv1[0:1, :], start=False, stop=True).then_inc(second_products, 1)


def recurrence(k):
    nc = k.nc
    G = T // TPC
    ITEMS = G * STEPS_KERNEL
    YB, TB = 4, 2
    DVE_TILES, POOL_TILES, ACT_TILES = (2, 3), (slice(2, 3), slice(3, 4)), slice(3, 4)
    UNIT_LAG, LEAVE_LAG = 4, 6
    with ExitStack() as ctx:
        def ring(name, n):
            return [k.sb(f"r_{name}{g}", [P, TPC * D], F32, ctx) for g in range(n)]

        R = 4
        tanh, h, z_t, z, z_unit = ring("tanh", R), ring("h", R), ring("z_t", R), ring("z", G), ring("z_unit", G)
        parts = [k.sb(f"r_parts{g}", [P, TPC // 2, 6], F32, ctx) for g in range(G)]
        stat = [k.sb(f"r_stat{g}", [P, 2, TPC], F32, ctx) for g in range(G)]
        p_y = [k.ps(f"r_p_y{i}", [P, TPC * D], ctx) for i in range(YB)]
        p_t = [k.ps(f"r_p_t{i}", [P, TPC * P], ctx) for i in range(TB)]
        names = ("start_ready", "y_ready", "tanh_ready", "h_ready", "z_ready", "measured", "padded", "rstd_ready",
                 "unit_ready", "unit_act_ready", "unit_pool_ready", "t_ready", "zt_ready")
        s = {n: k.sem("r_" + n, ctx) for n in names}
        x_stats = row_stats(k, "rx_", ctx)
        block = ctx.enter_context(nc.Block())

        def tiles(a):
            return a[:].rearrange("p (t d) -> p t d", t=TPC)

        @block.tensor
        def _(pe):
            def start(m):
                pe.wait_ge(s["start_ready"], m + 1)
                if m >= YB:
                    pe.wait_ge(s["h_ready"], m - YB + 1)
                nc.tensor.matmul(p_y[m % YB][:], k.ident[:], z_unit[m][:], start=True, stop=True).then_inc(s["y_ready"], 1)

            def turn(i, g, first):
                n = G * i + g
                pe.wait_ge(s["unit_ready"], n + 1)
                pe.wait_ge(s["unit_pool_ready"], n + 1)
                if g % 2 == 0:
                    pe.wait_ge(s["unit_act_ready"], G // 2 * i + g // 2 + 1)
                if not (first and g < TB):
                    pe.wait_ge(s["zt_ready"], n - TB + 1)
                for t in range(TPC):
                    last = nc.tensor.transpose(p_t[g % TB][:, P * t:P * t + P], z_unit[g][:, D * t:D * t + D], k.ident[:])
                last.then_inc(s["t_ready"], 1)

            def linear(n, g):
                pe.wait_ge(s["zt_ready"], n + 1)
                pe.wait_ge(s["h_ready"], n + G - YB + 1)
                out = p_y[g % YB]
                nc.tensor.matmul(out[:], k.ones_bf[:], k.bias_ffn[:].rearrange("p t d -> p (t d)"), start=True,
                                 stop=False, skip_group_check=True)
                for t in range(TPC):
                    last = nc.tensor.matmul(out[:, D * t:D * t + D], z_t[g % R][:, P * t:P * t + P], k.w_ffn[:], start=False,
                                            stop=(t == TPC - 1), skip_group_check=True)
                last.then_inc(s["y_ready"], 1)

            for m in range(G):
                start(m)

            def step(i, first):
                for g in range(G):
                    turn(i, g, first)
                    if not (first and g == 0):
                        linear(G * i + g - 1, (g - 1) % G)

            peeled(pe, STEPS_KERNEL, step)
            linear(ITEMS - 1, G - 1)

        @block.scalar
        def _(act):
            def tanhs(n, g):
                act.wait_ge(s["y_ready"], n + 1)
                nc.scalar.activation(tanh[g % R][:], p_y[g % YB][:], ACT.Tanh).then_inc(s["tanh_ready"], 1)

            def silus(n, g):
                act.wait_ge(s["h_ready"], n + 1)
                nc.scalar.activation(z[g][:], h[g % R][:], ACT.Silu).then_inc(s["z_ready"], 1)

            def unit(n, g):
                if g % 2:
                    return
                act.wait_ge(s["rstd_ready"], n + 1)
                for t in range(TPC)[ACT_TILES]:
                    last = nc.scalar.activation(z_unit[g][:, D * t:D * t + D], z[g][:, D * t:D * t + D], ACT.Copy,
                                                scale=stat[g][:, 1, t:t + 1])
                last.then_inc(s["unit_act_ready"], 1)

            def leave(n, g):
                act.wait_ge(s["t_ready"], n + 1)
                nc.scalar.copy(z_t[g % R][:], p_t[g % TB][:]).then_inc(s["zt_ready"], 1)

            stages = ((0, tanhs), (1, silus), (UNIT_LAG, unit), (LEAVE_LAG, leave))

            def step(i, first):
                for g in range(G):
                    for lag, stage in stages:
                        if not (first and g < lag):
                            stage(G * i + g - lag, (g - lag) % G)

            peeled(act, STEPS_KERNEL, step)
            for n in range(ITEMS, ITEMS + LEAVE_LAG):
                for lag, stage in stages:
                    if n - lag < ITEMS:
                        stage(n - lag, (n - lag) % G)

        @block.vector
        def _(dve):
            def start(g):
                for t in range(TPC):
                    last = normalised(k, z_unit[g][:, D * t:D * t + D], g, t)
                last.then_inc(s["start_ready"], 1)

            def add_tanh(n, g):
                dve.wait_ge(s["tanh_ready"], n + 1)
                nc.vector.scalar_tensor_tensor(h[g % R][:], tanh[g % R][:], 0.01, p_y[g % YB][:], ALU.mult, ALU.add)\
                    .then_inc(s["h_ready"], 1)

            def measure(n, g):
                dve.wait_ge(s["z_ready"], n + 1)
                for i in range(TPC // 2):
                    last = nc.vector.bn_stats(parts[g][:, i, :], tiles(z[g])[:, 2 * i:2 * i + 2, :].rearrange("p t d -> p d t"))
                last.then_inc(s["measured"], 1)

            def unit(n, g):
                dve.wait_ge(s["rstd_ready"], n + 1)
                own = DVE_TILES[g % 2]
                nc.vector.tensor_tensor(tiles(z_unit[g])[:, 0:own, :], tiles(z[g])[:, 0:own, :],
                                        stat[g][:, 1, 0:own].unsqueeze(2).broadcast_to([P, own, D]), ALU.mult).then_inc(s["unit_ready"], 1)

            stages = ((0, add_tanh), (1, measure), (UNIT_LAG, unit))
            for g in range(2):
                start(g)

            def step(i, first):
                for g in range(G):
                    if first and g + 2 < G:
                        start(g + 2)
                    for lag, stage in stages:
                        if not (first and g < lag):
                            stage(G * i + g - lag, (g - lag) % G)

            peeled(dve, STEPS_KERNEL, step)
            for n in range(ITEMS, ITEMS + UNIT_LAG):
                for lag, stage in stages:
                    if n - lag < ITEMS:
                        stage(n - lag, (n - lag) % G)
            for g in range(G):
                dve.wait_ge(s["y_ready"], ITEMS + g + 1)
                xr = k.x[:, TPC * g:TPC * g + TPC, :]
                nc.vector.tensor_tensor(xr, xr, tiles(p_y[g % YB]), ALU.add).then_inc(s["h_ready"], 1)
                dve.wait_ge(s["h_ready"], ITEMS + g + 1)
                measure_rows(k, x_stats, g)

        @block.gpsimd
        def _(pool):
            def rstds(n, g):
                pool.wait_ge(s["measured"], n + 1)
                nc.gpsimd.tensor_tensor(stat[g][:, 0, :].rearrange("p (a b) -> p a b", b=2), parts[g][:, :, 2:6:3],
                                        k.eps_sum[:].rearrange("p (a b) -> p a b", b=2), ALU.add).then_inc(s["padded"], 1)
                pool.wait_ge(s["padded"], n + 1)
                nc.gpsimd.tensor_tensor(stat[g][:, 1, :], stat[g][:, 0, :], k.minus_half[:], ALU.pow)\
                    .then_inc(s["rstd_ready"], 1)

            def unit(n, g):
                pool.wait_ge(s["rstd_ready"], n + 1)
                own = POOL_TILES[g % 2]
                nc.gpsimd.tensor_tensor(tiles(z_unit[g])[:, own, :], tiles(z[g])[:, own, :],
                                        stat[g][:, 1, own].unsqueeze(2).broadcast_to([P, 1, D]),
                                        ALU.mult).then_inc(s["unit_pool_ready"], 1)

            def step(i, first):
                for g in range(G):
                    rstds(G * i + g, g)
                    unit(G * i + g, g)

            peeled(pool, STEPS_KERNEL, step)
            peeled(pool, T // TPC, lambda g, first: invert_rows(k, x_stats, pool, g))


def normalise_b(k):
    nc = k.nc
    with ExitStack() as ctx:
        f = [k.sb(f"n_f{i}", [P, TPC, D], F32, ctx) for i in range(2)]
        f_t = [k.sb(f"n_f_t{i}", [P, TPC * P], F32, ctx) for i in range(2)]
        square = k.sb("n_square", [P, TPC, D], F32, ctx)
        length = k.sb("n_length", [P, T], F32, ctx)
        f_sum = k.sb("n_f_sum", [P, 1], F32, ctx)
        f_sums = k.sb("n_f_sums", [P, P], F32, ctx)
        p_ft = k.ps("n_p_ft", [P, TPC * P], ctx)
        p_g = [k.ps(f"n_p_g{i}", [P, 2, TPC, D], ctx) for i in range(2)]
        p_sum = k.ps("n_p_sum", [P, 1], ctx)
        p_mean = k.ps("n_p_mean", [P, D + 1], ctx)
        names = ("preset", "f_ready", "rows_hi", "rows_lo", "ft_ready", "ft_copied", "hi_ready", "lo_ready", "g_ready",
                 "squared", "g_kept", "sum_ready", "sum_copied", "sums_ready", "mean_ready")
        s = {n: k.sem("n_" + n, ctx) for n in names}
        block = ctx.enter_context(nc.Block())

        @block.vector
        def _(dve):
            for i in range(2):
                nc.vector.memset(f[i][:, :, D - 1:D], 1.0).then_inc(s["preset"], 1)

            def slot(i, b):
                if has(i, 0):
                    if past(i, 2):
                        dve.wait_ge(s["ft_ready"], i - 1)
                        dve.wait_ge(s["rows_hi"], i - 1)
                        dve.wait_ge(s["rows_lo"], i - 1)
                    for t in range(TPC):
                        last = normalised(k, f[b][:, t, 0:D - 1], i, t, D - 1)
                    last.then_inc(s["f_ready"], 1)
                if has(i, 1):
                    dve.wait_ge(s["hi_ready"], i)
                    nc.vector.tensor_tensor(k.sta_lo[:, ds(CHUNK * (i - 1), CHUNK)], f_t[1 - b][:],
                                            k.sta_hi[:, ds(CHUNK * (i - 1), CHUNK)], ALU.subtract).then_inc(s["lo_ready"], 1)
                    dve.wait_ge(s["g_ready"], i)
                    nc.vector.tensor_copy(k.g_rows[:, ds(TPC * (i - 1), TPC), :], p_g[1 - b][:, 1]).then_inc(s["g_kept"], 1)

            slots(dve, 1, slot)
            dve.wait_ge(s["squared"], CHUNKS)
            nc.vector.tensor_reduce(k.g_length[:, 0:1], length[:], AX.X, ALU.max)
            dve.wait_ge(s["sum_ready"], 1)
            nc.vector.tensor_copy(f_sum[:], p_sum[:]).then_inc(s["sum_copied"], 1)
            dve.wait_ge(s["sum_copied"], 1)
            nc.vector.tensor_scalar(f_sums[:], k.ones[:], f_sum[:, 0:1], None, ALU.mult).then_inc(s["sums_ready"], 1)
            dve.wait_ge(s["mean_ready"], 1)
            nc.vector.tensor_scalar(k.v_mean[:], p_mean[:, 0:D], 1.0 / N, None, ALU.mult)

        @block.gpsimd
        def _(pool):
            def slot(i, b):
                pool.wait_ge(s["rows_hi"], i + 1)
                nc.gpsimd.tensor_tensor(k.row_lo[:, ds(TPC * i, TPC), 0:D - 1], f[b][:, :, 0:D - 1],
                                        k.row_hi[:, ds(TPC * i, TPC), 0:D - 1], ALU.subtract).then_inc(s["rows_lo"], 1)

            slots(pool, 0, slot)

        @block.scalar
        def _(act):
            def slot(i, b):
                if has(i, 0):
                    act.wait_ge(s["ft_ready"], i + 1)
                    if past(i, 2):
                        act.wait_ge(s["g_ready"], i - 1)
                        act.wait_ge(s["lo_ready"], i - 1)
                    nc.scalar.copy(f_t[b][:], p_ft[:]).then_inc(s["ft_copied"], 1)
                    nc.scalar.copy(k.sta_hi[:, ds(CHUNK * i, CHUNK)], p_ft[:]).then_inc(s["hi_ready"], 1)
                    nc.scalar.copy(k.row_hi[:, ds(TPC * i, TPC), 0:D - 1], f[b][:, :, 0:D - 1]).then_inc(s["rows_hi"], 1)
                if has(i, 1):
                    act.wait_ge(s["g_ready"], i)
                    if past(i, 2):
                        act.wait_ge(s["squared"], i - 1)
                    for t in range(TPC):
                        last = nc.scalar.activation(square[:, t, :], p_g[1 - b][:, 0, t, :], ACT.Square,
                                                    accum_out=length[:, ds(TPC * (i - 1) + t, 1)])
                    last.then_inc(s["squared"], 1)

            slots(act, 1, slot)

        @block.tensor
        def _(pe):
            pe.wait_ge(s["preset"], 2)

            def slot(i, b):
                if has(i, 0):
                    pe.wait_ge(s["f_ready"], i + 1)
                    if past(i, 1):
                        pe.wait_ge(s["hi_ready"], i)
                    for t in range(TPC):
                        last = nc.tensor.transpose(p_ft[:, P * t:P * t + P], f[b][:, t, :], k.ident[:])
                    last.then_inc(s["ft_ready"], 1)
                if has(i, 1):
                    pe.wait_ge(s["rows_lo"], i)
                    for t in range(TPC):
                        for part in (k.row_hi, k.row_lo):
                            begin = isinstance(i, int) and i == 1 and t == 0 and part is k.row_hi
                            nc.tensor.matmul(p_sum[:], part[:, ds(TPC * (i - 1) + t, 1), :], k.ones_half[:, 0:1],
                                             start=begin, stop=False, skip_group_check=True)
                if has(i, 0):
                    pe.wait_ge(s["ft_copied"], i + 1)
                    if past(i, 2):
                        pe.wait_ge(s["g_kept"], i - 1)
                        pe.wait_ge(s["squared"], i - 1)
                    for t in range(TPC):
                        for w in range(2):
                            last = nc.tensor.matmul(p_g[b][:, w, t, :], f_t[b][:, P * t:P * t + P],
                                                    k.m_aug[:, D * w:D * w + D], start=True, stop=True)
                    last.then_inc(s["g_ready"], 1)

            slots(pe, 1, slot)
            nc.tensor.matmul(p_sum[:], k.zero_half[:], k.ones_half[:, 0:1], start=False, stop=True,
                             skip_group_check=True).then_inc(s["sum_ready"], 1)
            pe.wait_ge(s["sums_ready"], 1)
            nc.tensor.matmul(p_mean[:], f_sums[:], k.wv_aug[:], start=True, stop=True).then_inc(s["mean_ready"], 1)


def scale_queries(k):
    nc = k.nc
    with ExitStack() as ctx:
        top = k.sb("q_top", [P, 2], F32, ctx)
        unit = [k.sb(f"q_unit{i}", [P, TPC, D], F32, ctx) for i in range(2)]
        p_t = [k.ps(f"q_p_t{i}", [P, TPC * P], ctx) for i in range(2)]
        names = ("top_ready", "rooted", "clamped", "scale_ready", "unit_ready", "t_ready", "hi_ready", "lo_ready")
        s = {n: k.sem("q_" + n, ctx) for n in names}
        block = ctx.enter_context(nc.Block())

        @block.gpsimd
        def _(pool):
            nc.gpsimd.partition_all_reduce(top[:, 0:1], k.g_length[:, 0:1], P, bass.bass_isa.ReduceOp.max).then_inc(s["top_ready"], 1)

        @block.scalar
        def _(act):
            act.wait_ge(s["top_ready"], 1)
            nc.scalar.activation(top[:, 1:2], top[:, 0:1], ACT.Sqrt).then_inc(s["rooted"], 1)

            def group(gg, first):
                for par in range(2):
                    g = 2 * gg + par
                    act.wait_ge(s["t_ready"], g + 1)
                    nc.scalar.copy(k.mov_hi[:, ds(CHUNK * g, CHUNK)], p_t[par][:]).then_inc(s["hi_ready"], 1)

            peeled(act, CHUNKS // 2, group)

        @block.vector
        def _(dve):
            dve.wait_ge(s["rooted"], 1)
            nc.vector.tensor_scalar(k.g_unit[:], top[:, 1:2], 1e-15, 1.0 / 32, ALU.max, ALU.mult).then_inc(s["clamped"], 1)
            dve.wait_ge(s["clamped"], 1)
            nc.vector.reciprocal(k.g_scale[:], k.g_unit[:]).then_inc(s["scale_ready"], 1)
            nc.vector.tensor_scalar(k.wide_scores[:], top[:, 0:1], S_MAX ** 2 / D, None, ALU.is_gt)
            dve.wait_ge(s["scale_ready"], 1)

            def slot(i, b):
                if has(i, 0):
                    if past(i, 2):
                        dve.wait_ge(s["t_ready"], i - 1)
                    nc.vector.tensor_scalar(unit[b][:], k.g_rows[:, ds(TPC * i, TPC), :], k.g_scale[:, 0:1], None,
                                            ALU.mult).then_inc(s["unit_ready"], 1)
                if has(i, 1):
                    dve.wait_ge(s["hi_ready"], i)
                    nc.vector.tensor_tensor(k.mov_lo[:, ds(CHUNK * (i - 1), CHUNK)], p_t[1 - b][:],
                                            k.mov_hi[:, ds(CHUNK * (i - 1), CHUNK)], ALU.subtract).then_inc(s["lo_ready"], 1)

            slots(dve, 1, slot)

        @block.tensor
        def _(pe):
            def group(gg, first):
                for par in range(2):
                    g = 2 * gg + par
                    pe.wait_ge(s["unit_ready"], g + 1)
                    if not first:
                        pe.wait_ge(s["lo_ready"], g - 1)
                    for t in range(TPC):
                        last = nc.tensor.transpose(p_t[par][:, P * t:P * t + P], unit[par][:, t, :], k.ident[:])
                    last.then_inc(s["t_ready"], 1)

            peeled(pe, CHUNKS // 2, group)


def row_maxima(k):
    nc = k.nc
    LIFT = 384.0
    with ExitStack() as ctx:
        adj = k.sb("m_adj", [P, 2, 2 * CHUNK], I32, ctx)
        lifted = k.sb("m_lifted", [P, 2 * CHUNK], F32, ctx)
        masked = k.sb("m_masked", [P, 2 * CHUNK], F32, ctx)
        run = k.sb("m_run", [P, CHUNK], F32, ctx)
        top = k.sb("m_top", [P, 3, TPC], F32, ctx)
        lift = k.sb("m_lift", [P, 1], F32, ctx)
        unit = k.sb("m_unit", [P, TPC, D], F32, ctx)
        p_s = k.ps("m_p_s", [P, 2 * CHUNK], ctx)
        p_t = k.ps("m_p_t", [P, TPC * P], ctx)
        p_q = k.ps("m_p_q", [P, TPC * P], ctx)
        names = ("adj_in", "adj_free", "s_free", "s_ready", "lift_set", "run_step", "turned", "top_step", "unit_ready",
                 "q_turned", "q_hi", "q_lo")
        s = {n: k.sem("m_" + n, ctx) for n in names}
        block = ctx.enter_context(nc.Block())
        TRANSFERS = CHUNKS * STEPS // 2

        def wide(eng):
            return eng.value_load(k.wide_scores[0:1, 0:1], min_val=0, max_val=1) > 0

        @block.sync
        def _(sp):
            with sp.If(wide(sp)):
                with sp.Fori(0, TRANSFERS) as m:
                    sp.wait_ge(s["adj_free"], 2 * m + 1)
                    sp.dma_start(adj[:], k.io["adj_t"][ds(m, 1)]).then_inc(s["adj_in"], 16)

        @block.tensor
        def _(pe):
            with pe.If(wide(pe)):
                with pe.Fori(0, CHUNKS) as c:
                    q_hi, q_lo = (m[:, ds(CHUNK * c, CHUNK)] for m in (k.mov_hi, k.mov_lo))
                    with pe.Fori(0, STEPS) as st:
                        pe.wait_ge(s["s_free"], STEPS * c + st + 1)
                        for j in range(2):
                            key = ds(P * (2 * st + j), P)
                            out = p_s[:, CHUNK * j:CHUNK * j + CHUNK]
                            nc.tensor.matmul(out, k.sta_hi[:, key], q_hi, start=True, stop=False)
                            nc.tensor.matmul(out, k.sta_hi[:, key], q_lo, start=False, stop=False)
                            last = nc.tensor.matmul(out, k.sta_lo[:, key], q_hi, start=False, stop=True)
                        last.then_inc(s["s_ready"], 1)
                    pe.wait_ge(s["run_step"], (2 * STEPS + 1) * (c + 1))
                    for t in range(TPC):
                        last = nc.tensor.transpose(p_t[:, P * t:P * t + P], run[:, P * t:P * t + P], k.ident[:])
                    last.then_inc(s["turned"], 1)
                    pe.wait_ge(s["unit_ready"], c + 1)
                    for t in range(TPC):
                        last = nc.tensor.transpose(p_q[:, P * t:P * t + P], unit[:, t, :], k.ident[:])
                    last.then_inc(s["q_turned"], 1)

        @block.scalar
        def _(act):
            with act.If(wide(act)):
                act.wait_ge(s["lift_set"], 1)
                nc.scalar.activation(lifted[:, 0:1], lift[:], ACT.Identity).then_inc(s["s_free"], 1)
                with act.Fori(0, CHUNKS) as c:
                    with act.Fori(0, STEPS) as st:
                        act.wait_ge(s["s_ready"], STEPS * c + st + 1)
                        act.wait_ge(s["s_free"], STEPS * c + st + 1)
                        act.wait_ge(s["adj_free"], STEPS * c + st + 1)
                        nc.scalar.activation(lifted[:], p_s[:], ACT.Identity, bias=lift[:, 0:1]).then_inc(s["s_free"], 1)
                    act.wait_ge(s["q_turned"], c + 1)
                    nc.scalar.copy(k.mov_hi[:, ds(CHUNK * c, CHUNK)], p_q[:]).then_inc(s["q_hi"], 1)

        @block.vector
        def _(dve):
            with dve.If(wide(dve)):
                nc.vector.memset(lift[:], LIFT).then_inc(s["lift_set"], 1)
                nc.vector.memset(masked[:, 0:1], 0.0).then_inc(s["adj_free"], 1)
                dve.wait_ge(s["adj_free"], 1)
                with dve.Fori(0, CHUNKS) as c:
                    nc.vector.memset(run[:], 0.0).then_inc(s["run_step"], 1)
                    with dve.Fori(0, STEPS // 2) as q:
                        for half in range(2):
                            n = STEPS * c + 2 * q + half
                            dve.wait_ge(s["s_free"], n + 2)
                            dve.wait_ge(s["adj_in"], 8 * (n + 2 - half))
                            dve.wait_ge(s["run_step"], 2 * n + c + 1)
                            nc.vector.scalar_tensor_tensor(masked[:], adj[:, half, :], 0.0, lifted[:], ALU.is_gt,
                                                           ALU.mult).then_inc(s["adj_free"], 1)
                            dve.wait_ge(s["adj_free"], n + 2)
                            for j in range(2):
                                dve.wait_ge(s["run_step"], 2 * n + c + 1 + j)
                                nc.vector.tensor_tensor(run[:], run[:], masked[:, CHUNK * j:CHUNK * j + CHUNK],
                                                        ALU.max).then_inc(s["run_step"], 1)
                    dve.wait_ge(s["turned"], c + 1)
                    nc.vector.tensor_reduce(top[:, 0, :], p_t[:].rearrange("p (t j) -> p t j", t=TPC), AX.X,
                                            ALU.max).then_inc(s["top_step"], 1)
                    dve.wait_ge(s["top_step"], 4 * c + 1)
                    nc.vector.tensor_scalar(top[:, 1, :], top[:, 0, :], -LIFT, -1.0, ALU.add, ALU.mult)\
                        .then_inc(s["top_step"], 1)
                    dve.wait_ge(s["top_step"], 4 * c + 2)
                    nc.vector.scalar_tensor_tensor(top[:, 2, :], top[:, 0, :], 0.0, top[:, 1, :], ALU.is_gt,
                                                   ALU.mult).then_inc(s["top_step"], 1)
                    nc.vector.tensor_scalar(unit[:], k.g_rows[:, ds(TPC * c, TPC), :], k.g_scale[:, 0:1], None,
                                            ALU.mult).then_inc(s["top_step"], 1)
                    dve.wait_ge(s["top_step"], 4 * c + 4)
                    nc.vector.tensor_copy(unit[:, :, D - 1], top[:, 2, :]).then_inc(s["unit_ready"], 1)
                    dve.wait_ge(s["q_hi"], c + 1)
                    nc.vector.tensor_tensor(k.mov_lo[:, ds(CHUNK * c, CHUNK)], p_q[:], k.mov_hi[:, ds(CHUNK * c, CHUNK)],
                                            ALU.subtract).then_inc(s["q_lo"], 1)
                    dve.wait_ge(s["unit_ready"], c + 1)


def scale_experts(k):
    nc = k.nc
    with ExitStack() as ctx:
        square = k.sb("s_square", [P, HID], F32, ctx)
        bound = k.sb("s_bound", [P, 2, HC], F32, ctx)
        own = k.sb("s_own", [P, 3], F32, ctx)
        every = k.sb("s_every", [P, 3], F32, ctx)
        every2 = k.sb("s_every2", [P, 3], F32, ctx)
        wd = k.wd[:].rearrange("p c e d -> p (c e d)")
        p_b = k.ps("s_p_b", [P, HC], ctx)
        names = ("squared", "columns", "rooted", "bounds", "b1", "owned", "all_ready", "scaled", "inverted", "split")
        s = {n: k.sem("s_" + n, ctx) for n in names}
        block = ctx.enter_context(nc.Block())

        @block.scalar
        def _(act):
            nc.scalar.activation(square[:], k.w1[:], ACT.Square).then_inc(s["squared"], 1)
            act.wait_ge(s["columns"], 1)
            nc.scalar.activation(bound[:, 0, :], p_b[:], ACT.Sqrt, scale=float(D)).then_inc(s["rooted"], 1)
            act.wait_ge(s["scaled"], 1)
            nc.scalar.activation(wd, wd, ACT.Copy, scale=k.e_scale[:, 1:2]).then_inc(s["split"], 1)
            act.wait_ge(s["split"], 1)
            nc.scalar.copy(k.wd_hi[:].rearrange("p c e d -> p (c e d)"), wd).then_inc(s["split"], 1)

        @block.tensor
        def _(pe):
            pe.wait_ge(s["squared"], 1)
            for c in range(HC):
                last = nc.tensor.matmul(p_b[:, c:c + 1], square[:, P * c:P * c + P], k.ones[:, 0:1], start=True, stop=True)
            last.then_inc(s["columns"], 1)

        @block.gpsimd
        def _(pool):
            pool.wait_ge(s["owned"], 3)
            nc.gpsimd.partition_all_reduce(every[:], own[:], P, bass.bass_isa.ReduceOp.max).then_inc(s["all_ready"], 1)

        @block.vector
        def _(dve):
            nc.vector.tensor_reduce(own[:, 1:2], wd, AX.X, ALU.max, apply_absolute_value=True).then_inc(s["owned"], 1)
            nc.vector.tensor_reduce(own[:, 2:3], k.wg[:].rearrange("p c e -> p (c e)"), AX.X, ALU.max,
                                    apply_absolute_value=True).then_inc(s["owned"], 1)
            nc.vector.tensor_scalar(bound[:, 1, :], k.b1[:], -1.0, None, ALU.mult).then_inc(s["bounds"], 1)
            dve.wait_ge(s["bounds"], 1)
            nc.vector.tensor_tensor(bound[:, 1, :], bound[:, 1, :], k.b1[:], ALU.max).then_inc(s["bounds"], 1)
            dve.wait_ge(s["bounds"], 2)
            dve.wait_ge(s["rooted"], 1)
            nc.vector.tensor_tensor(bound[:, 0, :], bound[:, 0, :], bound[:, 1, :], ALU.add).then_inc(s["bounds"], 1)
            dve.wait_ge(s["bounds"], 3)
            nc.vector.tensor_reduce(own[:, 0:1], bound[:, 0, :], AX.X, ALU.max).then_inc(s["owned"], 1)
            dve.wait_ge(s["all_ready"], 1)
            nc.vector.tensor_scalar(k.e_unit[:], every[:], 1e-15, 2.0 ** -14, ALU.max, ALU.mult).then_inc(s["inverted"], 1)
            dve.wait_ge(s["inverted"], 1)
            nc.vector.reciprocal(k.e_scale[:], k.e_unit[:]).then_inc(s["scaled"], 1)
            nc.vector.tensor_scalar(k.e_back[:], k.e_unit[:, 1:3], k.e_unit[:, 0:1], None, ALU.mult)
            dve.wait_ge(s["scaled"], 1)
            wg = k.wg[:].rearrange("p c e -> p (c e)")
            nc.vector.tensor_scalar(wg, wg, k.e_scale[:, 2:3], None, ALU.mult).then_inc(s["b1"], 1)
            dve.wait_ge(s["b1"], 1)
            nc.vector.tensor_copy(k.wg_hi[:].rearrange("p c e -> p (c e)"), wg).then_inc(s["b1"], 1)
            dve.wait_ge(s["b1"], 2)
            nc.vector.tensor_tensor(k.wg_lo[:].rearrange("p c e -> p (c e)"), wg,
                                    k.wg_hi[:].rearrange("p c e -> p (c e)"), ALU.subtract)
            dve.wait_ge(s["split"], 2)
            nc.vector.tensor_tensor(k.wd_lo[:].rearrange("p c e d -> p (c e d)"), wd,
                                    k.wd_hi[:].rearrange("p c e d -> p (c e d)"), ALU.subtract)


def experts(k):
    nc = k.nc
    with ExitStack() as ctx:
        f = k.sb("e_f", [P, TPC, D], F32, ctx)
        f_t = k.sb("e_f_t", [P, TPC * P], F32, ctx)
        hid = [k.sb(f"e_hid{i}", [P, CHUNK], F32, ctx) for i in range(2)]
        hid_hi = [k.sb(f"e_hid_hi{i}", [P, HC, CHUNK], F16, ctx) for i in range(2)]
        hid_lo = [k.sb(f"e_hid_lo{i}", [P, HC, CHUNK], F16, ctx) for i in range(2)]
        logit = k.sb("e_logit", [P, TPC, E], F32, ctx)
        shifted = k.sb("e_shifted", [P, TPC, E], F32, ctx)
        expo = k.sb("e_expo", [P, TPC, E], F32, ctx)
        chosen = k.sb("e_chosen", [P, 3, TPC, E], F32, ctx)
        red = k.sb("e_red", [P, 4, TPC], F32, ctx)
        gate = k.sb("e_gate", [P, TPC, E], F32, ctx)
        gate_y = [k.sb(f"e_gate_y{i}", [P, TPC, E], F32, ctx) for i in range(2)]
        gate_t = k.sb("e_gate_t", [E, TPC * P], F32, ctx)
        acc = [k.sb(f"e_acc{i}", [P, TPC, D], F32, ctx) for i in range(2)]
        p_ft = k.ps("e_p_ft", [P, TPC * P], ctx)
        p_h = [k.ps(f"e_p_h{i}", [P, CHUNK], ctx) for i in range(2)]
        p_l = k.ps("e_p_l", [P, TPC, E], ctx)
        p_gt = k.ps("e_p_gt", [P, TPC * P], ctx)
        p_y = [k.ps(f"e_p_y{i}", [P, E // 2, D], ctx) for i in range(2)]
        p_b = k.ps("e_p_b", [P, TPC, D], ctx)
        names = ("f_ready", "ft_ready", "ft_copied", "h_ready", "gelu_ready", "hi_ready", "lo_ready", "l_ready", "logits",
                 "tops", "shifts", "exps", "sums", "recips", "equals", "ranks", "firsts", "choices", "gates", "gates_y",
                 "gt_ready", "gt_copied", "b_ready", "acc_started", "y_ready", "sum_step")
        s = {n: k.sem("e_" + n, ctx) for n in names}
        ROUNDS = 2 * TPC
        SUMS = E // 2
        stored = [k.sem(f"e_stored{i}", ctx) for i in range(2)]
        out_dram = k.io["out"].rearrange("(t p) d -> p t d", p=P)
        block = ctx.enter_context(nc.Block())

        @block.sync
        def _(sp):
            with sp.Fori(0, CHUNKS // 2) as cc:
                for par in range(2):
                    c = 2 * cc + par
                    sp.wait_ge(s["sum_step"], SUMS * ROUNDS * (c + 1))
                    sp.dma_start(out_dram[:, ds(TPC * c, TPC), :], acc[par][:]).then_inc(stored[par], 16)
            for par in range(2):
                sp.wait_ge(stored[par], 16 * (CHUNKS // 2))

        @block.tensor
        def _(pe):
            def hidden(c, par, first):
                pe.wait_ge(s["f_ready"], c + 1)
                if not first:
                    pe.wait_ge(s["ft_copied"], c)
                for t in range(TPC):
                    last = nc.tensor.transpose(p_ft[:, P * t:P * t + P], f[:, t, :], k.ident[:])
                last.then_inc(s["ft_ready"], 1)
                pe.wait_ge(s["ft_copied"], c + 1)
                for h in range(HC):
                    if not (first and h < 2):
                        pe.wait_ge(s["gelu_ready"], HC * c + h - 1)
                    nc.tensor.matmul(p_h[h % 2][:], k.w1[:, P * h:P * h + P], f_t[:], start=True, stop=True)\
                        .then_inc(s["h_ready"], 1)

            def logits(c, par, first):
                pe.wait_ge(s["lo_ready"], HC * (c + 1))
                if not first:
                    pe.wait_ge(s["logits"], c)
                for t in range(TPC):
                    rows = slice(P * t, P * t + P)
                    for h in range(HC):
                        nc.tensor.matmul(p_l[:, t, :], hid_hi[par][:, h, rows], k.wg_hi[:, h, :], start=(h == 0), stop=False)
                        nc.tensor.matmul(p_l[:, t, :], hid_hi[par][:, h, rows], k.wg_lo[:, h, :], start=False, stop=False)
                        last = nc.tensor.matmul(p_l[:, t, :], hid_lo[par][:, h, rows], k.wg_hi[:, h, :], start=False,
                                                stop=(h == HC - 1))
                last.then_inc(s["l_ready"], 1)

            def biases(c, first):
                pe.wait_ge(s["gates"], c + 1)
                if not first:
                    pe.wait_ge(s["gt_copied"], c)
                for t in range(TPC):
                    last = nc.tensor.transpose(p_gt[0:E, P * t:P * t + P], gate[:, t, :], k.ident[:])
                last.then_inc(s["gt_ready"], 1)
                pe.wait_ge(s["gt_copied"], c + 1)
                if not first:
                    pe.wait_ge(s["acc_started"], c)
                for t in range(TPC):
                    last = nc.tensor.matmul(p_b[:, t, :], gate_t[:, P * t:P * t + P], k.bd[0:E, :], start=True, stop=True)
                last.then_inc(s["b_ready"], 1)

            def products(c, par, first, t):
                for half in range(2):
                    r = 2 * t + half
                    if not (first and r < 2):
                        pe.wait_ge(s["sum_step"], SUMS * (ROUNDS * c + r - 1))
                    rows = slice(P * t, P * t + P)
                    out = p_y[half][:].rearrange("p e d -> p (e d)")
                    for h in range(HC):
                        w_hi, w_lo = (w[:, h, 4 * half:4 * half + 4, :].rearrange("p e d -> p (e d)")
                                      for w in (k.wd_hi, k.wd_lo))
                        nc.tensor.matmul(out, hid_hi[par][:, h, rows], w_hi, start=(h == 0), stop=False)
                        nc.tensor.matmul(out, hid_hi[par][:, h, rows], w_lo, start=False, stop=False)
                        last = nc.tensor.matmul(out, hid_lo[par][:, h, rows], w_hi, start=False, stop=(h == HC - 1))
                    last.then_inc(s["y_ready"], 1)

            def chunk(c, par, first=False, last=False):
                biases(c, first)
                if not last:
                    hidden(c + 1, 1 - par, False)
                products(c, par, first, 0)
                products(c, par, first, 1)
                if not last:
                    logits(c + 1, 1 - par, False)
                products(c, par, first, 2)
                products(c, par, first, 3)

            hidden(0, 0, True)
            logits(0, 0, True)
            chunk(0, 0, first=True)
            chunk(1, 1)
            with pe.Fori(1, CHUNKS // 2 - 1) as cc:
                chunk(2 * cc, 0)
                chunk(2 * cc + 1, 1)
            chunk(CHUNKS - 2, 0)
            chunk(CHUNKS - 1, 1, last=True)

        @block.scalar
        def _(act):
            def front(c, par, first):
                act.wait_ge(s["ft_ready"], c + 1)
                if not first:
                    act.wait_ge(s["h_ready"], HC * c)
                nc.scalar.copy(f_t[:], p_ft[:]).then_inc(s["ft_copied"], 1)
                for h in range(HC):
                    act.wait_ge(s["h_ready"], HC * c + h + 1)
                    if not (first and h < 2):
                        act.wait_ge(s["lo_ready"], HC * c + h - 1)
                    nc.scalar.activation(hid[h % 2][:], p_h[h % 2][:], ACT.Gelu, bias=k.b1[:, h:h + 1])\
                        .then_inc(s["gelu_ready"], 1)
                    act.wait_ge(s["gelu_ready"], HC * c + h + 1)
                    if h == 0 and not (isinstance(c, int) and c < 2):
                        act.wait_ge(s["y_ready"], ROUNDS * (c - 1))
                    nc.scalar.activation(hid_hi[par][:, h, :], hid[h % 2][:], ACT.Copy, scale=k.e_scale[:, 0:1])\
                        .then_inc(s["hi_ready"], 1)

            front(0, 0, True)

            def step(c, par, first=False, last=False):
                act.wait_ge(s["shifts"], c + 1)
                nc.scalar.activation(expo[:], shifted[:], ACT.Exp).then_inc(s["exps"], 1)
                act.wait_ge(s["gt_ready"], c + 1)
                if not first:
                    act.wait_ge(s["b_ready"], c)
                nc.scalar.copy(gate_t[:], p_gt[0:E, :]).then_inc(s["gt_copied"], 1)
                if not last:
                    front(c + 1, 1 - par, False)

            step(0, 0, first=True)
            step(1, 1)
            with act.Fori(1, CHUNKS // 2 - 1) as cc:
                step(2 * cc, 0)
                step(2 * cc + 1, 1)
            step(CHUNKS - 2, 0)
            step(CHUNKS - 1, 1, last=True)

        @block.vector
        def _(dve):
            def rows(c, first):
                if not first:
                    dve.wait_ge(s["ft_ready"], c)
                for t in range(TPC):
                    last = normalised(k, f[:, t, :], c, t)
                last.then_inc(s["f_ready"], 1)

            def lows(c, par):
                for h in range(HC):
                    dve.wait_ge(s["hi_ready"], HC * c + h + 1)
                    nc.vector.scalar_tensor_tensor(hid_lo[par][:, h, :], hid[h % 2][:], k.e_scale[:, 0:1],
                                                   hid_hi[par][:, h, :], ALU.mult, ALU.subtract).then_inc(s["lo_ready"], 1)

            def wide(a):
                return a.unsqueeze(2).broadcast_to([P, TPC, E])

            def choose(c, par, first):
                dve.wait_ge(s["l_ready"], c + 1)
                nc.vector.scalar_tensor_tensor(logit[:].rearrange("p t e -> p (t e)"), p_l[:].rearrange("p t e -> p (t e)"),
                                               k.e_back[:, 1:2], k.bg[:], ALU.mult, ALU.add).then_inc(s["logits"], 1)
                dve.wait_ge(s["logits"], c + 1)
                nc.vector.tensor_reduce(red[:, 0, :], logit[:], AX.X, ALU.max).then_inc(s["tops"], 1)
                dve.wait_ge(s["tops"], c + 1)
                nc.vector.tensor_tensor(shifted[:], logit[:], wide(red[:, 0, :]), ALU.subtract).then_inc(s["shifts"], 1)
                nc.vector.tensor_tensor(chosen[:, 0], logit[:], wide(red[:, 0, :]), ALU.is_equal).then_inc(s["equals"], 1)
                dve.wait_ge(s["equals"], c + 1)
                nc.vector.tensor_tensor(chosen[:, 1], chosen[:, 0], k.ranks[:], ALU.mult).then_inc(s["ranks"], 1)
                dve.wait_ge(s["ranks"], c + 1)
                nc.vector.tensor_reduce(red[:, 1, :], chosen[:, 1], AX.X, ALU.max).then_inc(s["firsts"], 1)
                dve.wait_ge(s["firsts"], c + 1)
                nc.vector.tensor_tensor(chosen[:, 2], chosen[:, 1], wide(red[:, 1, :]), ALU.is_equal).then_inc(s["choices"], 1)
                dve.wait_ge(s["exps"], c + 1)
                nc.vector.tensor_reduce(red[:, 2, :], expo[:], AX.X, ALU.add).then_inc(s["sums"], 1)
                dve.wait_ge(s["sums"], c + 1)
                nc.vector.reciprocal(red[:, 3, :], red[:, 2, :]).then_inc(s["recips"], 1)
                dve.wait_ge(s["recips"], c + 1)
                dve.wait_ge(s["choices"], c + 1)
                if not first:
                    dve.wait_ge(s["gt_ready"], c)
                nc.vector.tensor_tensor(gate[:], chosen[:, 2], wide(red[:, 3, :]), ALU.mult).then_inc(s["gates"], 1)
                dve.wait_ge(s["gates"], c + 1)
                nc.vector.tensor_scalar(gate_y[par][:], gate[:], k.e_back[:, 0:1], None, ALU.mult).then_inc(s["gates_y"], 1)

            def begin(c, par):
                dve.wait_ge(s["b_ready"], c + 1)
                if not (isinstance(c, int) and c < 2):
                    dve.wait_ge(stored[par], 8 * (c - par))
                nc.vector.tensor_tensor(acc[par][:], p_b[:], k.x[:, ds(TPC * c, TPC), :], ALU.add).then_inc(s["acc_started"], 1)

            def add(c, par, t):
                dve.wait_ge(s["gates_y"], c + 1)
                for half in range(2):
                    r = 2 * t + half
                    dve.wait_ge(s["y_ready"], ROUNDS * c + r + 1)
                    for e in range(SUMS):
                        if r == 0 and e == 0:
                            dve.wait_ge(s["acc_started"], c + 1)
                        else:
                            dve.wait_ge(s["sum_step"], SUMS * (ROUNDS * c + r) + e)
                        nc.vector.scalar_tensor_tensor(acc[par][:, t, :], p_y[half][:, e, :],
                                                       gate_y[par][:, t, SUMS * half + e:SUMS * half + e + 1],
                                                       acc[par][:, t, :], ALU.mult, ALU.add).then_inc(s["sum_step"], 1)

            def step(c, par, first=False, last=False, rows_left=True):
                begin(c, par)
                add(c, par, 0)
                if rows_left:
                    rows(c + 2, False)
                if not last:
                    lows(c + 1, 1 - par)
                add(c, par, 1)
                if not last:
                    choose(c + 1, 1 - par, False)
                add(c, par, 2)
                add(c, par, 3)

            rows(0, True)
            rows(1, False)
            lows(0, 0)
            choose(0, 0, True)
            step(0, 0, first=True)
            step(1, 1)
            with dve.Fori(1, CHUNKS // 2 - 1) as cc:
                step(2 * cc, 0)
                step(2 * cc + 1, 1)
            step(CHUNKS - 2, 0, rows_left=False)
            step(CHUNKS - 1, 1, last=True, rows_left=False)


def build(nc, io):
    with ExitStack() as ctx:
        k = Core(nc, ctx, io)
        k.x = k.sb("x_rows", [P, T, D])
        k.g_rows = k.sb("g_rows", [P, T, D])
        k.row_hi, k.row_lo = (k.sb(n, [P, T, D], F16) for n in ("row_hi", "row_lo"))
        k.mov_hi, k.mov_lo = (k.sb(n, [P, N], F16) for n in ("mov_hi", "mov_lo"))
        k.sta_hi, k.sta_lo = (k.sb(n, [P, N], F16) for n in ("sta_hi", "sta_lo"))
        k.x_stats = k.sb("x_stats", [P, T // 2, 6])
        k.rstd, k.empty = (k.sb(n, [P, T]) for n in ("rstd", "empty"))
        k.ident, k.center, k.unaug_t = (k.sb(n, [P, D]) for n in ("ident", "center", "unaug_t"))
        k.unaug, k.wv_aug = (k.sb(n, [P, D + 1]) for n in ("unaug", "wv_aug"))
        k.ones = k.sb("ones", [P, P])
        k.ones_bf = k.sb("ones_bf", [P, P], BF16)
        k.ones_half = k.sb("ones_half", [P, 1], F16)
        k.zero_half = k.sb("zero_half", [P, P], F16)
        k.last_row = k.sb("last_row", [1, P])
        k.minus_half, k.eps, k.eps_sum, k.inv_d = (k.sb(n, [P, TPC]) for n in ("minus_half", "eps", "eps_sum", "inv_d"))
        k.shift = k.sb("shift", [P, 1])
        k.wkq_t = k.sb("wkq_t", [P, 2 * D])
        k.lnw, k.lnb, k.bq1 = (k.sb(n, [P, 1]) for n in ("lnw_col", "lnb_col", "bq1_col"))
        k.b_ffn, k.bv1 = (k.sb(n, [1, D]) for n in ("b_ffn_row", "bv1_row"))
        k.w_ffn_t, k.w_ffn, k.wq1, k.wk1 = (k.sb(n, [P, D]) for n in ("w_ffn_raw", "w_ffn", "wq1_raw", "wk1_raw"))
        k.wv1_t = k.sb("wv1_raw", [P, D])
        k.bias_ffn = k.sb("bias_ffn", [P, TPC, D], BF16)
        k.bias_mid = k.sb("bias_mid", [1, D], BF16)
        k.m_aug = k.sb("m_aug", [P, 2 * D])
        k.v_mean = k.sb("v_mean", [P, D])
        k.g_length, k.g_unit, k.g_scale = (k.sb(n, [P, 1]) for n in ("g_length", "g_unit", "g_scale"))
        k.wide_scores = k.sb("wide_scores", [P, 1], I32)
        k.w1 = k.sb("w1_raw", [P, HID])
        k.b1 = k.sb("b1_cols", [P, HC])
        k.wg = k.sb("wg_raw", [P, HC, E])
        k.wg_hi, k.wg_lo = (k.sb(n, [P, HC, E], F16) for n in ("wg_hi", "wg_lo"))
        k.bg, k.ranks = k.sb("bg_rows", [P, TPC * E]), k.sb("ranks", [P, TPC, E])
        k.wd = k.sb("wd_raw", [P, HC, E, D])
        k.wd_hi, k.wd_lo = (k.sb(n, [P, HC, E, D], F16) for n in ("wd_hi", "wd_lo"))
        k.bd = k.sb("bd_rows", [E, D])
        k.e_unit, k.e_scale, k.e_back = (k.sb(n, [P, w]) for n, w in (("e_unit", 3), ("e_scale", 3), ("e_back", 2)))

        load(k)
        prepare_weights(k)
        scale_experts(k)
        normalise_a(k)
        attention(k, "a_")
        recurrence(k)
        normalise_b(k)
        scale_queries(k)
        row_maxima(k)
        attention(k, "b_")
        experts(k)


def kernel(**inputs):
    import numpy as np
    import concourse.bacc as bacc
    from concourse.bass_utils import run_bass_kernel_spmd

    a = {n: np.ascontiguousarray(v) for n, v in inputs.items()}
    eye = np.eye(D, dtype=np.float32)
    unaug = np.concatenate([eye, eye[:, D - 1:]], axis=1)
    unaug[:D - 1, D - 1] = -1.0
    unaug[D - 1, D - 1] = 0.0
    arrays = {
        "x": a["x"],
        "adj_t": a["adj"].reshape(CHUNKS, CHUNK, STEPS // 2, 2, 2, P).transpose(0, 2, 5, 3, 4, 1)
                         .reshape(CHUNKS * STEPS // 2, P, 2, 2 * CHUNK),
        "wk0_t": a["L0_gnn_Wk"].T, "wq0_t": a["L0_gnn_Wq"].T,
        "lnw": a["L0_ffn_ln_w"].reshape(D, 1), "lnb": a["L0_ffn_ln_b"].reshape(D, 1),
        "w_ffn_t": a["L0_ffn_W"].T, "b_ffn": a["L0_ffn_b"].reshape(1, D),
        "wq1": a["L1_gnn_Wq"], "wk1": a["L1_gnn_Wk"], "wv1_t": a["L1_gnn_Wv"].T,
        "bq1": a["L1_gnn_bq"].reshape(D, 1), "bv1": a["L1_gnn_bv"].reshape(1, D),
        "w1": a["L1_ffn_W1"], "b1": a["L1_ffn_b1"].reshape(HC, P).T,
        "wg": a["L1_ffn_Wg"].reshape(HC, P, E).transpose(1, 0, 2),
        "bg": np.broadcast_to(a["L1_ffn_bg"], (P, TPC, E)).reshape(P, TPC * E),
        "wd": a["L1_ffn_Wd"].reshape(E, HC, P, D).transpose(2, 1, 0, 3),
        "bd": a["L1_ffn_bd"],
        "eye": eye, "centering": eye - np.float32(1.0 / D), "unaugment": unaug,
        "unaugment_t": unaug[:, :D].T, "last_row": eye[D - 1:],
        "ranks": np.broadcast_to(np.arange(E, 0, -1, dtype=np.float32), (P, TPC, E)),
    }
    arrays = {n: np.ascontiguousarray(v) for n, v in arrays.items()}
    nc = bacc.Bacc("TRN2", target_bir_lowering=False, num_devices=1)
    io = {n: nc.dram_tensor("in_" + n, v.shape, mybir.dt.from_np(v.dtype), kind="ExternalInput").ap()
          for n, v in arrays.items()}
    io["out"] = nc.dram_tensor("out_x", (N, D), F32, kind="ExternalOutput").ap()
    build(nc, io)
    result = run_bass_kernel_spmd(nc, [{"in_" + n: v for n, v in arrays.items()}], core_ids=[0])
    return result.results[0]["out_x"]
```

```python
from contextlib import ExitStack

import concourse.bass as bass
from concourse import mybir

F32 = mybir.dt.float32
F16 = mybir.dt.float16
BF16 = mybir.dt.bfloat16
I32 = mybir.dt.int32
ALU = mybir.AluOpType
ACT = mybir.ActivationFunctionType
AX = mybir.AxisListType
ds = bass.ds

P = 128
N = 4096
D = 128
T = N // P
CHUNK = 512
CHUNKS = N // CHUNK
TPC = CHUNK // P
STEPS = T // 2
ADJ = 4
STEPS_KERNEL = 30
HID = 512
HC = HID // P
E = 8
LN_EPS = 1e-5
COS_EPS = 1e-4
X_PARTS = 4
UNIT = 64.0
SHIFT = 3.5
S_MAX = 7.25


EARLY = {"ident": D, "wkq_t": 2 * D}
LATE = {"center": D, "unaug": D + 1, "unaug_t": D, "w_ffn_t": D, "wq1": D, "wk1": D, "wv1_t": D, "w1": HID, "lnw": 1,
        "lnb": 1, "bq1": 1, "b1": HC, "wg": HC * E, "bg": TPC * E, "ranks": TPC * E}
ROWS = {"last_row": D, "b_ffn": D, "bv1": D}


class Core:

    def __init__(self, nc, ctx, io):
        self.nc, self.ctx, self.io = nc, ctx, io

    def sb(self, name, shape, dt=F32, ctx=None):
        return (ctx or self.ctx).enter_context(self.nc.sbuf_tensor(name, shape, dt))

    def ps(self, name, shape, ctx):
        return ctx.enter_context(self.nc.psum_tensor(name, shape, F32))

    def sem(self, name, ctx):
        return ctx.enter_context(self.nc.semaphore(name))


def columns(tensor, widths):
    found, at = {}, 0
    for name, width in widths.items():
        found[name] = tensor[:, at:at + width]
        at += width
    return found


def peeled(eng, n, body):
    body(0, True)
    with eng.Fori(1, n) as i:
        body(i, False)


def slots(eng, tail, slot, ahead=0, head=2):
    for i in range(head):
        slot(i, i % 2)
    with eng.Fori(head // 2, (CHUNKS - ahead) // 2) as i:
        slot(2 * i, 0)
        slot(2 * i + 1, 1)
    for i in range(CHUNKS - ahead, CHUNKS + tail):
        slot(i, i % 2)


def has(i, lag):
    return not isinstance(i, int) or 0 <= i - lag < CHUNKS


def adjacency(k, tag, ctx):
    return ([k.sb(f"{tag}adj{i}", [P, 2, 2 * CHUNK], I32, ctx) for i in range(ADJ)],
            [k.sem(f"{tag}adj_in{i}", ctx) for i in range(ADJ)])


def prefetch(k, sp, adj, adj_in):
    for m in range(ADJ):
        sp.dma_start(adj[m][:], k.io["adj_t"][m:m + 1]).then_inc(adj_in[m], 16)


def past(g, before):
    return not isinstance(g, int) or g >= before


def row_stats(k, tag, ctx):
    names = ("measured", "inverting")
    s = {n: k.sem(tag + n, ctx) for n in names}
    s["variance"] = k.sb(tag + "variance", [P, 2, TPC], F32, ctx)
    return s


def measure_rows(k, s, g):
    for i in range(TPC // 2):
        k.nc.vector.bn_stats(k.x_stats[:, ds(TPC // 2 * g + i, 1), :],
                             k.x[:, ds(TPC * g + 2 * i, 2), :].rearrange("p t d -> p d t")).then_inc(s["measured"], 1)


def invert_rows(k, s, pool, g):
    nc = k.nc
    var, padded = s["variance"][:, 0], s["variance"][:, 1]
    pool.wait_ge(s["measured"], TPC // 2 * (g + 1))
    nc.gpsimd.tensor_tensor(var.rearrange("p (a b) -> p a b", b=2), k.x_stats[:, ds(TPC // 2 * g, TPC // 2), 2:6:3],
                            k.inv_d[:].rearrange("p (a b) -> p a b", b=2), ALU.mult).then_inc(s["inverting"], 1)
    pool.wait_ge(s["inverting"], 3 * g + 1)
    nc.gpsimd.tensor_tensor(padded, var, k.eps[:], ALU.add).then_inc(s["inverting"], 1)
    pool.wait_ge(s["inverting"], 3 * g + 2)
    nc.gpsimd.tensor_tensor(k.rstd[:, ds(TPC * g, TPC)], padded, k.minus_half[:], ALU.pow).then_inc(s["inverting"], 1)
    pool.wait_ge(s["inverting"], 3 * g + 3)


def normalised(k, out, g, t, features=D):
    tile = ds(TPC * g + t, 1)
    mean = k.x_stats[:, ds(TPC // 2 * g + t // 2, 1), 1 + 3 * (t % 2)]
    return k.nc.vector.tensor_scalar(out, k.x[:, tile, 0:features], mean, k.rstd[:, tile], ALU.subtract, ALU.mult)


def normalise_a(k, adj, adj_in):
    nc, io = k.nc, k.io
    with ExitStack() as ctx:
        f = [k.sb(f"a_f{i}", [P, TPC, D], F32, ctx) for i in range(2)]
        f_t = [k.sb(f"a_f_t{i}", [P, TPC * P], F32, ctx) for i in range(2)]
        square = k.sb("a_square", [P, 2 * TPC, D], F32, ctx)
        unit = k.sb("a_unit", [P, 2 * TPC, D], F32, ctx)
        norm = k.sb("a_norm", [P, 4, 2 * TPC], F32, ctx)
        p_ft = k.ps("a_p_ft", [P, TPC * P], ctx)
        p_kq = [k.ps(f"a_p_kq{i}", [P, TPC, 2 * D], ctx) for i in range(2)]
        p_t = k.ps("a_p_t", [P, 2, TPC * P], ctx)
        names = ("f_ready", "rows_hi", "rows_lo", "ft_ready", "ft_copied", "kq_ready", "squared", "rooted", "clamped",
                 "inverted", "unit_ready", "t_ready", "hi_ready", "lo_ready")
        s = {n: k.sem("a_" + n, ctx) for n in names}
        x_in = [k.sem(f"x_in{i}", ctx) for i in range(X_PARTS)]
        early_in, preset = k.sem("early_in", ctx), k.sem("preset", ctx)
        x_stats = row_stats(k, "ax_", ctx)
        block = ctx.enter_context(nc.Block())

        @block.sync
        def _(sp):
            x = io["x"].rearrange("(t p) d -> p t d", p=P)
            for i in range(X_PARTS):
                part = slice(T // X_PARTS * i, T // X_PARTS * (i + 1))
                sp.dma_start(k.x[:, part, :], x[:, part, :]).then_inc(x_in[i], 16)
                if i == 0:
                    sp.dma_start(k.early[:], io["early"]).then_inc(early_in, 16)
            for to, of in ((k.late[:], "late"), (k.rows[:], "rows"), (k.bd[0:E, :], "bd"), (k.wd[:], "wd")):
                sp.dma_start(to, io[of]).then_inc(k.late_in, 16)
            prefetch(k, sp, adj, adj_in)

        @block.vector
        def _(dve):
            nc.vector.memset(k.minus_half[:], -0.5)
            nc.vector.memset(k.inv_d[:], 1.0 / D)
            nc.vector.memset(k.eps[:], LN_EPS).then_inc(preset, 1)
            nc.vector.memset(k.eps_sum[:], LN_EPS * D)
            nc.vector.memset(k.ones_bf[:], 1.0)
            nc.vector.memset(k.ones[:], 1.0)
            nc.vector.memset(k.ones_half[:], 1.0)
            nc.vector.memset(k.zero_half[:], 0.0)
            nc.vector.memset(k.shift[:], SHIFT)
            nc.vector.memset(k.row_hi[:, :, D - 1:D], 1.0)
            nc.vector.memset(k.row_lo[:, :, D - 1:D], 0.0)
            groups_per_part = CHUNKS // X_PARTS

            def measure(g):
                if isinstance(g, int) and g < 4 and g % groups_per_part == 0:
                    dve.wait_ge(x_in[g // groups_per_part], 16)
                measure_rows(k, x_stats, g)

            measure(0)
            measure(1)

            def normalise(g, b):
                if past(g, 2):
                    dve.wait_ge(s["ft_ready"], g - 1)
                    dve.wait_ge(s["rows_hi"], g - 1)
                    dve.wait_ge(s["rows_lo"], g - 1)
                dve.wait_ge(x_stats["inverting"], 3 * g + 3)
                for t in range(TPC):
                    last = normalised(k, f[b][:, t, :], g, t)
                last.then_inc(s["f_ready"], 1)

            def scale(g, b):
                dve.wait_ge(s["rooted"], g + 1)
                nc.vector.tensor_scalar(norm[:, 2, :], norm[:, 1, :], COS_EPS, 1.0 / UNIT, ALU.max,
                                        ALU.mult).then_inc(s["clamped"], 1)
                dve.wait_ge(s["clamped"], g + 1)
                nc.vector.reciprocal(norm[:, 3, :], norm[:, 2, :]).then_inc(s["inverted"], 1)
                dve.wait_ge(s["inverted"], g + 1)
                if past(g, 1):
                    dve.wait_ge(s["t_ready"], g)
                for h in range(2):
                    last = nc.vector.tensor_tensor(
                        unit[:, TPC * h:TPC * h + TPC, :],
                        p_kq[b][:, 2 * h:2 * h + 2, :].rearrange("p t (w d) -> p (t w) d", w=2),
                        norm[:, 3, TPC * h:TPC * h + TPC].unsqueeze(2).broadcast_to([P, TPC, D]), ALU.mult)
                last.then_inc(s["unit_ready"], 1)

            def lows(g):
                dve.wait_ge(s["hi_ready"], g + 1)
                for w, lo, hi in ((0, k.mov_lo, k.mov_hi), (1, k.sta_lo, k.sta_hi)):
                    last = nc.vector.tensor_tensor(lo[:, ds(CHUNK * g, CHUNK)], p_t[:, w, :],
                                                   hi[:, ds(CHUNK * g, CHUNK)], ALU.subtract)
                last.then_inc(s["lo_ready"], 1)

            def slot(i, b):
                if has(i, 0):
                    normalise(i, b)
                if has(i, 1):
                    scale(i - 1, 1 - b)
                if has(i, 2):
                    lows(i - 2)
                if has(i, -2):
                    measure(i + 2)
                if isinstance(i, int) and i == 1:
                    for part in range(4 // groups_per_part, X_PARTS):
                        dve.wait_ge(x_in[part], 16)

            slots(dve, 2, slot, ahead=2)

        @block.gpsimd
        def _(pool):
            pool.wait_ge(preset, 1)
            invert_rows(k, x_stats, pool, 0)
            invert_rows(k, x_stats, pool, 1)

            def slot(i, b):
                pool.wait_ge(s["rows_hi"], i + 1)
                nc.gpsimd.tensor_tensor(k.row_lo[:, ds(TPC * i, TPC), 0:D - 1], f[b][:, :, 0:D - 1],
                                        k.row_hi[:, ds(TPC * i, TPC), 0:D - 1], ALU.subtract).then_inc(s["rows_lo"], 1)
                if has(i, -2):
                    invert_rows(k, x_stats, pool, i + 2)

            slots(pool, 0, slot, ahead=2)

        @block.scalar
        def _(act):
            def lengths(g, b):
                if past(g, 1):
                    act.wait_ge(s["rooted"], g)
                for half in range(2):
                    act.wait_ge(s["kq_ready"], 2 * g + half + 1)
                    for t in range(2 * half, 2 * half + 2):
                        for w in range(2):
                            j = 2 * t + w
                            last = nc.scalar.activation(square[:, j, :], p_kq[b][:, t, D * w:D * w + D], ACT.Square,
                                                        accum_out=norm[:, 0, j:j + 1])
                last.then_inc(s["squared"], 1)
                act.wait_ge(s["squared"], g + 1)
                if past(g, 1):
                    act.wait_ge(s["clamped"], g)
                nc.scalar.activation(norm[:, 1, :], norm[:, 0, :], ACT.Sqrt).then_inc(s["rooted"], 1)

            def slot(i, b):
                if has(i, 2):
                    act.wait_ge(s["t_ready"], i - 1)
                    nc.scalar.copy(k.mov_hi[:, ds(CHUNK * (i - 2), CHUNK)], p_t[:, 0, :])
                    nc.scalar.copy(k.sta_hi[:, ds(CHUNK * (i - 2), CHUNK)], p_t[:, 1, :]).then_inc(s["hi_ready"], 1)
                if has(i, 0):
                    act.wait_ge(s["ft_ready"], i + 1)
                    nc.scalar.copy(f_t[b][:], p_ft[:]).then_inc(s["ft_copied"], 1)
                    nc.scalar.copy(k.row_hi[:, ds(TPC * i, TPC), 0:D - 1], f[b][:, :, 0:D - 1]).then_inc(s["rows_hi"], 1)
                    lengths(i, b)

            slots(act, 2, slot)

        @block.tensor
        def _(pe):
            pe.wait_ge(early_in, 16)

            def keys_queries(g, b):
                pe.wait_ge(s["f_ready"], g + 1)
                if past(g, 1):
                    pe.wait_ge(s["ft_copied"], g)
                for t in range(TPC):
                    last = nc.tensor.transpose(p_ft[:, P * t:P * t + P], f[b][:, t, :], k.ident[:])
                last.then_inc(s["ft_ready"], 1)
                pe.wait_ge(s["ft_copied"], g + 1)
                if past(g, 2):
                    pe.wait_ge(s["unit_ready"], g - 1)
                for t in range(TPC):
                    last = nc.tensor.matmul(p_kq[b][:, t, :], f_t[b][:, P * t:P * t + P], k.wkq_t[:], start=True, stop=True)
                    if t % 2:
                        last.then_inc(s["kq_ready"], 1)

            def turn(g):
                pe.wait_ge(s["unit_ready"], g + 1)
                if past(g, 1):
                    pe.wait_ge(s["lo_ready"], g)
                for t in range(TPC):
                    for w in range(2):
                        last = nc.tensor.transpose(p_t[:, w, P * t:P * t + P], unit[:, 2 * t + w, :], k.ident[:])
                last.then_inc(s["t_ready"], 1)

            def slot(i, b):
                if has(i, 0):
                    keys_queries(i, b)
                if has(i, 1):
                    turn(i - 1)

            slots(pe, 1, slot)


def attention(k, tag, adj, adj_in):
    nc = k.nc
    is_a = tag == "a_"
    RING = 4
    LAG = 3
    POOL_STEP = 3
    QUADS = STEPS // 4
    LEAVE, TO_ROWS, FINISH = 3, 5, 6
    adj_dram = k.io["adj_t"]
    with ExitStack() as ctx:
        prob = [k.sb(f"{tag}prob{i}", [P, 2 * CHUNK], F32, ctx) for i in range(RING)]
        hi = [k.sb(f"{tag}hi{i}", [P, 2 * CHUNK], F16, ctx) for i in range(RING)]
        lo = [k.sb(f"{tag}lo{i}", [P, 2 * CHUNK], F16, ctx) for i in range(RING)]
        gathered = k.sb(tag + "gathered", [P, CHUNK], F32, ctx)
        small = k.sb(tag + "small", [P, 6, TPC], F32, ctx)
        rows = k.sb(tag + "rows", [P, 4, TPC, D], F32, ctx)
        p_s = [k.ps(f"{tag}p_s{i}", [P, 2 * CHUNK], ctx) for i in range(2)]
        p_o = [k.ps(f"{tag}p_o{i}", [P, CHUNK], ctx) for i in range(2)]
        p_r = k.ps(tag + "p_r", [P, 2, 512], ctx)
        names = ("s_ready", "exp_ready", "masked", "hi_ready", "lo_ready", "lo_pool_ready", "o_ready", "gathered_ready",
                 "r_ready", "post", "row_part", "elu_exp", "x_done", "split")
        s = {n: k.sem(tag + n, ctx) for n in names}
        x_stats = row_stats(k, tag, ctx)
        block = ctx.enter_context(nc.Block())

        def exists(f):
            return not isinstance(f, int) or f >= 0

        def wait_split(eng, f, st):
            if st == POOL_STEP:
                eng.wait_ge(s["lo_pool_ready"], f + 1)
            else:
                eng.wait_ge(s["lo_ready"], 3 * f + st + 1)

        def wait_used(eng, f, st):
            if exists(f - 1):
                eng.wait_ge(s["o_ready"], 4 * f + st - RING + 1)

        r_row = [p_r[:, t // 2, 129 * (t % 2):129 * (t % 2) + D] for t in range(TPC)]
        den = p_r[:, :, 0:258].rearrange("p b (t e) -> p b t e", e=129)[:, :, :, D]

        @block.sync
        def _(sp):
            def chunk(c, first):
                for q in range(CHUNKS):
                    m = CHUNKS * c + q
                    if first and q < ADJ:
                        continue
                    sp.wait_ge(s["masked"], 2 * (m - ADJ) + 2)
                    sp.dma_start(adj[q % ADJ][:], adj_dram[ds(m, 1)]).then_inc(adj_in[q % ADJ], 16)

            peeled(sp, CHUNKS, chunk)

        @block.tensor
        def _(pe):
            def scores(c, q, st):
                f = QUADS * c + q
                if exists(4 * f + st - 2):
                    pe.wait_ge(s["exp_ready"], 4 * f + st - 1)
                for j in range(2):
                    key = ds(P * (2 * (4 * q + st) + j), P)
                    out = p_s[st % 2][:, CHUNK * j:CHUNK * j + CHUNK]
                    q_hi, q_lo = (m[:, ds(CHUNK * c, CHUNK)] for m in (k.mov_hi, k.mov_lo))
                    nc.tensor.matmul(out, k.sta_hi[:, key], q_hi, start=True, stop=False)
                    nc.tensor.matmul(out, k.sta_hi[:, key], q_lo, start=False, stop=False)
                    last = nc.tensor.matmul(out, k.sta_lo[:, key], q_hi, start=False, stop=True)
                last.then_inc(s["s_ready"], 1)

            def values(c, par, q, st):
                wait_split(pe, QUADS * c + q, st)
                for j in range(2):
                    begin = isinstance(q, int) and q == 0 and st == 0 and j == 0
                    end = isinstance(q, int) and q == QUADS - 1 and st == 3 and j == 1
                    part = slice(CHUNK * j, CHUNK * j + CHUNK)
                    v_hi, v_lo = (m[:, ds(2 * (4 * q + st) + j, 1), :] for m in (k.row_hi, k.row_lo))
                    nc.tensor.matmul(p_o[par][:], v_hi, hi[st][:, part], start=begin, stop=False, skip_group_check=True)
                    nc.tensor.matmul(p_o[par][:], v_hi, lo[st][:, part], start=False, stop=False, skip_group_check=True)
                    last = nc.tensor.matmul(p_o[par][:], v_lo, hi[st][:, part], start=False, stop=end,
                                            skip_group_check=True)
                last.then_inc(s["o_ready"], 1)

            def to_rows(c):
                pe.wait_ge(s["gathered_ready"], c + 1)
                if exists(c - 1):
                    pe.wait_ge(s["post"], c)
                for t in range(TPC):
                    last = nc.tensor.matmul(p_r[:, t // 2, 129 * (t % 2):129 * (t % 2) + 129],
                                            gathered[:, P * t:P * t + P], (k.unaug if is_a else k.wv_aug)[:],
                                            start=True, stop=True)
                last.then_inc(s["r_ready"], 1)

            def steps(c, par, q):
                for st in range(4):
                    scores(c, q, st)
                    if st >= LAG:
                        if isinstance(q, int) and q == 0 and exists(c - 2):
                            pe.wait_ge(s["gathered_ready"], c - 1)
                        values(c, par, q, st - LAG)
                    elif not (isinstance(q, int) and q == 0):
                        values(c, par, q - 1, st - LAG + 4)
                    elif exists(c - 1):
                        values(c - 1, 1 - par, QUADS - 1, st - LAG + 4)
                    if isinstance(q, int) and 4 * q + st == TO_ROWS and exists(c - 1):
                        to_rows(c - 1)

            def chunk(c, par):
                steps(c, par, 0)
                steps(c, par, 1)
                with pe.Fori(2, QUADS) as q:
                    steps(c, par, q)

            chunk(0, 0)
            chunk(1, 1)
            with pe.Fori(1, CHUNKS // 2) as cc:
                chunk(2 * cc, 0)
                chunk(2 * cc + 1, 1)
            for st in range(4 - LAG, 4):
                values(CHUNKS - 1, 1, QUADS - 1, st)
            to_rows(CHUNKS - 1)

        @block.scalar
        def _(act):
            def exps(f, st):
                act.wait_ge(s["s_ready"], 4 * f + st + 1)
                if exists(f - 1):
                    wait_split(act, f - 1, st)
                nc.scalar.activation(prob[st][:], p_s[st % 2][:], ACT.Exp,
                                     bias=0.0 if is_a else k.shift[:, 0:1],
                                     scale=1.0 / UNIT ** 2 if is_a else k.g_unit[:, 0:1]).then_inc(s["exp_ready"], 1)

            def highs(f, st):
                act.wait_ge(s["masked"], 4 * f + st + 1)
                wait_used(act, f, st)
                nc.scalar.copy(hi[st][:], prob[st][:]).then_inc(s["hi_ready"], 1)

            def elu(c):
                act.wait_ge(s["row_part"], c + 1)
                nc.scalar.activation(rows[:, 2], rows[:, 1], ACT.Exp).then_inc(s["elu_exp"], 1)

            def chunk(c, first):
                for q in range(QUADS):
                    f = QUADS * c + q
                    for st in range(4):
                        exps(f, st)
                        if st > 0:
                            highs(f, st - 1)
                        elif exists(f - 1):
                            highs(f - 1, 3)
                        if not is_a and not first and 4 * q + st == FINISH + 5:
                            elu(c - 1)

            peeled(act, CHUNKS, chunk)
            highs(QUADS * CHUNKS - 1, 3)
            if not is_a:
                elu(CHUNKS - 1)

        @block.gpsimd
        def _(pool):
            def lows(f):
                pool.wait_ge(s["hi_ready"], 4 * f + POOL_STEP + 1)
                wait_used(pool, f, POOL_STEP)
                nc.gpsimd.tensor_tensor(lo[POOL_STEP][:], prob[POOL_STEP][:], hi[POOL_STEP][:],
                                        ALU.subtract).then_inc(s["lo_pool_ready"], 1)

            def split_weights(c, part):
                def eighths(tensors, width):
                    return [t[:, ds(width // CHUNKS * c, width // CHUNKS)] for t in tensors]

                flat = [w[:].rearrange("p c e d -> p (c e d)") for w in (k.wd, k.wd_hi, k.wd_lo)]
                wd, wd_hi, wd_lo = eighths(flat, HC * E * D)
                w1, w1_hi, w1_lo = eighths((k.w1, k.w1_hi, k.w1_lo), HID)
                if part == 0:
                    nc.gpsimd.tensor_tensor(wd, wd, k.e_scale[:, 1:2].broadcast_to([P, HC * E * D // CHUNKS]),
                                            ALU.mult).then_inc(s["split"], 1)
                    nc.gpsimd.tensor_tensor(w1, w1, k.e_scale[:, 3:4].broadcast_to([P, HID // CHUNKS]),
                                            ALU.mult).then_inc(s["split"], 1)
                elif part == 1:
                    pool.wait_ge(s["split"], 4 * c + 2)
                    nc.gpsimd.tensor_copy(wd_hi, wd).then_inc(s["split"], 1)
                    nc.gpsimd.tensor_copy(w1_hi, w1).then_inc(s["split"], 1)
                elif part == 2:
                    pool.wait_ge(s["split"], 4 * c + 4)
                    nc.gpsimd.tensor_tensor(wd_lo, wd, wd_hi, ALU.subtract)
                    nc.gpsimd.tensor_tensor(w1_lo, w1, w1_hi, ALU.subtract)

            def chunk(c, first):
                for q in range(QUADS):
                    lows(QUADS * c + q)
                    if is_a:
                        split_weights(c, q)
                if not first:
                    invert_rows(k, x_stats, pool, c - 1)

            peeled(pool, CHUNKS, chunk)
            invert_rows(k, x_stats, pool, CHUNKS - 1)

        @block.vector
        def _(dve):
            def mask(c, q, st):
                f = QUADS * c + q
                dve.wait_ge(s["exp_ready"], 4 * f + st + 1)
                transfer = 2 * q + st // 2
                dve.wait_ge(adj_in[transfer % ADJ], 16 * (2 * c + transfer // ADJ + 1))
                nc.vector.scalar_tensor_tensor(prob[st][:], adj[transfer % ADJ][:, st % 2, :], 0.0, prob[st][:],
                                               ALU.is_gt, ALU.mult).then_inc(s["masked"], 1)

            def lows(f, st):
                if st == POOL_STEP:
                    return
                dve.wait_ge(s["hi_ready"], 4 * f + st + 1)
                wait_used(dve, f, st)
                nc.vector.tensor_tensor(lo[st][:], prob[st][:], hi[st][:], ALU.subtract).then_inc(s["lo_ready"], 1)

            def leave(c, par):
                dve.wait_ge(s["o_ready"], STEPS * (c + 1))
                if exists(c - 1):
                    dve.wait_ge(s["r_ready"], c)
                nc.vector.tensor_copy(gathered[:], p_o[par][:]).then_inc(s["gathered_ready"], 1)

            def tile(c, t):
                return k.x[:, ds(TPC * c + t, 1), :]

            def finish_a(c, part):
                empty = k.empty[:, ds(TPC * c, TPC)]
                half_den, inv_den, w, w_rstd, x_factor, offset = (small[:, i, :] for i in range(6))
                if part == 0:
                    dve.wait_ge(s["r_ready"], c + 1)
                    nc.vector.tensor_scalar(empty, den, 0.0, None, ALU.is_equal).then_inc(s["row_part"], 1)
                    nc.vector.tensor_scalar(half_den, den, 1e-30, 2.0, ALU.max, ALU.mult).then_inc(s["row_part"], 1)
                elif part == 1:
                    dve.wait_ge(s["row_part"], 7 * c + 2)
                    nc.vector.tensor_scalar(w, empty, 0.5, 0.5, ALU.mult, ALU.add).then_inc(s["row_part"], 1)
                    nc.vector.reciprocal(inv_den, half_den).then_inc(s["row_part"], 1)
                elif part == 2:
                    dve.wait_ge(s["row_part"], 7 * c + 4)
                    nc.vector.tensor_tensor(w_rstd, w, k.rstd[:, ds(TPC * c, TPC)], ALU.mult).then_inc(s["row_part"], 1)
                elif part == 3:
                    dve.wait_ge(s["row_part"], 7 * c + 5)
                    nc.vector.tensor_scalar(x_factor, w_rstd, 1.0, None, ALU.add).then_inc(s["row_part"], 1)
                    nc.vector.scalar_tensor_tensor(offset.rearrange("p (a b) -> p a b", b=2),
                                                   k.x_stats[:, ds(TPC // 2 * c, TPC // 2), 1:5:3], -1.0,
                                                   w_rstd.rearrange("p (a b) -> p a b", b=2),
                                                   ALU.mult, ALU.mult).then_inc(s["row_part"], 1)
                elif part == 4:
                    dve.wait_ge(s["row_part"], 7 * c + 7)
                    for t in range(TPC):
                        last = nc.vector.tensor_scalar(rows[:, 0, t, :], tile(c, t), x_factor[:, t:t + 1],
                                                       offset[:, t:t + 1], ALU.mult, ALU.add)
                    last.then_inc(s["x_done"], 1)
                elif part == 5:
                    dve.wait_ge(s["x_done"], c + 1)
                    for t in range(TPC):
                        last = nc.vector.scalar_tensor_tensor(tile(c, t), r_row[t], inv_den[:, t:t + 1],
                                                              rows[:, 0, t, :], ALU.mult, ALU.add)
                    last.then_inc(s["post"], 1)
                elif part == 6:
                    dve.wait_ge(s["post"], c + 1)
                    measure_rows(k, x_stats, c)

            def finish_b(c, part):
                some_den, inv_den = small[:, 0, :], small[:, 1, :]
                att, negative, expo, total = (rows[:, i] for i in range(4))
                x = k.x[:, ds(TPC * c, TPC), :]
                if part == 0:
                    dve.wait_ge(s["r_ready"], c + 1)
                    nc.vector.tensor_scalar(some_den, den, 1e-30, None, ALU.max).then_inc(s["x_done"], 1)
                elif part == 1:
                    dve.wait_ge(s["x_done"], 5 * c + 1)
                    nc.vector.reciprocal(inv_den, some_den).then_inc(s["x_done"], 1)
                elif part == 2:
                    dve.wait_ge(s["x_done"], 5 * c + 2)
                    for t in range(TPC):
                        last = nc.vector.tensor_scalar(total[:, t, :], r_row[t], inv_den[:, t:t + 1], None, ALU.mult)
                    last.then_inc(s["post"], 1)
                elif part == 3:
                    dve.wait_ge(s["post"], c + 1)
                    for t in range(TPC):
                        last = nc.vector.scalar_tensor_tensor(att[:, t, :], k.v_mean[:], k.empty[:, ds(TPC * c + t, 1)],
                                                              total[:, t, :], ALU.mult, ALU.add)
                    last.then_inc(s["x_done"], 1)
                elif part == 4:
                    dve.wait_ge(s["x_done"], 5 * c + 3)
                    nc.vector.tensor_scalar(negative, att, 0.0, None, ALU.min).then_inc(s["row_part"], 1)
                elif part == 7:
                    dve.wait_ge(s["elu_exp"], c + 1)
                    nc.vector.scalar_tensor_tensor(total, att, 0.0, expo, ALU.max, ALU.add).then_inc(s["x_done"], 1)
                elif part == 8:
                    dve.wait_ge(s["x_done"], 5 * c + 4)
                    nc.vector.scalar_tensor_tensor(x, total, -1.0, x, ALU.add, ALU.add).then_inc(s["x_done"], 1)
                elif part == 9:
                    dve.wait_ge(s["x_done"], 5 * c + 5)
                    measure_rows(k, x_stats, c)

            finish = finish_a if is_a else finish_b

            def chunk(c, par):
                for q in range(QUADS):
                    for st in range(4):
                        mask(c, q, st)
                        if st > 0:
                            lows(QUADS * c + q, st - 1)
                        elif exists(QUADS * c + q - 1):
                            lows(QUADS * c + q - 1, 3)
                        if exists(c - 1):
                            if 4 * q + st == LEAVE:
                                leave(c - 1, 1 - par)
                            if 4 * q + st >= FINISH:
                                finish(c - 1, 4 * q + st - FINISH)

            chunk(0, 0)
            chunk(1, 1)
            with dve.Fori(1, CHUNKS // 2) as cc:
                chunk(2 * cc, 0)
                chunk(2 * cc + 1, 1)
            lows(QUADS * CHUNKS - 1, 3)
            leave(CHUNKS - 1, 1)
            for part in range(STEPS - FINISH):
                finish(CHUNKS - 1, part)


def prepare_weights(k):
    nc = k.nc
    with ExitStack() as ctx:
        scaled = k.sb("w_scaled", [P, D], F32, ctx)
        row = k.sb("w_row", [1, 4, D], F32, ctx)
        m_qk = k.sb("w_m_qk", [P, D], F32, ctx)
        square = k.sb("w_square", [P, HID], F32, ctx)
        bound = k.sb("w_bound", [P, 2, HC], F32, ctx)
        own, every = (k.sb("w_" + n, [P, 4], F32, ctx) for n in ("own", "every"))
        p_w, p_bias, p_qk, p_bq, p_m, p_v, p_b = (k.ps("w_p_" + n, [P, D], ctx)
                                                  for n in ("w", "bias", "qk", "bq", "m", "v", "b"))
        names = ("scaled", "bias", "qk", "first", "second", "m_ready", "squared", "columns", "rooted", "bounds", "owned",
                 "all_ready", "e_unit", "e_scale", "wg")
        s = {n: k.sem("w_" + n, ctx) for n in names}
        wd = k.wd[:].rearrange("p c e d -> p (c e d)")
        wg = k.wg[:]
        wg_hi, wg_lo = (w[:].rearrange("p c e -> p (c e)") for w in (k.wg_hi, k.wg_lo))
        block = ctx.enter_context(nc.Block())
        LOADED = 16 * 4

        @block.vector
        def _(dve):
            dve.wait_ge(k.late_in, LOADED)
            nc.vector.tensor_scalar(scaled[:], k.w_ffn_t[:], k.lnw[:, 0:1], None, ALU.mult).then_inc(s["scaled"], 1)
            nc.vector.memset(k.bias_ffn[:], 0.0).then_inc(s["bias"], 1)
            nc.vector.tensor_reduce(own[:, 2:3], wg, AX.X, ALU.max, apply_absolute_value=True).then_inc(s["owned"], 1)
            nc.vector.tensor_reduce(own[:, 3:4], k.w1[:], AX.X, ALU.max, apply_absolute_value=True).then_inc(s["owned"], 1)
            nc.vector.tensor_scalar(bound[:, 1, :], k.b1[:], -1.0, None, ALU.mult).then_inc(s["bounds"], 1)
            nc.vector.tensor_reduce(own[:, 1:2], wd, AX.X, ALU.max, apply_absolute_value=True).then_inc(s["owned"], 1)
            dve.wait_ge(s["bounds"], 1)
            nc.vector.tensor_tensor(bound[:, 1, :], bound[:, 1, :], k.b1[:], ALU.max).then_inc(s["bounds"], 1)
            dve.wait_ge(s["bounds"], 2)
            dve.wait_ge(s["rooted"], 1)
            nc.vector.tensor_tensor(bound[:, 0, :], bound[:, 0, :], bound[:, 1, :], ALU.add).then_inc(s["bounds"], 1)
            dve.wait_ge(s["bounds"], 3)
            nc.vector.tensor_reduce(own[:, 0:1], bound[:, 0, :], AX.X, ALU.max).then_inc(s["owned"], 1)

            dve.wait_ge(s["first"], 4)
            nc.vector.tensor_scalar(k.w_ffn[:], p_w[:], D ** 0.5, None, ALU.mult)
            nc.vector.tensor_tensor(row[:, 0, :], p_bias[0:1, :], k.b_ffn[0:1, :], ALU.add).then_inc(s["bias"], 1)
            nc.vector.tensor_scalar(m_qk[:], p_qk[:], D ** -0.5, None, ALU.mult).then_inc(s["qk"], 1)
            nc.vector.tensor_scalar(row[:, 3, :], p_bq[0:1, :], D ** -0.5, None, ALU.mult).then_inc(s["qk"], 1)
            dve.wait_ge(s["bias"], 2)
            for t in range(TPC):
                last = nc.vector.tensor_copy(k.bias_ffn[0:1, t, :], row[:, 0, :])
            last.then_inc(s["bias"], 1)
            dve.wait_ge(s["bias"], 3)
            nc.vector.tensor_tensor(row[:, 1, :], row[:, 0, :], k.bias_ffn[0:1, 0, :], ALU.subtract).then_inc(s["bias"], 1)
            dve.wait_ge(s["bias"], 4)
            for t in range(TPC):
                nc.vector.tensor_copy(k.bias_ffn[32:33, t, :], row[:, 1, :])
            nc.vector.tensor_copy(k.bias_mid[:], row[:, 1, :]).then_inc(s["bias"], 1)
            dve.wait_ge(s["bias"], 5)
            nc.vector.tensor_tensor(row[:, 2, :], row[:, 1, :], k.bias_mid[:], ALU.subtract).then_inc(s["bias"], 1)
            dve.wait_ge(s["bias"], 6)
            for t in range(TPC):
                nc.vector.tensor_copy(k.bias_ffn[64:65, t, :], row[:, 2, :])
            dve.wait_ge(s["second"], 2)
            nc.vector.tensor_copy(k.m_aug[:, 0:D], p_m[:]).then_inc(s["m_ready"], 1)
            nc.vector.tensor_copy(k.wv_aug[:, 0:D], p_v[:])
            nc.vector.tensor_copy(k.wv_aug[:, D:D + 1], k.unaug[:, D:D + 1])
            dve.wait_ge(s["m_ready"], 1)
            nc.vector.tensor_scalar(k.m_aug[:, D:2 * D], k.m_aug[:, 0:D], k.m_aug[:, D - 1:D], None, ALU.subtract)

            dve.wait_ge(s["all_ready"], 1)
            nc.vector.tensor_scalar(k.e_unit[:], every[:], 1e-15, 2.0 ** -14, ALU.max, ALU.mult).then_inc(s["e_unit"], 1)
            dve.wait_ge(s["e_unit"], 1)
            nc.vector.reciprocal(k.e_scale[:], k.e_unit[:]).then_inc(s["e_scale"], 1)
            nc.vector.tensor_scalar(k.e_back[:], k.e_unit[:, 1:3], k.e_unit[:, 0:1], None, ALU.mult)
            dve.wait_ge(s["e_scale"], 1)
            nc.vector.tensor_scalar(wg, wg, k.e_scale[:, 2:3], None, ALU.mult).then_inc(s["wg"], 1)
            dve.wait_ge(s["wg"], 1)
            nc.vector.tensor_copy(wg_hi, wg).then_inc(s["wg"], 1)
            dve.wait_ge(s["wg"], 2)
            nc.vector.tensor_tensor(wg_lo, wg, wg_hi, ALU.subtract)

        @block.scalar
        def _(act):
            act.wait_ge(k.late_in, LOADED)
            nc.scalar.activation(square[:], k.w1[:], ACT.Square).then_inc(s["squared"], 1)
            act.wait_ge(s["columns"], 1)
            nc.scalar.activation(bound[:, 0, :], p_b[:, 0:HC], ACT.Sqrt, scale=float(D)).then_inc(s["rooted"], 1)

        @block.gpsimd
        def _(pool):
            pool.wait_ge(s["owned"], 4)
            nc.gpsimd.partition_all_reduce(every[:], own[:], P, bass.bass_isa.ReduceOp.max).then_inc(s["all_ready"], 1)

        @block.tensor
        def _(pe):
            pe.wait_ge(k.late_in, LOADED)
            pe.wait_ge(s["scaled"], 1)
            nc.tensor.matmul(p_w[:], k.center[:], scaled[:], start=True, stop=True).then_inc(s["first"], 1)
            nc.tensor.matmul(p_bias[0:1, :], k.lnb[:], k.w_ffn_t[:], start=True, stop=True).then_inc(s["first"], 1)
            nc.tensor.matmul(p_qk[:], k.wq1[:], k.wk1[:], start=True, stop=True).then_inc(s["first"], 1)
            nc.tensor.matmul(p_bq[0:1, :], k.bq1[:], k.wk1[:], start=True, stop=True).then_inc(s["first"], 1)
            pe.wait_ge(s["squared"], 1)
            for c in range(HC):
                last = nc.tensor.matmul(p_b[:, c:c + 1], square[:, P * c:P * c + P], k.ones[:, 0:1], start=True, stop=True)
            last.then_inc(s["columns"], 1)
            pe.wait_ge(s["qk"], 2)
            nc.tensor.matmul(p_m[:], k.unaug_t[:], m_qk[:], start=True, stop=False)
            nc.tensor.matmul(p_m[:], k.last_row[0:1, :], row[:, 3, :], start=False, stop=True).then_inc(s["second"], 1)
            nc.tensor.matmul(p_v[:], k.unaug_t[:], k.wv1_t[:], start=True, stop=False)
            nc.tensor.matmul(p_v[:], k.last_row[0:1, :], k.bv1[0:1, :], start=False, stop=True).then_inc(s["second"], 1)


def recurrence(k, x_stats):
    nc = k.nc
    G = T // TPC
    ITEMS = G * STEPS_KERNEL
    YB, TB = 4, 2
    DVE_TILES, POOL_TILES = (2, 3) * (G // 2), (1,) * G
    act_groups = [g for g in range(G) if DVE_TILES[g] + POOL_TILES[g] < TPC]
    UNIT_LAG, LEAVE_LAG = 4, 6
    with ExitStack() as ctx:
        def ring(name, n):
            return [k.sb(f"r_{name}{g}", [P, TPC * D], F32, ctx) for g in range(n)]

        R = 4
        tanh, h, z_t, z, z_unit = ring("tanh", R), ring("h", R), ring("z_t", R), ring("z", G), ring("z_unit", G)
        parts = [k.sb(f"r_parts{g}", [P, TPC // 2, 6], F32, ctx) for g in range(G)]
        stat = [k.sb(f"r_stat{g}", [P, 2, TPC], F32, ctx) for g in range(G)]
        p_y = [k.ps(f"r_p_y{i}", [P, TPC * D], ctx) for i in range(YB)]
        p_t = [k.ps(f"r_p_t{i}", [P, TPC * P], ctx) for i in range(TB)]
        names = ("start_ready", "y_ready", "tanh_ready", "h_ready", "z_ready", "measured", "padded", "rstd_ready",
                 "unit_ready", "unit_act_ready", "unit_pool_ready", "t_ready", "zt_ready")
        s = {n: k.sem("r_" + n, ctx) for n in names}
        block = ctx.enter_context(nc.Block())

        def tiles(a):
            return a[:].rearrange("p (t d) -> p t d", t=TPC)

        @block.tensor
        def _(pe):
            def start(m):
                pe.wait_ge(s["start_ready"], m + 1)
                if m >= YB:
                    pe.wait_ge(s["h_ready"], m - YB + 1)
                nc.tensor.matmul(p_y[m % YB][:], k.ident[:], z_unit[m][:], start=True, stop=True).then_inc(s["y_ready"], 1)

            def turn(i, g, first):
                n = G * i + g
                pe.wait_ge(s["unit_ready"], n + 1)
                pe.wait_ge(s["unit_pool_ready"], n + 1)
                if g in act_groups:
                    pe.wait_ge(s["unit_act_ready"], len(act_groups) * i + act_groups.index(g) + 1)
                if not (first and g < TB):
                    pe.wait_ge(s["zt_ready"], n - TB + 1)
                for t in range(TPC):
                    last = nc.tensor.transpose(p_t[g % TB][:, P * t:P * t + P], z_unit[g][:, D * t:D * t + D], k.ident[:])
                last.then_inc(s["t_ready"], 1)

            def linear(n, g):
                pe.wait_ge(s["zt_ready"], n + 1)
                pe.wait_ge(s["h_ready"], n + G - YB + 1)
                out = p_y[g % YB]
                nc.tensor.matmul(out[:], k.ones_bf[:], k.bias_ffn[:].rearrange("p t d -> p (t d)"), start=True,
                                 stop=False, skip_group_check=True)
                for t in range(TPC):
                    last = nc.tensor.matmul(out[:, D * t:D * t + D], z_t[g % R][:, P * t:P * t + P], k.w_ffn[:], start=False,
                                            stop=(t == TPC - 1), skip_group_check=True)
                last.then_inc(s["y_ready"], 1)

            for m in range(G):
                start(m)

            def step(i, first):
                for g in range(G):
                    turn(i, g, first)
                    if not (first and g == 0):
                        linear(G * i + g - 1, (g - 1) % G)

            peeled(pe, STEPS_KERNEL, step)
            linear(ITEMS - 1, G - 1)

        @block.scalar
        def _(act):
            def tanhs(n, g):
                act.wait_ge(s["y_ready"], n + 1)
                nc.scalar.activation(tanh[g % R][:], p_y[g % YB][:], ACT.Tanh).then_inc(s["tanh_ready"], 1)

            def silus(n, g):
                act.wait_ge(s["h_ready"], n + 1)
                nc.scalar.activation(z[g][:], h[g % R][:], ACT.Silu).then_inc(s["z_ready"], 1)

            def unit(n, g):
                if g not in act_groups:
                    return
                act.wait_ge(s["rstd_ready"], n + 1)
                for t in range(DVE_TILES[g] + POOL_TILES[g], TPC):
                    last = nc.scalar.activation(z_unit[g][:, D * t:D * t + D], z[g][:, D * t:D * t + D], ACT.Copy,
                                                scale=stat[g][:, 1, t:t + 1])
                last.then_inc(s["unit_act_ready"], 1)

            def leave(n, g):
                act.wait_ge(s["t_ready"], n + 1)
                nc.scalar.copy(z_t[g % R][:], p_t[g % TB][:]).then_inc(s["zt_ready"], 1)

            stages = ((0, tanhs), (1, silus), (UNIT_LAG, unit), (LEAVE_LAG, leave))

            def step(i, first):
                for g in range(G):
                    for lag, stage in stages:
                        if not (first and g < lag):
                            stage(G * i + g - lag, (g - lag) % G)

            peeled(act, STEPS_KERNEL, step)
            for n in range(ITEMS, ITEMS + LEAVE_LAG):
                for lag, stage in stages:
                    if n - lag < ITEMS:
                        stage(n - lag, (n - lag) % G)

        @block.vector
        def _(dve):
            def start(g):
                for t in range(TPC):
                    last = normalised(k, z_unit[g][:, D * t:D * t + D], g, t)
                last.then_inc(s["start_ready"], 1)

            def add_tanh(n, g):
                dve.wait_ge(s["tanh_ready"], n + 1)
                nc.vector.scalar_tensor_tensor(h[g % R][:], tanh[g % R][:], 0.01, p_y[g % YB][:], ALU.mult, ALU.add)\
                    .then_inc(s["h_ready"], 1)

            def measure(n, g):
                dve.wait_ge(s["z_ready"], n + 1)
                for i in range(TPC // 2):
                    last = nc.vector.bn_stats(parts[g][:, i, :], tiles(z[g])[:, 2 * i:2 * i + 2, :].rearrange("p t d -> p d t"))
                last.then_inc(s["measured"], 1)

            def unit(n, g):
                dve.wait_ge(s["rstd_ready"], n + 1)
                own = DVE_TILES[g]
                nc.vector.tensor_tensor(tiles(z_unit[g])[:, 0:own, :], tiles(z[g])[:, 0:own, :],
                                        stat[g][:, 1, 0:own].unsqueeze(2).broadcast_to([P, own, D]), ALU.mult).then_inc(s["unit_ready"], 1)

            stages = ((0, add_tanh), (1, measure), (UNIT_LAG, unit))
            for g in range(2):
                start(g)

            def step(i, first):
                for g in range(G):
                    if first and g + 2 < G:
                        start(g + 2)
                    for lag, stage in stages:
                        if not (first and g < lag):
                            stage(G * i + g - lag, (g - lag) % G)

            peeled(dve, STEPS_KERNEL, step)
            for n in range(ITEMS, ITEMS + UNIT_LAG):
                for lag, stage in stages:
                    if n - lag < ITEMS:
                        stage(n - lag, (n - lag) % G)
            for g in range(G):
                dve.wait_ge(s["y_ready"], ITEMS + g + 1)
                xr = k.x[:, TPC * g:TPC * g + TPC, :]
                nc.vector.tensor_tensor(xr, xr, tiles(p_y[g % YB]), ALU.add).then_inc(s["h_ready"], 1)
                dve.wait_ge(s["h_ready"], ITEMS + g + 1)
                measure_rows(k, x_stats, g)

        @block.gpsimd
        def _(pool):
            def rstds(n, g):
                pool.wait_ge(s["measured"], n + 1)
                nc.gpsimd.tensor_tensor(stat[g][:, 0, :].rearrange("p (a b) -> p a b", b=2), parts[g][:, :, 2:6:3],
                                        k.eps_sum[:].rearrange("p (a b) -> p a b", b=2), ALU.add).then_inc(s["padded"], 1)
                pool.wait_ge(s["padded"], n + 1)
                nc.gpsimd.tensor_tensor(stat[g][:, 1, :], stat[g][:, 0, :], k.minus_half[:], ALU.pow)\
                    .then_inc(s["rstd_ready"], 1)

            def unit(n, g):
                pool.wait_ge(s["rstd_ready"], n + 1)
                own = slice(DVE_TILES[g], DVE_TILES[g] + POOL_TILES[g])
                nc.gpsimd.tensor_tensor(tiles(z_unit[g])[:, own, :], tiles(z[g])[:, own, :],
                                        stat[g][:, 1, own].unsqueeze(2).broadcast_to([P, POOL_TILES[g], D]),
                                        ALU.mult).then_inc(s["unit_pool_ready"], 1)

            def step(i, first):
                for g in range(G):
                    rstds(G * i + g, g)
                    unit(G * i + g, g)

            peeled(pool, STEPS_KERNEL, step)


def normalise_b(k, x_stats, adj, adj_in):
    nc = k.nc
    with ExitStack() as ctx:
        f = [k.sb(f"n_f{i}", [P, TPC, D], F32, ctx) for i in range(2)]
        f_t = [k.sb(f"n_f_t{i}", [P, TPC * P], F32, ctx) for i in range(2)]
        square = [k.sb(f"n_square{i}", [P, TPC, D], F32, ctx) for i in range(2)]
        length = k.sb("n_length", [P, T], F32, ctx)
        f_sum = k.sb("n_f_sum", [P, 1], F32, ctx)
        f_sums = k.sb("n_f_sums", [P, P], F32, ctx)
        p_ft = k.ps("n_p_ft", [P, TPC * P], ctx)
        p_g = [k.ps(f"n_p_g{i}", [P, 2, TPC, D], ctx) for i in range(2)]
        p_sum = k.ps("n_p_sum", [P, 1], ctx)
        p_mean = k.ps("n_p_mean", [P, D + 1], ctx)
        names = ("preset", "f_ready", "rows_hi", "rows_lo", "ft_ready", "ft_copied", "hi_ready", "lo_ready", "g_ready",
                 "squared", "g_kept", "sum_ready", "sum_copied", "sums_ready", "mean_ready")
        s = {n: k.sem("n_" + n, ctx) for n in names}
        block = ctx.enter_context(nc.Block())

        @block.sync
        def _(sp):
            prefetch(k, sp, adj, adj_in)

        @block.vector
        def _(dve):
            for i in range(2):
                nc.vector.memset(f[i][:, :, D - 1:D], 1.0).then_inc(s["preset"], 1)

            def slot(i, b):
                if has(i, 0):
                    if past(i, 2):
                        dve.wait_ge(s["ft_ready"], i - 1)
                        dve.wait_ge(s["rows_hi"], i - 1)
                        dve.wait_ge(s["rows_lo"], i - 1)
                    dve.wait_ge(x_stats["inverting"], 3 * i + 3)
                    for t in range(TPC):
                        last = normalised(k, f[b][:, t, 0:D - 1], i, t, D - 1)
                    last.then_inc(s["f_ready"], 1)
                if has(i, 1):
                    dve.wait_ge(s["hi_ready"], i)
                    nc.vector.tensor_tensor(k.sta_lo[:, ds(CHUNK * (i - 1), CHUNK)], f_t[1 - b][:],
                                            k.sta_hi[:, ds(CHUNK * (i - 1), CHUNK)], ALU.subtract).then_inc(s["lo_ready"], 1)
                if has(i, 2):
                    dve.wait_ge(s["g_ready"], i - 1)
                    nc.vector.tensor_copy(k.g_rows[:, ds(TPC * (i - 2), TPC), :], p_g[b][:, 1]).then_inc(s["g_kept"], 1)

            slots(dve, 2, slot)
            dve.wait_ge(s["squared"], CHUNKS)
            nc.vector.tensor_reduce(k.g_length[:, 0:1], length[:], AX.X, ALU.max)
            dve.wait_ge(s["sum_ready"], 1)
            nc.vector.tensor_copy(f_sum[:], p_sum[:]).then_inc(s["sum_copied"], 1)
            dve.wait_ge(s["sum_copied"], 1)
            nc.vector.tensor_scalar(f_sums[:], k.ones[:], f_sum[:, 0:1], None, ALU.mult).then_inc(s["sums_ready"], 1)
            dve.wait_ge(s["mean_ready"], 1)
            nc.vector.tensor_scalar(k.v_mean[:], p_mean[:, 0:D], 1.0 / N, None, ALU.mult)

        @block.gpsimd
        def _(pool):
            invert_rows(k, x_stats, pool, 0)
            invert_rows(k, x_stats, pool, 1)

            def slot(i, b):
                if has(i, -2):
                    invert_rows(k, x_stats, pool, i + 2)
                pool.wait_ge(s["rows_hi"], i + 1)
                nc.gpsimd.tensor_tensor(k.row_lo[:, ds(TPC * i, TPC), 0:D - 1], f[b][:, :, 0:D - 1],
                                        k.row_hi[:, ds(TPC * i, TPC), 0:D - 1], ALU.subtract).then_inc(s["rows_lo"], 1)

            slots(pool, 0, slot, ahead=2)

        @block.scalar
        def _(act):
            def slot(i, b):
                if has(i, 0):
                    act.wait_ge(s["ft_ready"], i + 1)
                    if past(i, 2):
                        act.wait_ge(s["g_ready"], i - 1)
                        act.wait_ge(s["lo_ready"], i - 1)
                    nc.scalar.copy(f_t[b][:], p_ft[:]).then_inc(s["ft_copied"], 1)
                    nc.scalar.copy(k.sta_hi[:, ds(CHUNK * i, CHUNK)], p_ft[:]).then_inc(s["hi_ready"], 1)
                    nc.scalar.copy(k.row_hi[:, ds(TPC * i, TPC), 0:D - 1], f[b][:, :, 0:D - 1]).then_inc(s["rows_hi"], 1)
                if has(i, 2):
                    act.wait_ge(s["g_ready"], i - 1)
                    for t in range(TPC):
                        last = nc.scalar.activation(square[b][:, t, :], p_g[b][:, 0, t, :], ACT.Square,
                                                    accum_out=length[:, ds(TPC * (i - 2) + t, 1)])
                    last.then_inc(s["squared"], 1)

            slots(act, 2, slot)

        @block.tensor
        def _(pe):
            pe.wait_ge(s["preset"], 2)

            def slot(i, b):
                if has(i, 0):
                    pe.wait_ge(s["f_ready"], i + 1)
                    if past(i, 1):
                        pe.wait_ge(s["hi_ready"], i)
                    for t in range(TPC):
                        last = nc.tensor.transpose(p_ft[:, P * t:P * t + P], f[b][:, t, :], k.ident[:])
                    last.then_inc(s["ft_ready"], 1)
                if has(i, 1):
                    if past(i, 3):
                        pe.wait_ge(s["g_kept"], i - 2)
                        pe.wait_ge(s["squared"], i - 2)
                    pe.wait_ge(s["ft_copied"], i)
                    for t in range(TPC):
                        for w in range(2):
                            last = nc.tensor.matmul(p_g[1 - b][:, w, t, :], f_t[1 - b][:, P * t:P * t + P],
                                                    k.m_aug[:, D * w:D * w + D], start=True, stop=True)
                    last.then_inc(s["g_ready"], 1)
                    pe.wait_ge(s["rows_lo"], i)
                    for t in range(TPC):
                        for part in (k.row_hi, k.row_lo):
                            begin = isinstance(i, int) and i == 1 and t == 0 and part is k.row_hi
                            nc.tensor.matmul(p_sum[:], part[:, ds(TPC * (i - 1) + t, 1), :], k.ones_half[:, 0:1],
                                             start=begin, stop=False, skip_group_check=True)

            slots(pe, 1, slot, head=4)
            nc.tensor.matmul(p_sum[:], k.zero_half[:], k.ones_half[:, 0:1], start=False, stop=True,
                             skip_group_check=True).then_inc(s["sum_ready"], 1)
            pe.wait_ge(s["sums_ready"], 1)
            nc.tensor.matmul(p_mean[:], f_sums[:], k.wv_aug[:], start=True, stop=True).then_inc(s["mean_ready"], 1)


def scale_queries(k):
    nc = k.nc
    with ExitStack() as ctx:
        top = k.sb("q_top", [P, 2], F32, ctx)
        unit = [k.sb(f"q_unit{i}", [P, TPC, D], F32, ctx) for i in range(4)]
        p_t = [k.ps(f"q_p_t{i}", [P, TPC * P], ctx) for i in range(4)]
        names = ("top_ready", "rooted", "clamped", "scale_ready", "unit_ready", "t_ready", "hi_ready", "lo_ready")
        s = {n: k.sem("q_" + n, ctx) for n in names}
        block = ctx.enter_context(nc.Block())

        @block.gpsimd
        def _(pool):
            nc.gpsimd.partition_all_reduce(top[:, 0:1], k.g_length[:, 0:1], P, bass.bass_isa.ReduceOp.max).then_inc(s["top_ready"], 1)

        @block.scalar
        def _(act):
            act.wait_ge(s["top_ready"], 1)
            nc.scalar.activation(top[:, 1:2], top[:, 0:1], ACT.Sqrt).then_inc(s["rooted"], 1)

            def four(i, first):
                for b in range(4):
                    g = 4 * i + b
                    act.wait_ge(s["t_ready"], g + 1)
                    nc.scalar.copy(k.mov_hi[:, ds(CHUNK * g, CHUNK)], p_t[b][:]).then_inc(s["hi_ready"], 1)

            peeled(act, CHUNKS // 4, four)

        @block.vector
        def _(dve):
            dve.wait_ge(s["rooted"], 1)
            nc.vector.tensor_scalar(k.g_unit[:], top[:, 1:2], 1e-15, 1.0 / 32, ALU.max, ALU.mult).then_inc(s["clamped"], 1)
            dve.wait_ge(s["clamped"], 1)
            nc.vector.reciprocal(k.g_scale[:], k.g_unit[:]).then_inc(s["scale_ready"], 1)
            nc.vector.tensor_scalar(k.wide_scores[:], top[:, 0:1], S_MAX ** 2 / D, None, ALU.is_gt)
            dve.wait_ge(s["scale_ready"], 1)

            def scale(g, b):
                if past(g, 4):
                    dve.wait_ge(s["t_ready"], g - 3)
                nc.vector.tensor_scalar(unit[b][:], k.g_rows[:, ds(TPC * g, TPC), :], k.g_scale[:, 0:1], None,
                                        ALU.mult).then_inc(s["unit_ready"], 1)

            def lows(g, b):
                dve.wait_ge(s["hi_ready"], g + 1)
                nc.vector.tensor_tensor(k.mov_lo[:, ds(CHUNK * g, CHUNK)], p_t[b][:],
                                        k.mov_hi[:, ds(CHUNK * g, CHUNK)], ALU.subtract).then_inc(s["lo_ready"], 1)

            def four(i, first):
                for b in range(4):
                    scale(4 * i + b, b)
                    if not (first and b < 2):
                        lows(4 * i + b - 2, (b - 2) % 4)

            peeled(dve, CHUNKS // 4, four)
            for g in range(CHUNKS - 2, CHUNKS):
                lows(g, g % 4)

        @block.tensor
        def _(pe):
            def four(i, first):
                for b in range(4):
                    g = 4 * i + b
                    pe.wait_ge(s["unit_ready"], g + 1)
                    if not first:
                        pe.wait_ge(s["lo_ready"], g - 3)
                    for t in range(TPC):
                        last = nc.tensor.transpose(p_t[b][:, P * t:P * t + P], unit[b][:, t, :], k.ident[:])
                    last.then_inc(s["t_ready"], 1)

            peeled(pe, CHUNKS // 4, four)


def row_maxima(k):
    nc = k.nc
    LIFT = 384.0
    with ExitStack() as ctx:
        adj = k.sb("m_adj", [P, 2, 2 * CHUNK], I32, ctx)
        lifted = k.sb("m_lifted", [P, 2 * CHUNK], F32, ctx)
        masked = k.sb("m_masked", [P, 2 * CHUNK], F32, ctx)
        run = k.sb("m_run", [P, CHUNK], F32, ctx)
        top = k.sb("m_top", [P, 3, TPC], F32, ctx)
        lift = k.sb("m_lift", [P, 1], F32, ctx)
        unit = k.sb("m_unit", [P, TPC, D], F32, ctx)
        p_s = k.ps("m_p_s", [P, 2 * CHUNK], ctx)
        p_t = k.ps("m_p_t", [P, TPC * P], ctx)
        p_q = k.ps("m_p_q", [P, TPC * P], ctx)
        names = ("adj_in", "adj_free", "s_free", "s_ready", "lift_set", "run_step", "turned", "top_step", "unit_ready",
                 "q_turned", "q_hi")
        s = {n: k.sem("m_" + n, ctx) for n in names}
        block = ctx.enter_context(nc.Block())
        TRANSFERS = CHUNKS * STEPS // 2

        def wide(eng):
            return eng.value_load(k.wide_scores[0:1, 0:1], min_val=0, max_val=1) > 0

        @block.sync
        def _(sp):
            with sp.If(wide(sp)):
                with sp.Fori(0, TRANSFERS) as m:
                    sp.wait_ge(s["adj_free"], 2 * m + 1)
                    sp.dma_start(adj[:], k.io["adj_t"][ds(m, 1)]).then_inc(s["adj_in"], 16)

        @block.tensor
        def _(pe):
            with pe.If(wide(pe)):
                with pe.Fori(0, CHUNKS) as c:
                    q_hi, q_lo = (m[:, ds(CHUNK * c, CHUNK)] for m in (k.mov_hi, k.mov_lo))
                    with pe.Fori(0, STEPS) as st:
                        pe.wait_ge(s["s_free"], STEPS * c + st + 1)
                        for j in range(2):
                            key = ds(P * (2 * st + j), P)
                            out = p_s[:, CHUNK * j:CHUNK * j + CHUNK]
                            nc.tensor.matmul(out, k.sta_hi[:, key], q_hi, start=True, stop=False)
                            nc.tensor.matmul(out, k.sta_hi[:, key], q_lo, start=False, stop=False)
                            last = nc.tensor.matmul(out, k.sta_lo[:, key], q_hi, start=False, stop=True)
                        last.then_inc(s["s_ready"], 1)
                    pe.wait_ge(s["run_step"], (2 * STEPS + 1) * (c + 1))
                    for t in range(TPC):
                        last = nc.tensor.transpose(p_t[:, P * t:P * t + P], run[:, P * t:P * t + P], k.ident[:])
                    last.then_inc(s["turned"], 1)
                    pe.wait_ge(s["unit_ready"], c + 1)
                    for t in range(TPC):
                        last = nc.tensor.transpose(p_q[:, P * t:P * t + P], unit[:, t, :], k.ident[:])
                    last.then_inc(s["q_turned"], 1)

        @block.scalar
        def _(act):
            with act.If(wide(act)):
                act.wait_ge(s["lift_set"], 1)
                nc.scalar.activation(lifted[:, 0:1], lift[:], ACT.Identity).then_inc(s["s_free"], 1)
                with act.Fori(0, CHUNKS) as c:
                    with act.Fori(0, STEPS) as st:
                        act.wait_ge(s["s_ready"], STEPS * c + st + 1)
                        act.wait_ge(s["s_free"], STEPS * c + st + 1)
                        act.wait_ge(s["adj_free"], STEPS * c + st + 1)
                        nc.scalar.activation(lifted[:], p_s[:], ACT.Identity, bias=lift[:, 0:1]).then_inc(s["s_free"], 1)
                    act.wait_ge(s["q_turned"], c + 1)
                    nc.scalar.copy(k.mov_hi[:, ds(CHUNK * c, CHUNK)], p_q[:]).then_inc(s["q_hi"], 1)

        @block.vector
        def _(dve):
            with dve.If(wide(dve)):
                nc.vector.memset(lift[:], LIFT).then_inc(s["lift_set"], 1)
                nc.vector.memset(masked[:, 0:1], 0.0).then_inc(s["adj_free"], 1)
                dve.wait_ge(s["adj_free"], 1)
                with dve.Fori(0, CHUNKS) as c:
                    nc.vector.memset(run[:], 0.0).then_inc(s["run_step"], 1)
                    with dve.Fori(0, STEPS // 2) as q:
                        for half in range(2):
                            n = STEPS * c + 2 * q + half
                            dve.wait_ge(s["s_free"], n + 2)
                            dve.wait_ge(s["adj_in"], 8 * (n + 2 - half))
                            dve.wait_ge(s["run_step"], 2 * n + c + 1)
                            nc.vector.scalar_tensor_tensor(masked[:], adj[:, half, :], 0.0, lifted[:], ALU.is_gt,
                                                           ALU.mult).then_inc(s["adj_free"], 1)
                            dve.wait_ge(s["adj_free"], n + 2)
                            for j in range(2):
                                dve.wait_ge(s["run_step"], 2 * n + c + 1 + j)
                                nc.vector.tensor_tensor(run[:], run[:], masked[:, CHUNK * j:CHUNK * j + CHUNK],
                                                        ALU.max).then_inc(s["run_step"], 1)
                    dve.wait_ge(s["turned"], c + 1)
                    nc.vector.tensor_reduce(top[:, 0, :], p_t[:].rearrange("p (t j) -> p t j", t=TPC), AX.X,
                                            ALU.max).then_inc(s["top_step"], 1)
                    dve.wait_ge(s["top_step"], 4 * c + 1)
                    nc.vector.tensor_scalar(top[:, 1, :], top[:, 0, :], -LIFT, -1.0, ALU.add, ALU.mult)\
                        .then_inc(s["top_step"], 1)
                    dve.wait_ge(s["top_step"], 4 * c + 2)
                    nc.vector.scalar_tensor_tensor(top[:, 2, :], top[:, 0, :], 0.0, top[:, 1, :], ALU.is_gt,
                                                   ALU.mult).then_inc(s["top_step"], 1)
                    nc.vector.tensor_scalar(unit[:], k.g_rows[:, ds(TPC * c, TPC), :], k.g_scale[:, 0:1], None,
                                            ALU.mult).then_inc(s["top_step"], 1)
                    dve.wait_ge(s["top_step"], 4 * c + 4)
                    nc.vector.tensor_copy(unit[:, :, D - 1], top[:, 2, :]).then_inc(s["unit_ready"], 1)
                    dve.wait_ge(s["q_hi"], c + 1)
                    nc.vector.tensor_tensor(k.mov_lo[:, ds(CHUNK * c, CHUNK)], p_q[:], k.mov_hi[:, ds(CHUNK * c, CHUNK)],
                                            ALU.subtract)
                    dve.wait_ge(s["unit_ready"], c + 1)


def experts(k):
    nc = k.nc
    with ExitStack() as ctx:
        f = k.sb("e_f", [P, TPC, D], F32, ctx)
        f_hi, f_lo = (k.sb("e_f_" + n, [P, TPC * P], F16, ctx) for n in ("hi", "lo"))
        hid = [k.sb(f"e_hid{i}", [P, CHUNK], F32, ctx) for i in range(2)]
        hid_hi = [k.sb(f"e_hid_hi{i}", [P, HC, CHUNK], F16, ctx) for i in range(2)]
        hid_lo = [k.sb(f"e_hid_lo{i}", [P, HC, CHUNK], F16, ctx) for i in range(2)]
        logit = k.sb("e_logit", [P, TPC, E], F32, ctx)
        shifted = k.sb("e_shifted", [P, TPC, E], F32, ctx)
        expo = k.sb("e_expo", [P, TPC, E], F32, ctx)
        chosen = k.sb("e_chosen", [P, 3, TPC, E], F32, ctx)
        red = k.sb("e_red", [P, 4, TPC], F32, ctx)
        gate = k.sb("e_gate", [P, TPC, E], F32, ctx)
        gate_y = [k.sb(f"e_gate_y{i}", [P, TPC, E], F32, ctx) for i in range(2)]
        gate_t = k.sb("e_gate_t", [E, TPC * P], F32, ctx)
        acc = [k.sb(f"e_acc{i}", [P, TPC, D], F32, ctx) for i in range(2)]
        p_ft = k.ps("e_p_ft", [P, TPC * P], ctx)
        p_h = [k.ps(f"e_p_h{i}", [P, CHUNK], ctx) for i in range(2)]
        p_l = k.ps("e_p_l", [P, TPC, E], ctx)
        p_gt = k.ps("e_p_gt", [P, TPC * P], ctx)
        p_y = [k.ps(f"e_p_y{i}", [P, E // 2, D], ctx) for i in range(2)]
        p_b = k.ps("e_p_b", [P, TPC, D], ctx)
        names = ("f_ready", "ft_ready", "ft_hi", "ft_lo", "h_ready", "gelu_ready", "hi_ready", "lo_ready", "l_ready", "logits",
                 "tops", "shifts", "exps", "sums", "recips", "equals", "ranks", "firsts", "choices", "gates", "gates_y",
                 "gt_ready", "gt_copied", "b_ready", "acc_started", "y_ready", "sum_step")
        s = {n: k.sem("e_" + n, ctx) for n in names}
        ROUNDS = 2 * TPC
        SUMS = E // 2
        HIDDEN = ((0, 1), (2,), (3,)) + ((),) * (ROUNDS - 3)
        LOGITS = 4
        stored = [k.sem(f"e_stored{i}", ctx) for i in range(2)]
        out_dram = k.io["out"].rearrange("(t p) d -> p t d", p=P)
        block = ctx.enter_context(nc.Block())

        @block.sync
        def _(sp):
            with sp.Fori(0, CHUNKS // 2) as cc:
                for par in range(2):
                    c = 2 * cc + par
                    sp.wait_ge(s["sum_step"], SUMS * ROUNDS * (c + 1))
                    sp.dma_start(out_dram[:, ds(TPC * c, TPC), :], acc[par][:]).then_inc(stored[par], 16)
            for par in range(2):
                sp.wait_ge(stored[par], 16 * (CHUNKS // 2))

        @block.tensor
        def _(pe):
            def turn_rows(c, first):
                pe.wait_ge(s["f_ready"], c + 1)
                if not first:
                    pe.wait_ge(s["ft_lo"], c)
                for t in range(TPC):
                    last = nc.tensor.transpose(p_ft[:, P * t:P * t + P], f[:, t, :], k.ident[:])
                last.then_inc(s["ft_ready"], 1)

            def hidden(c, h, first):
                pe.wait_ge(s["ft_lo"], c + 1)
                if not (first and h < 2):
                    pe.wait_ge(s["gelu_ready"], HC * c + h - 1)
                w_hi, w_lo = (w[:, P * h:P * h + P] for w in (k.w1_hi, k.w1_lo))
                nc.tensor.matmul(p_h[h % 2][:], w_hi, f_hi[:], start=True, stop=False)
                nc.tensor.matmul(p_h[h % 2][:], w_hi, f_lo[:], start=False, stop=False)
                nc.tensor.matmul(p_h[h % 2][:], w_lo, f_hi[:], start=False, stop=True).then_inc(s["h_ready"], 1)

            def logits(c, par, first):
                pe.wait_ge(s["lo_ready"], HC * (c + 1))
                if not first:
                    pe.wait_ge(s["logits"], c)
                for t in range(TPC):
                    rows = slice(P * t, P * t + P)
                    for h in range(HC):
                        nc.tensor.matmul(p_l[:, t, :], hid_hi[par][:, h, rows], k.wg_hi[:, h, :], start=(h == 0), stop=False)
                        nc.tensor.matmul(p_l[:, t, :], hid_hi[par][:, h, rows], k.wg_lo[:, h, :], start=False, stop=False)
                        last = nc.tensor.matmul(p_l[:, t, :], hid_lo[par][:, h, rows], k.wg_hi[:, h, :], start=False,
                                                stop=(h == HC - 1))
                last.then_inc(s["l_ready"], 1)

            def turn_gate(c, first):
                pe.wait_ge(s["gates"], c + 1)
                if not first:
                    pe.wait_ge(s["gt_copied"], c)
                for t in range(TPC):
                    last = nc.tensor.transpose(p_gt[0:E, P * t:P * t + P], gate[:, t, :], k.ident[:])
                last.then_inc(s["gt_ready"], 1)

            def biases(c, first):
                pe.wait_ge(s["gt_copied"], c + 1)
                if not first:
                    pe.wait_ge(s["acc_started"], c)
                for t in range(TPC):
                    last = nc.tensor.matmul(p_b[:, t, :], gate_t[:, P * t:P * t + P], k.bd[0:E, :], start=True, stop=True)
                last.then_inc(s["b_ready"], 1)

            def product(c, par, first, r):
                t, half = r // 2, r % 2
                if not (first and r < 2):
                    pe.wait_ge(s["sum_step"], SUMS * (ROUNDS * c + r - 1))
                rows = slice(P * t, P * t + P)
                out = p_y[half][:].rearrange("p e d -> p (e d)")
                for h in range(HC):
                    w_hi, w_lo = (w[:, h, 4 * half:4 * half + 4, :].rearrange("p e d -> p (e d)")
                                  for w in (k.wd_hi, k.wd_lo))
                    nc.tensor.matmul(out, hid_hi[par][:, h, rows], w_hi, start=(h == 0), stop=False)
                    nc.tensor.matmul(out, hid_hi[par][:, h, rows], w_lo, start=False, stop=False)
                    last = nc.tensor.matmul(out, hid_lo[par][:, h, rows], w_hi, start=False, stop=(h == HC - 1))
                last.then_inc(s["y_ready"], 1)

            def chunk(c, par, first=False, last=False):
                if not first:
                    turn_gate(c, False)
                if not last:
                    turn_rows(c + 1, False)
                for r in range(ROUNDS):
                    product(c, par, first, r)
                    if r == 0 and first:
                        turn_gate(c, True)
                    if r == 0:
                        biases(c, first)
                    if last:
                        continue
                    for h in HIDDEN[r]:
                        hidden(c + 1, h, False)
                    if r == LOGITS:
                        logits(c + 1, 1 - par, False)

            turn_rows(0, True)
            for h in range(HC):
                hidden(0, h, True)
            logits(0, 0, True)
            chunk(0, 0, first=True)
            chunk(1, 1)
            with pe.Fori(1, CHUNKS // 2 - 1) as cc:
                chunk(2 * cc, 0)
                chunk(2 * cc + 1, 1)
            chunk(CHUNKS - 2, 0)
            chunk(CHUNKS - 1, 1, last=True)

        @block.scalar
        def _(act):
            def front(c, par, first):
                act.wait_ge(s["ft_ready"], c + 1)
                if not first:
                    act.wait_ge(s["h_ready"], HC * c)
                nc.scalar.copy(f_hi[:], p_ft[:]).then_inc(s["ft_hi"], 1)
                for h in range(HC):
                    act.wait_ge(s["h_ready"], HC * c + h + 1)
                    if not (first and h < 2):
                        act.wait_ge(s["lo_ready"], HC * c + h - 1)
                    nc.scalar.activation(hid[h % 2][:], p_h[h % 2][:], ACT.Gelu, bias=k.b1[:, h:h + 1],
                                         scale=k.e_unit[:, 3:4]).then_inc(s["gelu_ready"], 1)
                    act.wait_ge(s["gelu_ready"], HC * c + h + 1)
                    if h == 0 and not (isinstance(c, int) and c < 2):
                        act.wait_ge(s["y_ready"], ROUNDS * (c - 1))
                    nc.scalar.activation(hid_hi[par][:, h, :], hid[h % 2][:], ACT.Copy, scale=k.e_scale[:, 0:1])\
                        .then_inc(s["hi_ready"], 1)

            def exps(c):
                act.wait_ge(s["shifts"], c + 1)
                nc.scalar.activation(expo[:], shifted[:], ACT.Exp).then_inc(s["exps"], 1)

            front(0, 0, True)
            exps(0)

            def step(c, par, first=False, last=False):
                act.wait_ge(s["gt_ready"], c + 1)
                if not first:
                    act.wait_ge(s["b_ready"], c)
                nc.scalar.copy(gate_t[:], p_gt[0:E, :]).then_inc(s["gt_copied"], 1)
                if not last:
                    front(c + 1, 1 - par, False)
                    exps(c + 1)

            step(0, 0, first=True)
            step(1, 1)
            with act.Fori(1, CHUNKS // 2 - 1) as cc:
                step(2 * cc, 0)
                step(2 * cc + 1, 1)
            step(CHUNKS - 2, 0)
            step(CHUNKS - 1, 1, last=True)

        @block.vector
        def _(dve):
            def rows(c, first):
                if not first:
                    dve.wait_ge(s["ft_ready"], c)
                for t in range(TPC):
                    last = normalised(k, f[:, t, :], c, t)
                last.then_inc(s["f_ready"], 1)

            def rows_low(c):
                dve.wait_ge(s["ft_hi"], c + 1)
                nc.vector.tensor_tensor(f_lo[:], p_ft[:], f_hi[:], ALU.subtract).then_inc(s["ft_lo"], 1)

            def lows(c, par, h):
                dve.wait_ge(s["hi_ready"], HC * c + h + 1)
                nc.vector.scalar_tensor_tensor(hid_lo[par][:, h, :], hid[h % 2][:], k.e_scale[:, 0:1],
                                               hid_hi[par][:, h, :], ALU.mult, ALU.subtract).then_inc(s["lo_ready"], 1)

            def wide(a):
                return a.unsqueeze(2).broadcast_to([P, TPC, E])

            def choose(c):
                dve.wait_ge(s["l_ready"], c + 1)
                nc.vector.scalar_tensor_tensor(logit[:].rearrange("p t e -> p (t e)"), p_l[:].rearrange("p t e -> p (t e)"),
                                               k.e_back[:, 1:2], k.bg[:], ALU.mult, ALU.add).then_inc(s["logits"], 1)
                dve.wait_ge(s["logits"], c + 1)
                nc.vector.tensor_reduce(red[:, 0, :], logit[:], AX.X, ALU.max).then_inc(s["tops"], 1)
                dve.wait_ge(s["tops"], c + 1)
                nc.vector.tensor_tensor(shifted[:], logit[:], wide(red[:, 0, :]), ALU.subtract).then_inc(s["shifts"], 1)
                nc.vector.tensor_tensor(chosen[:, 0], logit[:], wide(red[:, 0, :]), ALU.is_equal).then_inc(s["equals"], 1)
                dve.wait_ge(s["equals"], c + 1)
                nc.vector.tensor_tensor(chosen[:, 1], chosen[:, 0], k.ranks[:], ALU.mult).then_inc(s["ranks"], 1)
                dve.wait_ge(s["ranks"], c + 1)
                nc.vector.tensor_reduce(red[:, 1, :], chosen[:, 1], AX.X, ALU.max).then_inc(s["firsts"], 1)
                dve.wait_ge(s["firsts"], c + 1)
                nc.vector.tensor_tensor(chosen[:, 2], chosen[:, 1], wide(red[:, 1, :]), ALU.is_equal).then_inc(s["choices"], 1)

            def weigh(c, par, first):
                dve.wait_ge(s["exps"], c + 1)
                nc.vector.tensor_reduce(red[:, 2, :], expo[:], AX.X, ALU.add).then_inc(s["sums"], 1)
                dve.wait_ge(s["sums"], c + 1)
                nc.vector.reciprocal(red[:, 3, :], red[:, 2, :]).then_inc(s["recips"], 1)
                dve.wait_ge(s["recips"], c + 1)
                dve.wait_ge(s["choices"], c + 1)
                if not first:
                    dve.wait_ge(s["gt_ready"], c)
                nc.vector.tensor_tensor(gate[:], chosen[:, 2], wide(red[:, 3, :]), ALU.mult).then_inc(s["gates"], 1)
                dve.wait_ge(s["gates"], c + 1)
                nc.vector.tensor_scalar(gate_y[par][:], gate[:], k.e_back[:, 0:1], None, ALU.mult).then_inc(s["gates_y"], 1)

            def begin(c, par):
                dve.wait_ge(s["b_ready"], c + 1)
                if not (isinstance(c, int) and c < 2):
                    dve.wait_ge(stored[par], 8 * (c - par))
                nc.vector.tensor_tensor(acc[par][:], p_b[:], k.x[:, ds(TPC * c, TPC), :], ALU.add).then_inc(s["acc_started"], 1)

            def add(c, par, r):
                t, half = r // 2, r % 2
                dve.wait_ge(s["gates_y"], c + 1)
                dve.wait_ge(s["y_ready"], ROUNDS * c + r + 1)
                for e in range(SUMS):
                    if r == 0 and e == 0:
                        dve.wait_ge(s["acc_started"], c + 1)
                    else:
                        dve.wait_ge(s["sum_step"], SUMS * (ROUNDS * c + r) + e)
                    nc.vector.scalar_tensor_tensor(acc[par][:, t, :], p_y[half][:, e, :],
                                                   gate_y[par][:, t, SUMS * half + e:SUMS * half + e + 1],
                                                   acc[par][:, t, :], ALU.mult, ALU.add).then_inc(s["sum_step"], 1)

            def step(c, par, last=False, rows_left=True):
                if not last:
                    rows_low(c + 1)
                begin(c, par)
                for r in range(ROUNDS):
                    add(c, par, r)
                    if last:
                        continue
                    for h in HIDDEN[r]:
                        lows(c + 1, 1 - par, h)
                    if r == LOGITS - 1 and rows_left:
                        rows(c + 2, False)
                    if r == LOGITS:
                        choose(c + 1)
                    if r == LOGITS + 1:
                        weigh(c + 1, 1 - par, False)

            rows(0, True)
            rows_low(0)
            rows(1, False)
            for h in range(HC):
                lows(0, 0, h)
            choose(0)
            weigh(0, 0, True)
            step(0, 0)
            step(1, 1)
            with dve.Fori(1, CHUNKS // 2 - 1) as cc:
                step(2 * cc, 0)
                step(2 * cc + 1, 1)
            step(CHUNKS - 2, 0, rows_left=False)
            step(CHUNKS - 1, 1, last=True, rows_left=False)


def build(nc, io):
    with ExitStack() as ctx:
        k = Core(nc, ctx, io)
        k.x = k.sb("x_rows", [P, T, D])
        k.g_rows = k.sb("g_rows", [P, T, D])
        k.row_hi, k.row_lo = (k.sb(n, [P, T, D], F16) for n in ("row_hi", "row_lo"))
        k.mov_hi, k.mov_lo = (k.sb(n, [P, N], F16) for n in ("mov_hi", "mov_lo"))
        k.sta_hi, k.sta_lo = (k.sb(n, [P, N], F16) for n in ("sta_hi", "sta_lo"))
        k.x_stats = k.sb("x_stats", [P, T // 2, 6])
        k.rstd, k.empty = (k.sb(n, [P, T]) for n in ("rstd", "empty"))
        k.early = k.sb("early", [P, sum(EARLY.values())])
        k.late = k.sb("late", [P, sum(LATE.values())])
        k.rows = k.sb("rows", [1, sum(ROWS.values())])
        packed = {}
        for tensor, widths in ((k.early, EARLY), (k.late, LATE), (k.rows, ROWS)):
            packed.update(columns(tensor, widths))
        k.ident, k.wkq_t, k.center, k.unaug, k.unaug_t = (packed[n] for n in ("ident", "wkq_t", "center", "unaug", "unaug_t"))
        k.w_ffn_t, k.wq1, k.wk1, k.wv1_t, k.w1 = (packed[n] for n in ("w_ffn_t", "wq1", "wk1", "wv1_t", "w1"))
        k.lnw, k.lnb, k.bq1, k.b1, k.wg, k.bg = (packed[n] for n in ("lnw", "lnb", "bq1", "b1", "wg", "bg"))
        k.last_row, k.b_ffn, k.bv1 = (packed[n] for n in ("last_row", "b_ffn", "bv1"))
        k.ranks = packed["ranks"].rearrange("p (t e) -> p t e", e=E)
        k.wv_aug = k.sb("wv_aug", [P, D + 1])
        k.ones = k.sb("ones", [P, P])
        k.ones_bf = k.sb("ones_bf", [P, P], BF16)
        k.ones_half = k.sb("ones_half", [P, 1], F16)
        k.zero_half = k.sb("zero_half", [P, P], F16)
        k.minus_half, k.eps, k.eps_sum, k.inv_d = (k.sb(n, [P, TPC]) for n in ("minus_half", "eps", "eps_sum", "inv_d"))
        k.shift = k.sb("shift", [P, 1])
        k.w_ffn = k.sb("w_ffn", [P, D])
        k.bias_ffn = k.sb("bias_ffn", [P, TPC, D], BF16)
        k.bias_mid = k.sb("bias_mid", [1, D], BF16)
        k.m_aug = k.sb("m_aug", [P, 2 * D])
        k.v_mean = k.sb("v_mean", [P, D])
        k.g_length, k.g_unit, k.g_scale = (k.sb(n, [P, 1]) for n in ("g_length", "g_unit", "g_scale"))
        k.wide_scores = k.sb("wide_scores", [P, 1], I32)
        k.w1_hi, k.w1_lo = (k.sb(n, [P, HID], F16) for n in ("w1_hi", "w1_lo"))
        k.wg_hi, k.wg_lo = (k.sb(n, [P, HC, E], F16) for n in ("wg_hi", "wg_lo"))
        k.wd = k.sb("wd_raw", [P, HC, E, D])
        k.wd_hi, k.wd_lo = (k.sb(n, [P, HC, E, D], F16) for n in ("wd_hi", "wd_lo"))
        k.bd = k.sb("bd_rows", [E, D])
        k.e_unit, k.e_scale, k.e_back = (k.sb(n, [P, w]) for n, w in (("e_unit", 4), ("e_scale", 4), ("e_back", 2)))

        k.late_in = k.sem("late_in", ctx)

        with ExitStack() as span:
            adj, adj_in = adjacency(k, "a_", span)
            normalise_a(k, adj, adj_in)
            prepare_weights(k)
            attention(k, "a_", adj, adj_in)
        with ExitStack() as span:
            x_stats = row_stats(k, "rx_", span)
            recurrence(k, x_stats)
            adj, adj_in = adjacency(k, "b_", span)
            normalise_b(k, x_stats, adj, adj_in)
            scale_queries(k)
            row_maxima(k)
            attention(k, "b_", adj, adj_in)
        experts(k)


def kernel(**inputs):
    import numpy as np
    import concourse.bacc as bacc
    from concourse.bass_utils import run_bass_kernel_spmd

    a = {n: np.ascontiguousarray(v) for n, v in inputs.items()}
    eye = np.eye(D, dtype=np.float32)
    unaug = np.concatenate([eye, eye[:, D - 1:]], axis=1)
    unaug[:D - 1, D - 1] = -1.0
    unaug[D - 1, D - 1] = 0.0
    parts = {
        "ident": eye, "wkq_t": np.concatenate([a["L0_gnn_Wk"].T, a["L0_gnn_Wq"].T], axis=1),
        "center": eye - np.float32(1.0 / D), "unaug": unaug, "unaug_t": unaug[:, :D].T,
        "w_ffn_t": a["L0_ffn_W"].T, "wq1": a["L1_gnn_Wq"], "wk1": a["L1_gnn_Wk"], "wv1_t": a["L1_gnn_Wv"].T,
        "w1": a["L1_ffn_W1"], "lnw": a["L0_ffn_ln_w"].reshape(D, 1), "lnb": a["L0_ffn_ln_b"].reshape(D, 1),
        "bq1": a["L1_gnn_bq"].reshape(D, 1), "b1": a["L1_ffn_b1"].reshape(HC, P).T,
        "wg": a["L1_ffn_Wg"].reshape(HC, P, E).transpose(1, 0, 2).reshape(P, HC * E),
        "bg": np.broadcast_to(a["L1_ffn_bg"], (P, TPC, E)).reshape(P, TPC * E),
        "ranks": np.broadcast_to(np.arange(E, 0, -1, dtype=np.float32), (P, TPC, E)).reshape(P, TPC * E),
        "last_row": eye[D - 1:], "b_ffn": a["L0_ffn_b"].reshape(1, D), "bv1": a["L1_gnn_bv"].reshape(1, D),
    }
    early, late, rows = (np.concatenate([parts[n] for n in names], axis=1) for names in (EARLY, LATE, ROWS))
    arrays = {
        "x": a["x"], "early": early, "late": late, "rows": rows,
        "adj_t": a["adj"].reshape(CHUNKS, CHUNK, STEPS // 2, 2, 2, P).transpose(0, 2, 5, 3, 4, 1)
                         .reshape(CHUNKS * STEPS // 2, P, 2, 2 * CHUNK),
        "wd": a["L1_ffn_Wd"].reshape(E, HC, P, D).transpose(2, 1, 0, 3),
        "bd": a["L1_ffn_bd"],
    }
    arrays = {n: np.ascontiguousarray(v) for n, v in arrays.items()}
    nc = bacc.Bacc("TRN2", target_bir_lowering=False, num_devices=1)
    io = {n: nc.dram_tensor("in_" + n, v.shape, mybir.dt.from_np(v.dtype), kind="ExternalInput").ap()
          for n, v in arrays.items()}
    io["out"] = nc.dram_tensor("out_x", (N, D), F32, kind="ExternalOutput").ap()
    build(nc, io)
    result = run_bass_kernel_spmd(nc, [{"in_" + n: v for n, v in arrays.items()}], core_ids=[0])
    return result.results[0]["out_x"]
```
